# Optimizing a Trainium2 kernel written in Bass

```python
import numpy as np
import jax
import jax.numpy as jnp

def _softmax(x, axis=-1):
    return jax.nn.softmax(x, axis=axis)

def _gelu(x):
    return jax.nn.gelu(x, approximate=True)

def _silu(x):
    return jax.nn.silu(x)

def _sigmoid(x):
    return jax.nn.sigmoid(x)

def _layernorm(x, axis=-1, eps=1e-05):
    m = jnp.mean(x, axis=axis, keepdims=True)
    v = jnp.var(x, axis=axis, keepdims=True)
    return (x - m) / jnp.sqrt(v + eps)

def _scatter_add(tgt, idx, src, axis=0):
    return tgt.at[idx].add(src)

def _segment_sum(src, seg, n):
    return jax.ops.segment_sum(src, seg, n)
kernel_name = 'mk_adaln_d1_jaxref_r2_8aa7f7'

def setup_inputs(seed: int=0):
    np.random.seed(seed)
    _w = jnp.asarray

    def _L0_attn_setup():
        import jax, jax.numpy as jnp
        import numpy as np
        B, S, E, H = (2, 1024, 1024, 16)
        D = E // H
        key = jax.random.key(seed)
        ks = jax.random.split(key, 5)
        scale = 0.02
        return {'x': jax.random.normal(ks[0], (B, S, E), dtype=jnp.float32), 'Wq': jax.random.normal(ks[1], (E, E), dtype=jnp.float32) * scale, 'Wk': jax.random.normal(ks[2], (E, E), dtype=jnp.float32) * scale, 'Wv': jax.random.normal(ks[3], (E, E), dtype=jnp.float32) * scale, 'Wo': jax.random.normal(ks[4], (E, E), dtype=jnp.float32) * scale, 'bo': jnp.zeros((E,), dtype=jnp.float32)}
    _L0_attn_in = _L0_attn_setup()

    def _L0_ffn_setup():
        import jax, jax.numpy as jnp
        import numpy as np
        K = 2
        SCALING = 16.0 / 16.0
        key = jax.random.key(seed)
        ks = jax.random.split(key, 7)
        B, T, D, O, E, R = (2, 2048, 1024, 1024, 8, 16)
        return {'x': jax.random.normal(ks[0], (B, T, D), dtype=jnp.float32), 'W': jax.random.normal(ks[1], (O, D), dtype=jnp.float32) * (1.0 / np.sqrt(D)), 'b': jax.random.normal(ks[2], (O,), dtype=jnp.float32) * 0.02, 'lora_A': jax.random.normal(ks[3], (E, R, D), dtype=jnp.float32) * (1.0 / np.sqrt(D)), 'lora_B': jax.random.normal(ks[4], (E, O, R), dtype=jnp.float32) * 0.02, 'gate_w': jax.random.normal(ks[5], (E, D), dtype=jnp.float32) * 0.02, 'gate_b': jax.random.normal(ks[6], (E,), dtype=jnp.float32) * 0.02}
    _L0_ffn_in = _L0_ffn_setup()
    _L0_c = _w((lambda *s: np.random.randn(*s).astype(np.float32) * 0.05)(4, 1024))
    _L0_wmod = _w((lambda *s: np.random.randn(*s).astype(np.float32) * 0.05)(1024, 6 * 1024) * 1024 ** (-0.5))
    _d = {'L0_attn_x': _L0_attn_in['x'], 'L0_attn_Wq': _L0_attn_in['Wq'], 'L0_attn_Wk': _L0_attn_in['Wk'], 'L0_attn_Wv': _L0_attn_in['Wv'], 'L0_attn_Wo': _L0_attn_in['Wo'], 'L0_attn_bo': _L0_attn_in['bo'], 'L0_ffn_W': _L0_ffn_in['W'], 'L0_ffn_b': _L0_ffn_in['b'], 'L0_ffn_lora_A': _L0_ffn_in['lora_A'], 'L0_ffn_lora_B': _L0_ffn_in['lora_B'], 'L0_ffn_gate_w': _L0_ffn_in['gate_w'], 'L0_ffn_gate_b': _L0_ffn_in['gate_b'], 'L0_c': _L0_c, 'L0_wmod': _L0_wmod}
    _x0 = _d['L0_attn_x']
    _d['L0_attn_x'] = jax.random.normal(jax.random.fold_in(jax.random.key(seed), 1), (4, 1024, 1024), dtype=_x0.dtype)
    del _x0
    return _d

def reference(L0_attn_x, L0_attn_Wq, L0_attn_Wk, L0_attn_Wv, L0_attn_Wo, L0_attn_bo, L0_ffn_W, L0_ffn_b, L0_ffn_lora_A, L0_ffn_lora_B, L0_ffn_gate_w, L0_ffn_gate_b, L0_c, L0_wmod):

    def _L0_attn_ref(x, Wq, Wk, Wv, Wo, bo):
        import jax, jax.numpy as jnp
        import numpy as np
        B, S, E, H = (2, 1024, 1024, 16)
        D = E // H
        b, s, e = x.shape

        def split_heads(t):
            return t.reshape(b, s, H, D).transpose(0, 2, 1, 3)
        q = split_heads(x @ Wq.T)
        k = split_heads(x @ Wk.T)
        v = split_heads(x @ Wv.T)
        scores = jnp.einsum('bhqd,bhkd->bhqk', q, k)
        causal = jnp.tril(jnp.ones((s, s), dtype=bool))
        scores = jnp.where(causal, scores, -jnp.inf)
        attn = jax.nn.softmax(scores / jnp.sqrt(jnp.float32(D)), axis=-1)
        ctx = jnp.einsum('bhqk,bhkd->bhqd', attn, v)
        ctx = ctx.transpose(0, 2, 1, 3).reshape(b, s, e)
        return ctx @ Wo.T + bo

    def _L0_ffn_ref(x, W, b, lora_A, lora_B, gate_w, gate_b):
        import jax, jax.numpy as jnp
        import numpy as np
        K = 2
        SCALING = 16.0 / 16.0
        orig_shape = x.shape
        D = orig_shape[-1]
        O = W.shape[0]
        x_flat = x.reshape(-1, D)
        base = x_flat @ W.T + b
        logits = x_flat @ gate_w.T + gate_b
        topk_logits, topk_idx = jax.lax.top_k(logits, K)
        gates = jax.nn.softmax(topk_logits, axis=-1)
        xA = jnp.einsum('nd,erd->ner', x_flat, lora_A)
        delta_all = jnp.einsum('ner,eor->neo', xA, lora_B)
        delta_topk = jnp.take_along_axis(delta_all, topk_idx[:, :, None], axis=1)
        lora_update = jnp.sum(delta_topk * gates[:, :, None], axis=1)
        out = base + SCALING * lora_update
        return out.reshape(*orig_shape[:-1], O)
    x = L0_attn_x
    mod = (_silu(L0_c) @ L0_wmod).reshape(L0_c.shape[0], 6, 1, -1)
    sa, ca, ga, sb, cb, gb = (mod[:, 0], mod[:, 1], mod[:, 2], mod[:, 3], mod[:, 4], mod[:, 5])
    ga = (2 * (ga >= 0) - 1) * jnp.maximum(jnp.abs(ga), 0.25)
    gb = (2 * (gb >= 0) - 1) * jnp.maximum(jnp.abs(gb), 0.25)
    h = _layernorm(x, axis=-1) * (1 + ca) + sa
    x = x + ga * _L0_attn_ref(h, L0_attn_Wq, L0_attn_Wk, L0_attn_Wv, L0_attn_Wo, L0_attn_bo)
    h = _layernorm(x, axis=-1) * (1 + cb) + sb
    x = x + gb * _L0_ffn_ref(h, L0_ffn_W, L0_ffn_b, L0_ffn_lora_A, L0_ffn_lora_B, L0_ffn_gate_w, L0_ffn_gate_b)
    return x

_drawn_inputs = setup_inputs


def setup_inputs(seed=0):
    import zlib

    import numpy as np

    out = dict(_drawn_inputs(seed))
    spreads = {'L0_attn_bo': (0.0, 1.046)}
    factors = {'L0_attn_Wq': 8.0,
     'L0_attn_Wk': 8.0,
     'L0_attn_Wv': 5.798,
     'L0_attn_Wo': 5.807,
     'L0_ffn_b': 37.982,
     'L0_ffn_lora_A': 4.06,
     'L0_ffn_lora_B': 4.047,
     'L0_ffn_gate_w': 4.643,
     'L0_ffn_gate_b': 43.445}
    for name, (base, spread) in spreads.items():
        noise = np.random.default_rng([zlib.crc32(name.encode()), seed]).standard_normal(out[name].shape)
        drawn = base * np.exp(spread * noise) if base else spread * noise
        out[name] = jnp.asarray(drawn.astype(out[name].dtype))
    for name, factor in factors.items():
        out[name] = (out[name] * factor).astype(out[name].dtype)
    return out
```

```python
from contextlib import ExitStack

import concourse.bass as bass
from concourse import mybir

F32 = mybir.dt.float32
F32R = mybir.dt.float32r
BF16 = mybir.dt.bfloat16
I32 = mybir.dt.int32
U32 = mybir.dt.uint32
ALU = mybir.AluOpType
ACT = mybir.ActivationFunctionType
AX = mybir.AxisListType

P = 128
B, S, E = 4, 1024, 1024
H = 16
D = E // H
KT = E // P
TT = S // P
PAIRS = H // 2
NE, R = 8, 16
NAG = NE * R + NE
HALF = 512
EPS = 1e-5
QSCALE = D ** -0.5
MASKED = -3.0e38
RSQRT_MAGIC = 0x5F3759DF
NEWTON = 4

UNITS = 2 * TT


def unit_chunks(u):
    t = u % TT
    return [(k0, min(4, t + 1 - k0)) for k0 in range(0, t + 1, 4)]


CHUNK0 = [sum(len(unit_chunks(v)) for v in range(u)) for u in range(UNITS + 1)]
CHUNKS = CHUNK0[UNITS]
GROUPS = UNITS // 2
ZUNITS = 6
ZMM = KT * 3
SLOTS = UNITS + 3
ZPARTS = 3


def norm_statistics(eng, step, tiles, st, dm, mean, rstd, v, half_v, t):
    spread = lambda a: a.rearrange("p (t o) -> p t o", o=1).broadcast_to([P, tiles, 4])
    step(eng.tensor_reduce(mean, st[:, :, :, 1], AX.X, ALU.add))
    step(eng.tensor_scalar(mean, mean, 0.25, None, ALU.mult))
    step(eng.tensor_tensor(dm, st[:, :, :, 1], spread(mean), ALU.subtract))
    step(eng.tensor_tensor(dm, dm, dm, ALU.mult))
    step(eng.scalar_tensor_tensor(out=dm, in0=dm, scalar=E / 4.0, in1=st[:, :, :, 2], op0=ALU.mult, op1=ALU.add))
    step(eng.tensor_reduce(v, dm, AX.X, ALU.add))
    step(eng.tensor_scalar(v, v, 1.0 / E, EPS, ALU.mult, ALU.add))
    step(eng.tensor_scalar(half_v, v, 0.5, None, ALU.mult))
    step(eng.tensor_scalar(t.bitcast(I32), v.bitcast(I32), 1, None, ALU.logical_shift_right))
    step(eng.tensor_scalar(rstd.bitcast(I32), t.bitcast(I32), -1.0, float(RSQRT_MAGIC), ALU.mult, ALU.add))
    for _ in range(NEWTON):
        step(eng.tensor_tensor(t, rstd, rstd, ALU.mult))
        step(eng.tensor_tensor(t, t, half_v, ALU.mult))
        step(eng.tensor_scalar(t, t, -1.0, 1.5, ALU.mult, ALU.add))
        step(eng.tensor_tensor(rstd, rstd, t, ALU.mult))


STAT_STEPS = 10 + 4 * NEWTON


def modulation_phase(nc, cT, wmod, mod_cols, identf, gate_rows):
    CH = 6 * E // HALF
    RING = 3
    with ExitStack() as ctx:
        def sb(name, shape, dt=F32):
            return ctx.enter_context(nc.sbuf_tensor(name, shape, dt))

        def sem(name):
            return ctx.enter_context(nc.semaphore(name))

        c_in = sb("c_in", [P, KT, B])
        c_exp = sb("c_exp", [P, KT, B])
        c_silu = sb("c_silu", [P, KT, B])
        wring = sb("wring", [P, RING, KT, HALF])
        rows = sb("rows", [B, 6 * E])
        g_sign = sb("g_sign", [B, 2, E])
        g_abs = sb("g_abs", [B, 2, E])
        psM = ctx.enter_context(nc.psum_tensor("psM", [P, 2, HALF], F32))
        psMT = ctx.enter_context(nc.psum_tensor("psMT", [P, 4, KT, B], F32))
        c_loaded = sem("c_loaded")
        w_loaded = [sem(f"w_loaded{i}") for i in range(RING)]
        exp_done, dve_chain = sem("m_exp_done"), sem("m_dve_chain")
        silu_ready, ident_zeroed, ident_ready = sem("silu_ready"), sem("ident_zeroed"), sem("ident_ready")
        row_ready, row_copied = sem("row_ready"), sem("row_copied")
        cols_ready, cols_copied, gates_ready, gates_out = (
            sem("cols_ready"), sem("cols_copied"), sem("gates_ready"), sem("gates_out"))
        block = ctx.enter_context(nc.Block())

        @block.sync
        def _(sp):
            sp.dma_start(c_in[:, :, :], cT).then_inc(c_loaded, 16)
            for n in range(CH):
                if n >= RING:
                    sp.wait_ge(row_ready, n - RING + 1)
                sp.dma_start(wring[:, n % RING, :, :],
                             wmod[:, n * HALF:(n + 1) * HALF].rearrange("(k p) n -> p k n", p=P)
                             ).then_inc(w_loaded[n % RING], 16)
            sp.wait_ge(gates_ready, 1)
            sp.dma_start(gate_rows, g_abs[:, :, :]).then_inc(gates_out, 16)
            sp.wait_ge(gates_out, 16)

        @block.gpsimd
        def _(pool):
            pool.memset(identf[:, :], 0.0).then_inc(ident_zeroed, 1)
            pool.wait_ge(ident_zeroed, 1)
            pool.affine_select(out=identf[:, :], in_=identf[:, :], compare_op=ALU.not_equal, fill=1.0,
                               base=0, pattern=[[-1, P]], channel_multiplier=1).then_inc(ident_ready, 1)

        @block.scalar
        def _(act):
            act.wait_ge(c_loaded, 16)
            act.activation(c_exp[:, :, :], c_in[:, :, :], ACT.Exp, scale=-1.0).then_inc(exp_done, 1)
            for n in range(CH):
                act.wait_ge(row_ready, n + 1)
                act.activation(rows[:, n * HALF:(n + 1) * HALF], psM[0:B, n % 2, :], ACT.Copy
                               ).then_inc(row_copied, 1)

        @block.tensor
        def _(pe):
            pe.wait_ge(silu_ready, 1)
            for n in range(CH):
                pe.wait_ge(w_loaded[n % RING], 16 * (n // RING + 1))
                if n >= 2:
                    pe.wait_ge(row_copied, n - 1)
                for k in range(KT):
                    last = pe.matmul(psM[0:B, n % 2, :], c_silu[:, k, :], wring[:, n % RING, k, :],
                                     start=k == 0, stop=k == KT - 1)
                last.then_inc(row_ready, 1)
            pe.wait_ge(row_copied, CH)
            pe.wait_ge(ident_ready, 1)
            for v, chunk in enumerate((0, 1, 3, 4)):
                for k in range(KT):
                    c0 = chunk * E + k * P
                    last = pe.transpose(psMT[:, v, k, :], rows[:, c0:c0 + P], identf[0:B, 0:B])
            last.then_inc(cols_ready, 1)

        @block.vector
        def _(dve):
            chain = [0]

            def step(ins):
                chain[0] += 1
                ins.then_inc(dve_chain, 1)
                dve.wait_ge(dve_chain, chain[0])

            dve.wait_ge(exp_done, 1)
            step(dve.tensor_scalar(c_exp[:, :, :], c_exp[:, :, :], 1.0, None, ALU.add))
            step(dve.reciprocal(c_exp[:, :, :], c_exp[:, :, :]))
            dve.tensor_tensor(c_silu[:, :, :], c_in[:, :, :], c_exp[:, :, :], ALU.mult).then_inc(silu_ready, 1)
            dve.wait_ge(row_copied, CH)
            gates = rows[:, :].rearrange("b (c e) -> b c e", c=6)[:, 2:6:3, :]
            step(dve.tensor_scalar(g_sign[:, :, :], gates, 0.0, 2.0, ALU.is_ge, ALU.mult))
            step(dve.tensor_scalar(g_sign[:, :, :], g_sign[:, :, :], 1.0, None, ALU.subtract))
            step(dve.scalar_tensor_tensor(out=g_abs[:, :, :], in0=gates, scalar=-1.0, in1=gates,
                                          op0=ALU.mult, op1=ALU.max))
            step(dve.tensor_scalar(g_abs[:, :, :], g_abs[:, :, :], 0.25, None, ALU.max))
            dve.tensor_tensor(g_abs[:, :, :], g_abs[:, :, :], g_sign[:, :, :], ALU.mult).then_inc(gates_ready, 1)
            dve.wait_ge(cols_ready, 1)
            dve.tensor_copy(mod_cols[:, 0:4:2, :, :], psMT[:, 0:4:2, :, :]).then_inc(cols_copied, 1)
            dve.tensor_scalar(mod_cols[:, 1:4:2, :, :], psMT[:, 1:4:2, :, :], 1.0, None, ALU.add
                              ).then_inc(cols_copied, 1)
            dve.wait_ge(cols_copied, 2)


def attention_phase(nc, x, wqkv, mod_cols, identf, ctxT, nb=B):
    with ExitStack() as ctx:
        def sb(name, shape, dt=F32):
            return ctx.enter_context(nc.sbuf_tensor(name, shape, dt))

        def sem(name):
            return ctx.enter_context(nc.semaphore(name))

        base = nc.sbuf_base
        sb("pair_arena", [P, 2 * 4 * 2 * S])
        KB4 = 4 * 2 * S
        Qs, Qx, Ks, Vs = [], [], [], []
        for par in range(2):
            o = base + par * 4 * KB4
            Qs.append(nc.alloc_sbuf_tensor_at(f"Qs{par}", [P, 2, S], F32R, offset=o))
            Qx.append(nc.alloc_sbuf_tensor_at(f"Qx{par}", [P, 2, S], F32R, offset=o + KB4))
            Ks.append(nc.alloc_sbuf_tensor_at(f"Ks{par}", [P, 2, S], F32R, offset=o + 2 * KB4))
            Vs.append(nc.alloc_sbuf_tensor_at(f"Vs{par}", [P, 2, TT, 2 * D], F32R, offset=o + 3 * KB4))
        xn = nc.alloc_sbuf_tensor_at("xn", [P, TT, E], F32, offset=base)

        hT = [sb("hT_hi", [P, KT, S], F32R), sb("hT_lo", [P, KT, S], F32R)]
        W = [sb("W_hi", [P, 3, KT, P], F32R), sb("W_lo", [P, 3, KT, P], F32R)]
        W_in = sb("W_in", [P, 2, KT, P])
        PT = [[sb(f"PT_{part}{g}", [P, 6 + 2 * g, 2 * P], F32R) for part in ("hi", "lo")] for g in range(2)]
        Pb = sb("Pb", [P, 2, S])
        Zs = sb("Zs", [P, HALF])
        ctxs = sb("ctxs", [P, S])
        ctx_lo = sb("ctx_lo", [D, 2 * P])
        hn = [Zs, sb("hn1", [P, HALF])]
        ident16, mask16 = sb("ident16", [P, P], BF16), sb("mask16", [P, P], BF16)
        one = sb("one", [P, 1])
        negmax, rowsum, rinv = sb("negmax", [P, UNITS]), sb("rowsum", [P, UNITS]), sb("rinv", [P, UNITS])
        st, dm = sb("st", [P, TT, 4, 3]), sb("dm", [P, TT, 4])
        mean, rstd, var, hvar, rtmp = [sb(n, [P, TT]) for n in ("mean", "rstd", "var", "hvar", "rtmp")]
        modb = sb("modb", [P, 2, KT])

        def psum(name, shape):
            return ctx.enter_context(nc.psum_tensor(name, shape, F32))

        psS = [psum("psS0", [P, S]), psum("psS1", [P, S])]
        psT = [psum("psT0", [P, HALF]), psum("psT1", [P, HALF])]
        psPV = psum("psPV", [P, HALF])
        psZ = psum("psZ", [P, HALF])

        scores_done, max_done, exp_done, norm_done, rinv_done = (
            sem("scores_done"), sem("max_done"), sem("exp_done"), sem("norm_done"), sem("rinv_done"))
        tp_done, pthi_done, ptlo_done = sem("tp_done"), sem("pthi_done"), sem("ptlo_done")
        pv_done, ctxlo_done, ctx_done, ctx_out = sem("pv_done"), sem("ctxlo_done"), sem("ctx_done"), sem("ctx_out")
        z_done, zs_done, qkhi_done, qklo_done, qx_done = (
            sem("z_done"), sem("zs_done"), sem("qkhi_done"), sem("qklo_done"), sem("qx_done"))
        vt_done, vhi_done, vlo_done = sem("vt_done"), sem("vhi_done"), sem("vlo_done")
        w_in, whi_done, w_ready = [sem("w_in0"), sem("w_in1")], sem("whi_done"), sem("w_ready")
        consts_a, consts_ready = sem("consts_a"), sem("consts_ready")
        x_in = [sem("x_in0"), sem("x_in1")]
        st_done, xnorm_done, modb_done = sem("st_done"), sem("xnorm_done"), sem("modb_done")
        lnt_done, lnaff_done, lnhi_done, lnlo_done = (
            sem("lnt_done"), sem("lnaff_done"), sem("lnhi_done"), sem("lnlo_done"))

        def val(hk, per, n):
            h, k = hk
            return h * (2 * per) + (k * per + max(n, 0))

        def nxt(hk):
            return (hk[0], hk[1] + 1)

        def prev(hk):
            return (hk[0], hk[1] - 1)

        def run(eng, layer_norm, step, before_last=lambda b: None):
            layer_norm(0)
            step(None, (0, 0), 1, True)

            def batch(b, last):
                with eng.Fori(0, 3) as c:
                    h = eng.snap(4 * b + c)
                    step((h, 0), (h, 1), 2 * c + 2, True)
                    step((h, 1), (h, 2), 2 * c + 3, True)
                h = 4 * b + 3
                step((h, 0), (h, 1), 0, not last)
                if not last:
                    before_last(b + 1)
                step((h, 1), None, None, False)
                if not last:
                    layer_norm(b + 1)
                    step(None, (4 * b + 4, 0), 1, True)

            if nb > 1:
                with eng.Fori(0, nb - 1) as b:
                    batch(b, False)
            batch(nb - 1, True)

        block = ctx.enter_context(nc.Block())

        @block.sync
        def _(sp):
            def load_w(hk, pair, part):
                n = 3 * hk[1] + part
                if not (isinstance(hk[0], int) and val(hk, 3, part) < 2):
                    sp.wait_ge(w_ready, val(hk, 3, part - 1) if part else val(prev(hk), 3, 2))
                sp.dma_start(W_in[:, n % 2, :, :], wqkv[bass.ds(pair, 1), part, :, :, :] if not isinstance(pair, int)
                             else wqkv[pair:pair + 1, part, :, :, :]).then_inc(w_in[n % 2], 16)

            def load_x(b):
                xt = x.rearrange("b (t p) e -> b p t e", p=P)
                if not (isinstance(b, int) and b == 0):
                    sp.wait_ge(ctx_done, b * (PAIRS * GROUPS) - GROUPS)
                for half in range(2):
                    sp.dma_start(xn[:, 4 * half:4 * half + 4, :],
                                 (xt[b] if isinstance(b, int) else xt[bass.ds(b, 1)].rearrange("o p t e -> (o p) t e"))
                                 [:, 4 * half:4 * half + 4, :]).then_inc(x_in[half], 16)

            def step(att, proj, wnext, prefetch):
                if proj is not None:
                    par = proj[1] % 2
                    if prefetch:
                        load_w(nxt(proj), wnext, 0)
                    sp.wait_ge(qklo_done, val(proj, 8, 4))
                    sp.dma_start(Qx[par][0:D, :, :].bitcast(F32), Qs[par][D:P, :, :].bitcast(F32)).then_inc(qx_done, 16)
                    sp.dma_start(Qx[par][D:P, :, :].bitcast(F32), Qs[par][0:D, :, :].bitcast(F32)).then_inc(qx_done, 16)
                    if prefetch:
                        load_w(nxt(proj), wnext, 1)
                        load_w(nxt(proj), wnext, 2)
                if att is not None:
                    sp.wait_ge(ctx_done, val(att, GROUPS, GROUPS))
                    h, k = att
                    n = h * 2 + k
                    sp.dma_start((ctxT[n:n + 1] if isinstance(n, int) else ctxT[bass.ds(n, 1)])
                                 .rearrange("o p t -> (o p) t"), ctxs[:, :]).then_inc(ctx_out, 16)

            load_x(0)
            for part in range(3):
                load_w((0, 0), 0, part)
            run(sp, lambda b: None, step, before_last=load_x)
            sp.wait_ge(ctx_out, 16 * (nb * PAIRS + 1))

        @block.gpsimd
        def _(pool):
            pool.memset(ident16[:, :], 0.0).then_inc(consts_a, 1)
            pool.memset(mask16[:, :], 0.0).then_inc(consts_a, 1)
            pool.memset(one[:, :], 1.0).then_inc(consts_a, 1)
            pool.wait_ge(consts_a, 3)
            pool.affine_select(out=ident16[:, :], in_=ident16[:, :], compare_op=ALU.not_equal, fill=1.0,
                               base=0, pattern=[[-1, P]], channel_multiplier=1).then_inc(consts_ready, 1)
            pool.affine_select(out=mask16[:, :], in_=mask16[:, :], compare_op=ALU.is_ge, fill=MASKED,
                               base=0, pattern=[[-1, P]], channel_multiplier=1).then_inc(consts_ready, 1)

            def split_w(hk, part):
                n = 3 * hk[1] + part
                pool.wait_ge(w_in[n % 2], hk[0] * 48 + 16 * (n // 2 + 1))
                if not (isinstance(hk[0], int) and hk == (0, 0)):
                    pool.wait_ge(z_done, val(prev(hk), ZUNITS, 2 * part + 2))
                pool.tensor_tensor(out=W[0][:, part, :, :], in0=W_in[:, n % 2, :, :],
                                   in1=one[:, 0:1].rearrange("p (a b) -> p a b", a=1).broadcast_to([P, KT, P]),
                                   op=ALU.mult).then_inc(whi_done, 1)
                pool.wait_ge(whi_done, val(hk, 3, part + 1))
                pool.tensor_tensor(out=W[1][:, part, :, :], in0=W_in[:, n % 2, :, :],
                                   in1=W[0][:, part, :, :].bitcast(F32), op=ALU.subtract).then_inc(w_ready, 1)

            for part in range(3):
                split_w((0, 0), part)

            def step(att, proj, wnext, prefetch):
                if proj is not None and prefetch:
                    for part in range(3):
                        split_w(nxt(proj), part)

            run(pool, lambda b: None, step)

        @block.tensor
        def _(pe):
            def scores(att, u):
                par, head, t = att[1] % 2, u // TT, u % TT
                if u == 0:
                    pe.wait_ge(qklo_done, val(att, 8, 8))
                    pe.wait_ge(qx_done, val(att, 32, 32))
                if u >= 2:
                    pe.wait_ge(exp_done, val(att, UNITS, u - 1))
                for half in range(t // 4 + 1):
                    c0 = half * HALF
                    n = min(HALF, (t + 1) * P - c0)
                    diagonal = half == t // 4
                    out, keys = psS[u % 2][:, c0:c0 + n], Ks[par][:, head, c0:c0 + n]
                    q = slice(t * P, (t + 1) * P)
                    pe.matmul(out, Qs[par][:, head, q], keys, start=True, stop=False)
                    last = pe.matmul(out, Qx[par][:, head, q], keys, start=False, stop=not diagonal)
                    if diagonal:
                        last = pe.matmul(psS[u % 2][:, t * P:(t + 1) * P], ident16[:, :], mask16[:, :],
                                         start=False, stop=True)
                last.then_inc(scores_done, 1)

            def transposes(att, u):
                pe.wait_ge(norm_done, val(att, UNITS, u + 1))
                for n, (k0, nk) in enumerate(unit_chunks(u), CHUNK0[u]):
                    if n >= 2:
                        pe.wait_ge(ptlo_done, val(att, CHUNKS, n - 1))
                    for i in range(nk):
                        last = pe.transpose(psT[n % 2][:, i * P:(i + 1) * P],
                                            Pb[:, u % 2, (k0 + i) * P:(k0 + i + 1) * P], identf[:, :])
                    last.then_inc(tp_done, 1)

            def context(att, g, v_seen):
                par, head, gg = att[1] % 2, g // 4, g % 4
                pe.wait_ge(ptlo_done, val(att, CHUNKS, CHUNK0[2 * g + 2]))
                if g:
                    pe.wait_ge(ctx_done, val(att, GROUPS, g))
                pe.wait_ge(vlo_done, v_seen)
                hi, lo = PT[gg % 2]
                for k in range(2 * gg + 2):
                    q = slice(P if k == 2 * gg + 1 else 0, 2 * P)
                    v = Vs[par][:, head, k, :]
                    pe.matmul(psPV[:, q], v, hi[:, k, q], start=k == 0, stop=False)
                    last = pe.matmul(psPV[:, q], v, lo[:, k, q], start=False, stop=k == 2 * gg + 1)
                last.then_inc(pv_done, 1)

            def project(proj, first, unit, part):
                which, half = unit // 2, unit % 2
                if part == 0:
                    pe.wait_ge(zs_done, val(proj, ZUNITS, unit))
                    if half == 0:
                        pe.wait_ge(w_ready, val(proj, 3, which + 1))
                mms = [(k, a, b) for k in range(KT) for a, b in ((0, 0), (0, 1), (1, 0))]
                lo, hi = part * ZMM // ZPARTS, (part + 1) * ZMM // ZPARTS
                for i in range(lo, hi):
                    k, a, b = mms[i]
                    last = pe.matmul(psZ[:, :], W[a][:, which, k, :], hT[b][:, k, half * HALF:(half + 1) * HALF],
                                     start=i == 0, stop=i == ZMM - 1)
                if part == ZPARTS - 1:
                    last.then_inc(z_done, 1)

            def v_transposes(proj, half, ctx_seen):
                pe.wait_ge(zs_done, val(proj, ZUNITS, 5 + half))
                pe.wait_ge(ctx_done, ctx_seen)
                pe.wait_ge(vlo_done, val(proj, 2, half))
                for i in range(4):
                    last = pe.transpose(psPV[:, i * P:(i + 1) * P], Zs[:, i * P:(i + 1) * P], identf[:, :])
                last.then_inc(vt_done, 1)

            def layer_norm(b):
                pe.wait_ge(ptlo_done, b * (PAIRS * CHUNKS))
                for half in range(2):
                    pe.wait_ge(xnorm_done, b * TT + 4 * half + 4)
                    for k in range(KT):
                        n = half * KT + k
                        pe.wait_ge(lnaff_done, b * 16 + max(n - 1, 0))
                        for i in range(4):
                            last = pe.transpose(psT[n % 2][:, i * P:(i + 1) * P],
                                                xn[:, 4 * half + i, k * P:(k + 1) * P], identf[:, :])
                        last.then_inc(lnt_done, 1)

            def step(att, proj, wnext, prefetch):
                if proj is not None and att is None:
                    h = proj[0]
                    pe.wait_ge(lnlo_done, h * 4 + 16)
                for j in range(SLOTS):
                    if att is not None:
                        if j < UNITS:
                            scores(att, j)
                        if 2 <= j < UNITS + 2:
                            transposes(att, j - 2)
                        if j >= 4 and j % 2 == 0:
                            g = (j - 4) // 2
                            seen = val(att, 2, 2)
                            if proj is not None and g >= 6:
                                seen = val(proj, 2, 1)
                            context(att, g, seen)
                    if proj is not None:
                        if j < ZPARTS * ZUNITS:
                            project(proj, att is None, j // ZPARTS, j % ZPARTS)
                        if j in (15, 18):
                            half = (j - 15) // 3
                            v_transposes(proj, half, val(proj, GROUPS, 0) if att is None or half
                                         else val(att, GROUPS, 6))

            pe.wait_ge(consts_ready, 2)
            run(pe, layer_norm, step)

        @block.scalar
        def _(act):
            def pt_hi(att, u):
                g = u // 2
                hi = PT[g % 2][0]
                for n, (k0, nk) in enumerate(unit_chunks(u), CHUNK0[u]):
                    act.wait_ge(tp_done, val(att, CHUNKS, n + 1))
                    if g >= 2:
                        act.wait_ge(pv_done, val(att, GROUPS, g - 1))
                    q = (u % 2) * P
                    act.activation(hi[:, k0:k0 + nk, q:q + P],
                                   psT[n % 2][:, 0:nk * P].rearrange("p (k q) -> p k q", q=P), ACT.Copy
                                   ).then_inc(pthi_done, 1)

            def exps(att, u):
                n = (u % TT + 1) * P
                act.wait_ge(max_done, val(att, UNITS, u + 1))
                if u >= 2:
                    act.wait_ge(tp_done, val(att, CHUNKS, CHUNK0[u - 1]))
                act.activation(Pb[:, u % 2, 0:n], psS[u % 2][:, 0:n], ACT.Exp, bias=negmax[:, u:u + 1],
                               accum_out=rowsum[:, u:u + 1]).then_inc(exp_done, 1)

            def context_lo(att, g):
                act.wait_ge(pv_done, val(att, GROUPS, g + 1))
                if g:
                    act.wait_ge(ctx_done, val(att, GROUPS, g))
                act.activation(ctx_lo[:, :], psPV[D:P, 0:2 * P], ACT.Copy).then_inc(ctxlo_done, 1)

            def copy_z(proj, unit):
                act.wait_ge(z_done, val(proj, ZUNITS, unit + 1))
                if unit == 0:
                    act.wait_ge(vt_done, val(proj, 2, 0))
                elif unit == 5:
                    act.wait_ge(vt_done, val(proj, 2, 1))
                else:
                    act.wait_ge(qklo_done, val(proj, 8, 2 * unit))
                act.activation(Zs[:, :], psZ[:, :], ACT.Copy).then_inc(zs_done, 1)

            def qk_hi(proj, unit):
                par, c = proj[1] % 2, slice((unit % 2) * HALF, (unit % 2 + 1) * HALF)
                dst = (Qs if unit < 2 else Ks)[par]
                act.wait_ge(zs_done, val(proj, ZUNITS, unit + 1))
                for head in range(2):
                    rows = slice(head * D, (head + 1) * D)
                    act.activation(dst[rows, head, c], Zs[rows, :], ACT.Copy, scale=QSCALE if unit < 2 else 1.0
                                   ).then_inc(qkhi_done, 1)

            def v_hi(proj, half):
                act.wait_ge(vt_done, val(proj, 2, half + 1))
                act.activation(Vs[proj[1] % 2][:, :, 4 * half:4 * half + 4, 0:D],
                               psPV[:, :].rearrange("p (t h d) -> p h t d", h=2, d=D), ACT.Copy
                               ).then_inc(vhi_done, 1)

            def layer_norm(b):
                act.wait_ge(modb_done, b + 1)
                for n in range(16):
                    half, k = n // KT, n % KT
                    act.wait_ge(lnt_done, b * 16 + n + 1)
                    act.wait_ge(lnlo_done, b * 16 + max(n - 1, 0))
                    act.activation(hn[n % 2][:, :], psT[n % 2][:, :], ACT.Identity, bias=modb[:, 0, k:k + 1],
                                   scale=modb[:, 1, k:k + 1]).then_inc(lnaff_done, 1)
                    act.wait_ge(lnaff_done, b * 16 + n + 1)
                    act.activation(hT[0][:, k, half * HALF:(half + 1) * HALF], hn[n % 2][:, :], ACT.Copy
                                   ).then_inc(lnhi_done, 1)

            def step(att, proj, wnext, prefetch):
                for j in range(SLOTS):
                    if att is not None:
                        if 2 <= j < UNITS + 2:
                            pt_hi(att, j - 2)
                        if j < UNITS:
                            exps(att, j)
                        if j >= 4 and j % 2 == 0:
                            context_lo(att, (j - 4) // 2)
                    if proj is not None:
                        if j % 3 == 0 and 3 <= j <= 12:
                            qk_hi(proj, j // 3 - 1)
                        if j in (15, 18):
                            v_hi(proj, (j - 15) // 3)
                        if j % 3 == 2:
                            copy_z(proj, j // 3)

            run(act, layer_norm, step)

        @block.vector
        def _(dve):
            def row_max(att, u):
                dve.wait_ge(scores_done, val(att, UNITS, u + 1))
                dve.tensor_reduce(negmax[:, u:u + 1], psS[u % 2][:, 0:(u % TT + 1) * P], AX.X, ALU.max,
                                  negate=True).then_inc(max_done, 1)

            def invert(att, u):
                dve.wait_ge(exp_done, val(att, UNITS, u + 1))
                dve.reciprocal(rinv[:, u:u + 1], rowsum[:, u:u + 1]).then_inc(rinv_done, 1)

            def normalize(att, u):
                n = (u % TT + 1) * P
                dve.wait_ge(rinv_done, val(att, UNITS, u + 1))
                dve.tensor_scalar(Pb[:, u % 2, 0:n], Pb[:, u % 2, 0:n], rinv[:, u:u + 1], None, ALU.mult
                                  ).then_inc(norm_done, 1)

            def pt_lo(att, u):
                hi, lo = PT[(u // 2) % 2]
                for n, (k0, nk) in enumerate(unit_chunks(u), CHUNK0[u]):
                    dve.wait_ge(pthi_done, val(att, CHUNKS, n + 1))
                    q = (u % 2) * P
                    dve.tensor_tensor(lo[:, k0:k0 + nk, q:q + P],
                                      psT[n % 2][:, 0:nk * P].rearrange("p (k q) -> p k q", q=P),
                                      hi[:, k0:k0 + nk, q:q + P].bitcast(F32), ALU.subtract
                                      ).then_inc(ptlo_done, 1)

            def context_sum(att, g):
                head, gg = g // 4, g % 4
                dve.wait_ge(ctxlo_done, val(att, GROUPS, g + 1))
                if g == 0:
                    dve.wait_ge(ctx_out, val(att, 16, 16))
                dve.tensor_tensor(ctxs[head * D:(head + 1) * D, gg * 2 * P:(gg + 1) * 2 * P],
                                  psPV[0:D, 0:2 * P], ctx_lo[:, :], ALU.add).then_inc(ctx_done, 1)

            def qk_lo(proj, unit):
                par, c = proj[1] % 2, slice((unit % 2) * HALF, (unit % 2 + 1) * HALF)
                dst = (Qs if unit < 2 else Ks)[par]
                for head in range(2):
                    rows, other = slice(head * D, (head + 1) * D), slice((1 - head) * D, (2 - head) * D)
                    dve.wait_ge(qkhi_done, val(proj, 8, 2 * unit + head + 1))
                    if unit < 2:
                        ins = dve.scalar_tensor_tensor(out=dst[other, head, c], in0=Zs[rows, :], scalar=QSCALE,
                                                       in1=dst[rows, head, c].bitcast(F32), op0=ALU.mult,
                                                       op1=ALU.subtract)
                    else:
                        ins = dve.tensor_tensor(dst[other, head, c], Zs[rows, :], dst[rows, head, c].bitcast(F32),
                                                ALU.subtract)
                    ins.then_inc(qklo_done, 1)

            def v_lo(proj, half):
                v = Vs[proj[1] % 2][:, :, 4 * half:4 * half + 4, :]
                dve.wait_ge(vhi_done, val(proj, 2, half + 1))
                dve.tensor_tensor(v[:, :, :, D:2 * D], psPV[:, :].rearrange("p (t h d) -> p h t d", h=2, d=D),
                                  v[:, :, :, 0:D].bitcast(F32), ALU.subtract).then_inc(vlo_done, 1)

            def layer_norm(b):
                count = [0]

                def chain(ins):
                    count[0] += 1
                    ins.then_inc(st_done, 1)
                    dve.wait_ge(st_done, b * (1 + STAT_STEPS) + count[0])

                bs = slice(b, b + 1) if isinstance(b, int) else bass.ds(b, 1)
                dve.tensor_copy(modb[:, :, :], mod_cols[:, 0:2, :, bs].rearrange("p v k o -> p v (k o)")
                                ).then_inc(modb_done, 1)
                for t in range(TT):
                    if t % 4 == 0:
                        dve.wait_ge(x_in[t // 4], b * 16 + 16)
                    for half in range(2):
                        last = dve.bn_stats(st[:, t, 2 * half:2 * half + 2, :].rearrange("p a c -> p (a c)"),
                                            xn[:, t, half * HALF:(half + 1) * HALF])
                chain(last)
                norm_statistics(dve, chain, TT, st[:, :, :, :], dm[:, :, :], mean[:, :], rstd[:, :],
                                var[:, :], hvar[:, :], rtmp[:, :])
                for t in range(TT):
                    dve.tensor_scalar(xn[:, t, :], xn[:, t, :], mean[:, t:t + 1], rstd[:, t:t + 1],
                                      ALU.subtract, ALU.mult).then_inc(xnorm_done, 1)
                for n in range(16):
                    half, k = n // KT, n % KT
                    c = slice(half * HALF, (half + 1) * HALF)
                    dve.wait_ge(lnhi_done, b * 16 + n + 1)
                    dve.tensor_tensor(hT[1][:, k, c], hn[n % 2][:, :], hT[0][:, k, c].bitcast(F32), ALU.subtract
                                      ).then_inc(lnlo_done, 1)

            def step(att, proj, wnext, prefetch):
                for j in range(SLOTS):
                    if att is not None:
                        if 1 <= j < UNITS + 1:
                            invert(att, j - 1)
                        if j < UNITS:
                            row_max(att, j)
                        if 1 <= j < UNITS + 1:
                            normalize(att, j - 1)
                        if 2 <= j < UNITS + 2:
                            pt_lo(att, j - 2)
                        if j >= 4 and j % 2 == 0:
                            context_sum(att, (j - 4) // 2)
                    if proj is not None:
                        if j % 3 == 0 and 3 <= j <= 12:
                            qk_lo(proj, j // 3 - 1)
                        if j in (15, 18):
                            v_lo(proj, (j - 15) // 3)

            dve.memset(ctxs[:, :], 0.0).then_inc(ctx_out, 16)
            run(dve, layer_norm, step)


def feed_forward_phase(nc, x, ctxT, gate_rows, mod_cols, identf, wo, w, ag, lb, bo, bw, gate_b, out, nb=B):
    tiles = nb * TT
    with ExitStack() as ctx:
        def sb(name, shape, dt=F32):
            return ctx.enter_context(nc.sbuf_tensor(name, shape, dt))

        def sem(name):
            return ctx.enter_context(nc.semaphore(name))

        def split_pair(name, shape):
            hi = sb(name + "_hi", shape, F32R)
            at = nc.sbuf_base
            sb(name + "_bytes", shape)
            lo = nc.alloc_sbuf_tensor_at(name + "_lo", shape, F32R, offset=at)
            return hi, lo, nc.alloc_sbuf_tensor_at(name + "_in", shape, F32, offset=at)

        Wo_hi, Wo_lo, Wo_in = split_pair("Wo", [P, KT, E])
        Ww_hi, Ww_lo, Ww_in = split_pair("Ww", [P, KT, E])
        AG_hi, AG_lo, AG_in = split_pair("AG", [P, KT, NAG])
        LB_hi, LB_lo, LB_in = split_pair("LB", [P, E])
        ctx_in = sb("ctx_in", [P, 2, KT, P])
        c_hi, c_lo = sb("c_hi", [P, KT, P], F32R), sb("c_lo", [P, KT, P], F32R)
        xt = sb("xt", [P, 2, E])
        xn2 = sb("xn2", [P, E])
        h2n = sb("h2n", [P, KT, P])
        h2_hi, h2_lo = sb("h2_hi", [P, KT, P], F32R), sb("h2_lo", [P, KT, P], F32R)
        ga, gb = sb("ga", [P, E]), sb("gb", [P, E])
        bo_b, bw_b, gate_bb = sb("bo_b", [P, E]), sb("bw_b", [P, E]), sb("gate_bb", [P, NE])
        yb = sb("yb", [P, E])
        xa = sb("xa", [P, P])
        xaT_hi, xaT_lo = sb("xaT_hi", [P, P], F32R), sb("xaT_lo", [P, P], F32R)
        iota_i, iota = sb("iota_i", [P, NE], I32), sb("iota", [P, NE])
        logits, top, topi, topf = sb("logits", [P, NE]), sb("top", [P, 8]), sb("topi", [P, 8], U32), sb("topf", [P, 8])
        first, gates = sb("first", [P, NE]), sb("gates", [P, NE])
        gap, e2, g1, g2 = [sb(n, [P, 1]) for n in ("gap", "e2", "g1", "g2")]
        st, dm = sb("st2", [P, 1, 4, 3]), sb("dm2", [P, 1, 4])
        mean, rstd, var, hvar, rtmp = [sb(n + "2", [P, 1]) for n in ("mean", "rstd", "var", "hvar", "rtmp")]
        modb = sb("modb2", [P, 2, KT])

        def psum(name, shape):
            return ctx.enter_context(nc.psum_tensor(name, shape, F32))

        psO, psF = psum("psO", [P, E]), psum("psF", [P, E])
        psH = psum("psH", [P, 2, 4, P])
        psA, psX = psum("psA", [P, HALF]), psum("psX", [P, HALF])

        wo_in, ww_in = [sem(f"wo_in{k}") for k in range(KT)], [sem(f"ww_in{i}") for i in range(2)]
        aglb_in, rows_in = sem("aglb_in"), sem("rows_in")
        wo_hi, wo_ready, ww_hi, ww_ready = sem("wo_hi"), sem("wo_ready"), sem("ww_hi"), sem("ww_ready")
        iota_done, iota_ready = sem("iota_done"), sem("iota_ready")
        c_in, x_in = [sem("c_in0"), sem("c_in1")], [sem("xt_in0"), sem("xt_in1")]
        out_done = [sem("out_done0"), sem("out_done1")]
        ga_in, gb_in = sem("ga_in"), sem("gb_in")
        chi_done, clo_done, o_done, po_free, x1_done = (
            sem("chi_done"), sem("clo_done"), sem("o_done"), sem("po_free"), sem("x1_done"))
        x1_chain, xn_done, xt_done, aff_done, h2hi_done, h2lo_done, modb_done = (
            sem("x1_chain"), sem("xn2_done"), sem("xt_done"), sem("aff_done"), sem("h2hi_done"),
            sem("h2lo_done"), sem("modb2_done"))
        ag_done, xa_copied, gap_done, e2_done, gate_chain, xa_done = (
            sem("ag_done"), sem("xa_copied"), sem("gap_done"), sem("e2_done"), sem("gate_chain"), sem("xa_done"))
        xat_done, xathi_done, xatlo_done, f_done, pf_free, yb_done, y_done = (
            sem("xat_done"), sem("xathi_done"), sem("xatlo_done"), sem("f_done"), sem("pf_free"),
            sem("yb_done"), sem("y_done"))
        block = ctx.enter_context(nc.Block())

        def val(t, per, n):
            m, k = t
            return m * (2 * per) + (k * per + n)

        def uses(t, per=16):
            m, k = t
            return m * per + (k // 2 + 1) * per

        def add(t, n):
            return (t[0], t[1] + n)

        def number(t):
            return t[0] * 2 + t[1]

        def run(eng, head, body, tail):
            head()

            def batch(b, last):
                with eng.Fori(0, 3) as c:
                    m = eng.snap(4 * b + c)
                    body((m, 0), b, b)
                    body((m, 1), b, b)
                m = 4 * b + 3
                body((m, 0), b, b)
                if last:
                    tail((m, 1), b)
                else:
                    body((m, 1), b, b + 1)

            if nb > 1:
                with eng.Fori(0, nb - 1) as b:
                    batch(b, False)
            batch(nb - 1, True)

        def new_batch(t, b, b2):
            return b2 is not b

        @block.sync
        def _(sp):
            xf = x.rearrange("b (t p) e -> (b t) p e", p=P)
            of = out.rearrange("b (t p) e -> (b t) p e", p=P)

            def load_ctx(t, b, tile):
                c = ctxT.rearrange("(b k) p t -> b p k t", k=KT)
                c = c[b] if isinstance(b, int) else c[bass.ds(b, 1)].rearrange("o p k t -> (o p) k t")
                src = c[:, :, tile * P:(tile + 1) * P] if isinstance(tile, int) else c[:, :, bass.ds(tile * P, P)]
                sp.dma_start(ctx_in[:, t[1] % 2, :, :], src).then_inc(c_in[t[1] % 2], 16)

            def load_x(t):
                n = number(t)
                src = xf[n] if isinstance(n, int) else xf[bass.ds(n, 1)].rearrange("o p e -> (o p) e")
                sp.dma_start(xt[:, t[1] % 2, :], src).then_inc(x_in[t[1] % 2], 16)

            def load_gate(b, which, dst, s):
                src = gate_rows[b:b + 1, which, :] if isinstance(b, int) else gate_rows[bass.ds(b, 1), which, :]
                sp.dma_start(dst[:, :], src.broadcast_to([P, E])).then_inc(s, 16)

            load_ctx((0, 0), 0, 0)
            for k in range(KT):
                sp.dma_start(Wo_in[:, k, :], wo[:, k, :]).then_inc(wo_in[k], 16)
            for dst, src in ((bo_b, bo), (bw_b, bw)):
                sp.dma_start(dst[:, :], src.broadcast_to([P, E])).then_inc(rows_in, 16)
            sp.dma_start(gate_bb[:, :], gate_b.broadcast_to([P, NE])).then_inc(rows_in, 16)
            load_x((0, 0))
            load_gate(0, 0, ga, ga_in)
            load_gate(0, 1, gb, gb_in)
            for i in range(2):
                sp.dma_start(Ww_in[:, 4 * i:4 * i + 4, :], w[:, 4 * i:4 * i + 4, :]).then_inc(ww_in[i], 16)
            sp.dma_start(AG_in[:, :, :], ag).then_inc(aglb_in, 16)
            sp.dma_start(LB_in[:, :], lb).then_inc(aglb_in, 16)
            load_ctx((0, 1), 0, 1)
            load_x((0, 1))

            def store(t):
                sp.wait_ge(y_done, val(t, 1, 2))
                n = number(t)
                dst = of[n] if isinstance(n, int) else of[bass.ds(n, 1)].rearrange("o p e -> (o p) e")
                sp.dma_start(dst, xt[:, t[1] % 2, :]).then_inc(out_done[t[1] % 2], 16)

            def body(t, b, b2, ahead=None):
                b3, tile = ahead
                if b3 is not None:
                    sp.wait_ge(clo_done, val(t, 1, 1))
                    load_ctx(add(t, 2), b3, tile)
                if ahead_gate(t, b, b2, ahead):
                    sp.wait_ge(x1_done, val(t, 1, 1))
                    load_gate(b + 1, 0, ga, ga_in)
                store(t)
                if new_batch(t, b, b2):
                    sp.wait_ge(yb_done, val(t, 1, 1))
                    load_gate(b2, 1, gb, gb_in)
                if b3 is not None:
                    sp.wait_ge(out_done[t[1] % 2], uses(t))
                    load_x(add(t, 2))

            def ahead_gate(t, b, b2, ahead):
                return new_batch(t, b, b2)

            def batch(b, last):
                with sp.Fori(0, 3) as c:
                    m = sp.snap(4 * b + c)
                    body((m, 0), b, b, (b, 2 * c + 2))
                    body((m, 1), b, b, (b, 2 * c + 3))
                m = 4 * b + 3
                body((m, 0), b, b, (None, 0) if last else (b + 1, 0))
                if last:
                    store((m, 1))
                else:
                    body((m, 1), b, b + 1, (b + 1, 1))

            if nb > 1:
                with sp.Fori(0, nb - 1) as b:
                    batch(b, False)
            batch(nb - 1, True)
            for par in range(2):
                sp.wait_ge(out_done[par], 16 * (tiles // 2))

        @block.gpsimd
        def _(pool):
            pool.iota(iota_i[:, :], pattern=[[1, NE]], base=0, channel_multiplier=0).then_inc(iota_done, 1)

            def context_lo(t):
                pool.wait_ge(chi_done, val(t, 1, 1))
                pool.tensor_tensor(out=c_lo[:, :, :], in0=ctx_in[:, t[1] % 2, :, :],
                                   in1=c_hi[:, :, :].bitcast(F32), op=ALU.subtract).then_inc(clo_done, 1)

            def residual(t):
                pool.wait_ge(yb_done, val(t, 1, 1))
                pool.tensor_tensor(out=xt[:, t[1] % 2, :], in0=xt[:, t[1] % 2, :], in1=yb[:, :], op=ALU.add
                                   ).then_inc(y_done, 1)

            def head():
                context_lo((0, 0))
                context_lo((0, 1))

            def body(t, b, b2):
                if not (isinstance(t[0], int) and number(t) + 2 >= tiles):
                    context_lo(add(t, 2))
                residual(t)

            pool.memset(yb[:, :], 0.0).then_inc(y_done, 1)
            run(pool, head, body, lambda t, b: residual(t))

        @block.tensor
        def _(pe):
            def output_projection(t, begin=False):
                pe.wait_ge(clo_done, val(t, 1, 1))
                pe.wait_ge(po_free, val(t, 1, 0))
                for k in range(KT):
                    if begin:
                        pe.wait_ge(wo_ready, k + 1)
                    for a, wv in ((c_hi, Wo_hi), (c_hi, Wo_lo), (c_lo, Wo_hi)):
                        for half in range(2):
                            c = slice(half * HALF, (half + 1) * HALF)
                            last = pe.matmul(psO[:, c], a[:, k, :], wv[:, k, c], start=k == 0 and wv is Wo_hi and a is c_hi,
                                             stop=k == KT - 1 and a is c_lo)
                last.then_inc(o_done, 1)

            def norm_transposes(t):
                pe.wait_ge(xn_done, val(t, 1, 1))
                pe.wait_ge(aff_done, val(t, 2, 0))
                for k in range(KT):
                    last = pe.transpose(psH[:, k // 4, k % 4, :], xn2[:, k * P:(k + 1) * P], identf[:, :])
                    if k % 4 == 3:
                        last.then_inc(xt_done, 1)

            def feed_forward(t, begin=False):
                pe.wait_ge(h2lo_done, val(t, 1, 1))
                if begin:
                    pe.wait_ge(ww_ready, KT + 2)

                def base(k, half, stop=False):
                    c = slice(half * HALF, (half + 1) * HALF)
                    pe.matmul(psF[:, c], h2_hi[:, k, :], Ww_hi[:, k, c], start=k == 0, stop=False)
                    pe.matmul(psF[:, c], h2_hi[:, k, :], Ww_lo[:, k, c], start=False, stop=False)
                    pe.matmul(psF[:, c], h2_lo[:, k, :], Ww_hi[:, k, c], start=False, stop=False)

                for k in range(KT):
                    base(k, 0)
                    pe.matmul(psA[:, 0:NAG], h2_hi[:, k, :], AG_hi[:, k, :], start=k == 0, stop=False)
                    pe.matmul(psA[:, 0:NAG], h2_hi[:, k, :], AG_lo[:, k, :], start=False, stop=False)
                    last = pe.matmul(psA[:, 0:NAG], h2_lo[:, k, :], AG_hi[:, k, :], start=False, stop=k == KT - 1)
                last.then_inc(ag_done, 1)
                for k in range(KT):
                    if k == 5:
                        pe.wait_ge(xa_done, val(t, 1, 1))
                        pe.transpose(psX[:, 0:P], xa[:, :], identf[:, :]).then_inc(xat_done, 1)
                    base(k, 1)
                pe.wait_ge(xatlo_done, val(t, 1, 1))
                for half in range(2):
                    c = slice(half * HALF, (half + 1) * HALF)
                    pe.matmul(psF[:, c], xaT_hi[:, :], LB_hi[:, c], start=False, stop=False)
                    pe.matmul(psF[:, c], xaT_hi[:, :], LB_lo[:, c], start=False, stop=False)
                    last = pe.matmul(psF[:, c], xaT_lo[:, :], LB_hi[:, c], start=False, stop=True)
                last.then_inc(f_done, 1)

            def head():
                output_projection((0, 0), begin=True)
                norm_transposes((0, 0))

            def body(t, b, b2):
                output_projection(add(t, 1))
                feed_forward(t)
                norm_transposes(add(t, 1))

            pe_head = head

            def head_and_weights():
                pe_head()
                pe.wait_ge(ww_ready, KT + 2)

            run(pe, head_and_weights, body, lambda t, b: feed_forward(t))

        @block.scalar
        def _(act):
            def context_hi(t):
                act.wait_ge(c_in[t[1] % 2], uses(t))
                act.wait_ge(o_done, val(t, 1, 0))
                act.activation(c_hi[:, :, :], ctx_in[:, t[1] % 2, :, :], ACT.Copy).then_inc(chi_done, 1)

            def norm_hi(t):
                act.wait_ge(modb_done, val(t, 1, 1))
                act.wait_ge(h2lo_done, val(t, 1, 0))
                for k in range(KT):
                    if k % 4 == 0:
                        act.wait_ge(xt_done, val(t, 2, k // 4 + 1))
                    last = act.activation(h2n[:, k, :], psH[:, k // 4, k % 4, :], ACT.Identity,
                                          bias=modb[:, 0, k:k + 1], scale=modb[:, 1, k:k + 1])
                    if k % 4 == 3:
                        last.then_inc(aff_done, 1)
                act.wait_ge(aff_done, val(t, 2, 2))
                act.activation(h2_hi[:, :, :], h2n[:, :, :], ACT.Copy).then_inc(h2hi_done, 1)

            def gate_exp(t):
                act.wait_ge(gap_done, val(t, 1, 1))
                act.activation(e2[:, :], gap[:, :], ACT.Exp).then_inc(e2_done, 1)

            def xa_hi(t):
                act.wait_ge(xat_done, val(t, 1, 1))
                act.activation(xaT_hi[:, :], psX[:, 0:P], ACT.Copy).then_inc(xathi_done, 1)

            def head():
                context_hi((0, 0))
                for k in range(KT):
                    act.wait_ge(wo_in[k], 16)
                    act.activation(Wo_hi[:, k, :], Wo_in[:, k, :], ACT.Copy).then_inc(wo_hi, 1)
                for k in range(KT):
                    if k % 4 == 0:
                        act.wait_ge(ww_in[k // 4], 16)
                    act.activation(Ww_hi[:, k, :], Ww_in[:, k, :], ACT.Copy).then_inc(ww_hi, 1)
                act.wait_ge(aglb_in, 32)
                act.activation(AG_hi[:, :, :], AG_in[:, :, :], ACT.Copy).then_inc(ww_hi, 1)
                act.activation(LB_hi[:, :], LB_in[:, :], ACT.Copy).then_inc(ww_hi, 1)
                context_hi((0, 1))
                norm_hi((0, 0))

            def body(t, b, b2):
                if not (isinstance(t[0], int) and number(t) + 2 >= tiles):
                    context_hi(add(t, 2))
                gate_exp(t)
                xa_hi(t)
                norm_hi(add(t, 1))

            def tail(t, b):
                gate_exp(t)
                xa_hi(t)

            run(act, head, body, tail)

        @block.vector
        def _(dve):
            X_STEPS = 3 + STAT_STEPS
            G_STEPS = 10

            def norm_chain(t):
                count = [0]

                def chain(ins):
                    count[0] += 1
                    ins.then_inc(x1_chain, 1)
                    dve.wait_ge(x1_chain, val(t, X_STEPS, count[0]))
                return chain

            def residual(t, b, starts):
                chain = norm_chain(t)
                bs = slice(b, b + 1) if isinstance(b, int) else bass.ds(b, 1)
                dve.tensor_copy(modb[:, :, :], mod_cols[:, 2:4, :, bs].rearrange("p v k o -> p v (k o)")
                                ).then_inc(modb_done, 1)
                dve.wait_ge(o_done, val(t, 1, 1))
                if starts:
                    dve.wait_ge(ga_in, b * 16 + 16)
                dve.tensor_tensor(xn2[:, :], psO[:, :], bo_b[:, :], ALU.add).then_inc(po_free, 1)
                dve.wait_ge(po_free, val(t, 1, 1))
                chain(dve.tensor_tensor(xn2[:, :], xn2[:, :], ga[:, :], ALU.mult))
                dve.wait_ge(x_in[t[1] % 2], uses(t))
                x1 = xt[:, t[1] % 2, :]
                dve.tensor_tensor(x1, x1, xn2[:, :], ALU.add).then_inc(x1_done, 1)
                dve.wait_ge(x1_done, val(t, 1, 1))
                for half in range(2):
                    last = dve.bn_stats(st[:, 0, 2 * half:2 * half + 2, :].rearrange("p a c -> p (a c)"),
                                        x1[:, half * HALF:(half + 1) * HALF])
                chain(last)
                norm_statistics(dve, chain, 1, st[:, :, :, :], dm[:, :, :], mean[:, :], rstd[:, :],
                                var[:, :], hvar[:, :], rtmp[:, :])
                chain(dve.tensor_copy(rtmp[:, :], rstd[:, :]))

            def normalize(t):
                dve.tensor_scalar(xn2[:, :], xt[:, t[1] % 2, :], mean[:, 0:1], rstd[:, 0:1],
                                  ALU.subtract, ALU.mult).then_inc(xn_done, 1)

            def gating(t):
                count = [0]

                def chain(ins):
                    count[0] += 1
                    ins.then_inc(gate_chain, 1)
                    dve.wait_ge(gate_chain, val(t, G_STEPS, count[0]))

                dve.wait_ge(ag_done, val(t, 1, 1))
                chain(dve.tensor_tensor(logits[:, :], psA[:, P:NAG], gate_bb[:, :], ALU.add))
                dve.tensor_copy(xa[:, :], psA[:, 0:P]).then_inc(xa_copied, 1)
                chain(dve.max(out=top[:, :], in_=logits[:, :]))
                dve.tensor_tensor(gap[:, :], top[:, 1:2], top[:, 0:1], ALU.subtract).then_inc(gap_done, 1)
                chain(dve.max_index(out=topi[:, :], in_max=top[:, :], in_values=logits[:, :]))
                chain(dve.tensor_copy(topf[:, :], topi[:, :]))
                dve.wait_ge(e2_done, val(t, 1, 1))
                chain(dve.tensor_scalar(g2[:, :], e2[:, :], 1.0, None, ALU.add))
                chain(dve.reciprocal(g1[:, :], g2[:, :]))
                chain(dve.tensor_tensor(g2[:, :], e2[:, :], g1[:, :], ALU.mult))
                chain(dve.tensor_scalar(first[:, :], iota[:, :], topf[:, 0:1], g1[:, :], ALU.is_equal, ALU.mult))
                chain(dve.tensor_scalar(gates[:, :], iota[:, :], topf[:, 1:2], g2[:, :], ALU.is_equal, ALU.mult))
                chain(dve.tensor_tensor(gates[:, :], gates[:, :], first[:, :], ALU.add))
                assert count[0] == G_STEPS
                dve.wait_ge(xa_copied, val(t, 1, 1))
                dve.tensor_tensor(xa[:, :].rearrange("p (e r) -> p e r", r=R),
                                  xa[:, :].rearrange("p (e r) -> p e r", r=R),
                                  gates[:, :].rearrange("p (e o) -> p e o", o=1).broadcast_to([P, NE, R]),
                                  ALU.mult).then_inc(xa_done, 1)

            def xa_lo(t):
                dve.wait_ge(xathi_done, val(t, 1, 1))
                dve.tensor_tensor(xaT_lo[:, :], psX[:, 0:P], xaT_hi[:, :].bitcast(F32), ALU.subtract
                                  ).then_inc(xatlo_done, 1)

            def output(t, b, starts):
                dve.wait_ge(f_done, val(t, 1, 1))
                dve.wait_ge(y_done, val(t, 1, 1))
                dve.tensor_tensor(yb[:, :], psF[:, :], bw_b[:, :], ALU.add).then_inc(pf_free, 1)
                if starts:
                    dve.wait_ge(gb_in, b * 16 + 16)
                dve.wait_ge(pf_free, val(t, 1, 1))
                dve.tensor_tensor(yb[:, :], yb[:, :], gb[:, :], ALU.mult).then_inc(yb_done, 1)

            def norm_lo(t):
                dve.wait_ge(h2hi_done, val(t, 1, 1))
                dve.tensor_tensor(h2_lo[:, :, :], h2n[:, :, :], h2_hi[:, :, :].bitcast(F32), ALU.subtract
                                  ).then_inc(h2lo_done, 1)

            def head():
                for k in range(KT):
                    dve.wait_ge(wo_hi, k + 1)
                    dve.tensor_tensor(Wo_lo[:, k, :], Wo_in[:, k, :], Wo_hi[:, k, :].bitcast(F32), ALU.subtract
                                      ).then_inc(wo_ready, 1)
                for k in range(KT):
                    dve.wait_ge(ww_hi, k + 1)
                    dve.tensor_tensor(Ww_lo[:, k, :], Ww_in[:, k, :], Ww_hi[:, k, :].bitcast(F32), ALU.subtract
                                      ).then_inc(ww_ready, 1)
                dve.wait_ge(ww_hi, KT + 2)
                dve.tensor_tensor(AG_lo[:, :, :], AG_in[:, :, :], AG_hi[:, :, :].bitcast(F32), ALU.subtract
                                  ).then_inc(ww_ready, 1)
                dve.tensor_tensor(LB_lo[:, :], LB_in[:, :], LB_hi[:, :].bitcast(F32), ALU.subtract
                                  ).then_inc(ww_ready, 1)
                dve.wait_ge(iota_done, 1)
                dve.tensor_copy(iota[:, :], iota_i[:, :]).then_inc(iota_ready, 1)
                dve.wait_ge(iota_ready, 1)
                dve.wait_ge(rows_in, 48)
                residual((0, 0), 0, True)
                normalize((0, 0))
                norm_lo((0, 0))

            def body(t, b, b2):
                residual(add(t, 1), b2, new_batch(t, b, b2))
                gating(t)
                normalize(add(t, 1))
                xa_lo(t)
                output(t, b, True)
                norm_lo(add(t, 1))

            def tail(t, b):
                gating(t)
                xa_lo(t)
                output(t, b, True)

            run(dve, head, body, tail)


def program(nc, x, cT, wmod, wqkv, wo, w, ag, lb, bo, bw, gate_b, out, nb=B):
    gate_rows = nc.dram_tensor("gate_rows", [B, 2, E], F32, kind="Internal").ap()
    ctxT = nc.dram_tensor("ctxT", [nb * PAIRS, P, S], F32, kind="Internal").ap()
    with ExitStack() as ctx:
        identf = ctx.enter_context(nc.sbuf_tensor("identf", [P, P], F32))
        mod_cols = ctx.enter_context(nc.sbuf_tensor("mod_cols", [P, 4, KT, B], F32))
        modulation_phase(nc, cT, wmod, mod_cols, identf, gate_rows)
        attention_phase(nc, x, wqkv, mod_cols, identf, ctxT, nb)
        feed_forward_phase(nc, x, ctxT, gate_rows, mod_cols, identf, wo, w, ag, lb, bo, bw, gate_b, out, nb)


def kernel(L0_attn_x, L0_attn_Wq, L0_attn_Wk, L0_attn_Wv, L0_attn_Wo, L0_attn_bo, L0_ffn_W, L0_ffn_b,
           L0_ffn_lora_A, L0_ffn_lora_B, L0_ffn_gate_w, L0_ffn_gate_b, L0_c, L0_wmod):
    import numpy as np
    import concourse.bacc as bacc
    from concourse.bass_utils import run_bass_kernel_spmd

    def features_by_partition(a):
        return np.ascontiguousarray(a.T.reshape(KT, P, a.shape[0]).transpose(1, 0, 2))

    def by_pair(a):
        return a.T.reshape(KT, P, PAIRS, P).transpose(2, 1, 0, 3)

    c, W, A, gw = (np.asarray(a) for a in (L0_c, L0_ffn_W, L0_ffn_lora_A, L0_ffn_gate_w))
    arrays = {
        "x": np.ascontiguousarray(L0_attn_x),
        "cT": features_by_partition(c),
        "wmod": np.ascontiguousarray(L0_wmod),
        "wqkv": np.ascontiguousarray(np.stack([by_pair(np.asarray(a)) for a in (L0_attn_Wq, L0_attn_Wk, L0_attn_Wv)], 1)),
        "wo": features_by_partition(np.asarray(L0_attn_Wo)),
        "w": features_by_partition(W),
        "ag": features_by_partition(np.concatenate([A.reshape(NE * R, E), gw], 0)),
        "lb": np.ascontiguousarray(np.asarray(L0_ffn_lora_B).transpose(0, 2, 1).reshape(NE * R, E)),
        "bo": np.asarray(L0_attn_bo).reshape(1, E),
        "bw": np.asarray(L0_ffn_b).reshape(1, E),
        "gate_b": np.asarray(L0_ffn_gate_b).reshape(1, NE),
    }
    nc = bacc.Bacc("TRN2", target_bir_lowering=False, num_devices=1)
    args = [nc.dram_tensor(f"in_{n}", a.shape, F32, kind="ExternalInput").ap() for n, a in arrays.items()]
    out = nc.dram_tensor("out", (B, S, E), F32, kind="ExternalOutput").ap()
    program(nc, *args, out)
    r = run_bass_kernel_spmd(nc, [{f"in_{n}": a for n, a in arrays.items()}], core_ids=[0])
    return r.results[0]["out"]
```

```python
from contextlib import ExitStack

import concourse.bass as bass
from concourse import mybir

F32 = mybir.dt.float32
F32R = mybir.dt.float32r
BF16 = mybir.dt.bfloat16
I32 = mybir.dt.int32
U32 = mybir.dt.uint32
ALU = mybir.AluOpType
ACT = mybir.ActivationFunctionType
AX = mybir.AxisListType

P = 128
B, S, E = 4, 1024, 1024
H = 16
D = E // H
KT = E // P
TT = S // P
PAIRS = H // 2
NE, R = 8, 16
NAG = NE * R + NE
HALF = 512
EPS = 1e-5
QSCALE = D ** -0.5
MASKED = -3.0e38
RSQRT_MAGIC = 0x5F3759DF
NEWTON = 4

UNITS = 2 * TT


def unit_chunks(u):
    t = u % TT
    return [(k0, min(4, t + 1 - k0)) for k0 in range(0, t + 1, 4)]


CHUNK0 = [sum(len(unit_chunks(v)) for v in range(u)) for u in range(UNITS + 1)]
CHUNKS = CHUNK0[UNITS]
GROUPS = UNITS // 2
ZUNITS = 6
ZMM = KT * 3
SLOTS = UNITS + 3
ZPARTS = 3
LN_CHUNKS = 2 * KT
STAT_CHUNKS = 2 * TT

LN_FIRST, LN_END = 7, 14
PLAIN = [[j] if j < ZPARTS * ZUNITS else [] for j in range(SLOTS)]
AFTER_NORM = [[] for _ in range(LN_END + 1)] + [[2 * i, 2 * i + 1] for i in range(4)] + [
    [j] for j in range(8, ZPARTS * ZUNITS)] + [[]]


def slot_of(plan, unit):
    return next(j for j, parts in enumerate(plan) if ZPARTS * unit + ZPARTS - 1 in parts)


def norm_statistics(eng, step, tiles, st, dm, mean, rstd, v, half_v, t):
    sums = mean
    spread = sums.rearrange("p (t o) -> p t o", o=1).broadcast_to([P, tiles, 4])
    step(eng.tensor_reduce(sums, st[:, :, :, 1], AX.X, ALU.add))
    step(eng.scalar_tensor_tensor(out=dm, in0=spread, scalar=0.25, in1=st[:, :, :, 1],
                                  op0=ALU.mult, op1=ALU.subtract))
    eng.tensor_scalar(mean, sums, 0.25, None, ALU.mult)
    step(eng.tensor_tensor(dm, dm, dm, ALU.mult))
    step(eng.scalar_tensor_tensor(out=dm, in0=dm, scalar=E / 4.0, in1=st[:, :, :, 2], op0=ALU.mult, op1=ALU.add))
    step(eng.tensor_reduce(t, dm, AX.X, ALU.add))
    eng.tensor_scalar(half_v, t, 0.5 / E, 0.5 * EPS, ALU.mult, ALU.add)
    step(eng.tensor_scalar(v, t, 1.0 / E, EPS, ALU.mult, ALU.add))
    step(eng.tensor_scalar(t.bitcast(I32), v.bitcast(I32), 1, None, ALU.logical_shift_right))
    step(eng.tensor_scalar(rstd.bitcast(I32), t.bitcast(I32), -1.0, float(RSQRT_MAGIC), ALU.mult, ALU.add))
    for _ in range(NEWTON):
        if tiles == 1:
            step(eng.scalar_tensor_tensor(out=t, in0=rstd, scalar=half_v, in1=rstd, op0=ALU.mult, op1=ALU.mult))
        else:
            step(eng.tensor_tensor(t, rstd, rstd, ALU.mult))
            step(eng.tensor_tensor(t, t, half_v, ALU.mult))
        step(eng.scalar_tensor_tensor(out=rstd, in0=t, scalar=1.5, in1=rstd, op0=ALU.subtract, op1=ALU.mult))


def stat_steps(tiles):
    return 8 + (2 if tiles == 1 else 3) * NEWTON


def modulation_phase(nc, cT, wmod, mod_cols, identf, gate_rows):
    CH = 6 * E // HALF
    RING = 3
    with ExitStack() as ctx:
        def sb(name, shape, dt=F32):
            return ctx.enter_context(nc.sbuf_tensor(name, shape, dt))

        def sem(name):
            return ctx.enter_context(nc.semaphore(name))

        c_in = sb("c_in", [P, KT, B])
        c_exp = sb("c_exp", [P, KT, B])
        c_silu = sb("c_silu", [P, KT, B])
        wring = sb("wring", [P, RING, KT, HALF])
        rows = sb("rows", [B, 6 * E])
        g_sign = sb("g_sign", [B, 2, E])
        g_abs = sb("g_abs", [B, 2, E])
        psM = ctx.enter_context(nc.psum_tensor("psM", [P, 2, HALF], F32))
        psMT = ctx.enter_context(nc.psum_tensor("psMT", [P, 4, KT, B], F32))
        c_loaded = sem("c_loaded")
        w_loaded = [sem(f"w_loaded{i}") for i in range(RING)]
        exp_done, dve_chain = sem("m_exp_done"), sem("m_dve_chain")
        silu_ready, ident_zeroed, ident_ready = sem("silu_ready"), sem("ident_zeroed"), sem("ident_ready")
        row_ready, row_copied = sem("row_ready"), sem("row_copied")
        cols_ready, cols_copied, gates_ready, gates_out = (
            sem("cols_ready"), sem("cols_copied"), sem("gates_ready"), sem("gates_out"))
        block = ctx.enter_context(nc.Block())

        @block.sync
        def _(sp):
            sp.dma_start(c_in[:, :, :], cT).then_inc(c_loaded, 16)
            for n in range(CH):
                if n >= RING:
                    sp.wait_ge(row_ready, n - RING + 1)
                sp.dma_start(wring[:, n % RING, :, :],
                             wmod[:, n * HALF:(n + 1) * HALF].rearrange("(k p) n -> p k n", p=P)
                             ).then_inc(w_loaded[n % RING], 16)
            sp.wait_ge(gates_ready, 1)
            sp.dma_start(gate_rows, g_abs[:, :, :]).then_inc(gates_out, 16)
            sp.wait_ge(gates_out, 16)

        @block.gpsimd
        def _(pool):
            pool.memset(identf[:, :], 0.0).then_inc(ident_zeroed, 1)
            pool.wait_ge(ident_zeroed, 1)
            pool.affine_select(out=identf[:, :], in_=identf[:, :], compare_op=ALU.not_equal, fill=1.0,
                               base=0, pattern=[[-1, P]], channel_multiplier=1).then_inc(ident_ready, 1)

        @block.scalar
        def _(act):
            act.wait_ge(c_loaded, 16)
            act.activation(c_exp[:, :, :], c_in[:, :, :], ACT.Exp, scale=-1.0).then_inc(exp_done, 1)
            for n in range(CH):
                act.wait_ge(row_ready, n + 1)
                act.activation(rows[:, n * HALF:(n + 1) * HALF], psM[0:B, n % 2, :], ACT.Copy
                               ).then_inc(row_copied, 1)

        @block.tensor
        def _(pe):
            pe.wait_ge(silu_ready, 1)
            for n in range(CH):
                pe.wait_ge(w_loaded[n % RING], 16 * (n // RING + 1))
                if n >= 2:
                    pe.wait_ge(row_copied, n - 1)
                for k in range(KT):
                    last = pe.matmul(psM[0:B, n % 2, :], c_silu[:, k, :], wring[:, n % RING, k, :],
                                     start=k == 0, stop=k == KT - 1)
                last.then_inc(row_ready, 1)
            pe.wait_ge(row_copied, CH)
            pe.wait_ge(ident_ready, 1)
            for v, chunk in enumerate((0, 1, 3, 4)):
                for k in range(KT):
                    c0 = chunk * E + k * P
                    last = pe.transpose(psMT[:, v, k, :], rows[:, c0:c0 + P], identf[0:B, 0:B])
            last.then_inc(cols_ready, 1)

        @block.vector
        def _(dve):
            chain = [0]

            def step(ins):
                chain[0] += 1
                ins.then_inc(dve_chain, 1)
                dve.wait_ge(dve_chain, chain[0])

            dve.wait_ge(exp_done, 1)
            step(dve.tensor_scalar(c_exp[:, :, :], c_exp[:, :, :], 1.0, None, ALU.add))
            step(dve.reciprocal(c_exp[:, :, :], c_exp[:, :, :]))
            dve.tensor_tensor(c_silu[:, :, :], c_in[:, :, :], c_exp[:, :, :], ALU.mult).then_inc(silu_ready, 1)
            dve.wait_ge(row_copied, CH)
            gates = rows[:, :].rearrange("b (c e) -> b c e", c=6)[:, 2:6:3, :]
            step(dve.tensor_scalar(g_sign[:, :, :], gates, 0.0, 2.0, ALU.is_ge, ALU.mult))
            step(dve.tensor_scalar(g_sign[:, :, :], g_sign[:, :, :], 1.0, None, ALU.subtract))
            step(dve.scalar_tensor_tensor(out=g_abs[:, :, :], in0=gates, scalar=-1.0, in1=gates,
                                          op0=ALU.mult, op1=ALU.max))
            step(dve.tensor_scalar(g_abs[:, :, :], g_abs[:, :, :], 0.25, None, ALU.max))
            dve.tensor_tensor(g_abs[:, :, :], g_abs[:, :, :], g_sign[:, :, :], ALU.mult).then_inc(gates_ready, 1)
            dve.wait_ge(cols_ready, 1)
            dve.tensor_copy(mod_cols[:, 0:4:2, :, :], psMT[:, 0:4:2, :, :]).then_inc(cols_copied, 1)
            dve.tensor_scalar(mod_cols[:, 1:4:2, :, :], psMT[:, 1:4:2, :, :], 1.0, None, ALU.add
                              ).then_inc(cols_copied, 1)
            dve.wait_ge(cols_copied, 2)


def attention_phase(nc, x, wqkv, mod_cols, identf, ctxT, wo, Wo, wo_at, nb=B):
    with ExitStack() as ctx:
        def sb(name, shape, dt=F32):
            return ctx.enter_context(nc.sbuf_tensor(name, shape, dt))

        def sem(name):
            return ctx.enter_context(nc.semaphore(name))

        base = nc.sbuf_base
        sb("pair_arena", [P, 2 * 4 * 2 * S])
        KB4 = 4 * 2 * S
        Qs, Qx, Ks, Vs = [], [], [], []
        for par in range(2):
            o = base + par * 4 * KB4
            Qs.append(nc.alloc_sbuf_tensor_at(f"Qs{par}", [P, 2, S], F32R, offset=o))
            Qx.append(nc.alloc_sbuf_tensor_at(f"Qx{par}", [P, 2, S], F32R, offset=o + KB4))
            Ks.append(nc.alloc_sbuf_tensor_at(f"Ks{par}", [P, 2, S], F32R, offset=o + 2 * KB4))
            Vs.append(nc.alloc_sbuf_tensor_at(f"Vs{par}", [P, 2, TT, 2 * D], F32R, offset=o + 3 * KB4))
        xn = nc.alloc_sbuf_tensor_at("xn", [P, TT, E], F32, offset=base)

        hT = [nc.alloc_sbuf_tensor_at(n, [P, KT, S], F32R, offset=wo_at + i * 4 * KT * S)
              for i, n in enumerate(("hT_hi", "hT_lo"))]
        Wo_hi, Wo_lo, Wo_in = Wo
        W = [sb("W_hi", [P, 3, KT, P], F32R), sb("W_lo", [P, 3, KT, P], F32R)]
        W_in = sb("W_in", [P, 2, KT, P])
        PT = [[sb(f"PT_{part}{g}", [P, 6 + 2 * g, 2 * P], F32R) for part in ("hi", "lo")] for g in range(2)]
        Pb = sb("Pb", [P, 2, S])
        Zs = sb("Zs", [P, HALF])
        ctxs = sb("ctxs", [P, S])
        ctx_lo = sb("ctx_lo", [D, 2 * P])
        hn = [Zs, sb("hn1", [P, HALF])]
        ident16, mask16 = sb("ident16", [P, P], BF16), sb("mask16", [P, P], BF16)
        one = sb("one", [P, 1])
        negmax, rowsum, rinv = sb("negmax", [P, UNITS]), sb("rowsum", [P, UNITS]), sb("rinv", [P, UNITS])
        st, dm = sb("st", [P, TT, 4, 3]), sb("dm", [P, TT, 4])
        mean, rstd, var, hvar, rtmp = [sb(n, [P, TT]) for n in ("mean", "rstd", "var", "hvar", "rtmp")]
        modb = sb("modb", [P, 2, KT])

        def psum(name, shape):
            return ctx.enter_context(nc.psum_tensor(name, shape, F32))

        psS = [psum("psS0", [P, S]), psum("psS1", [P, S])]
        psT = [psum("psT0", [P, HALF]), psum("psT1", [P, HALF])]
        psPV = psum("psPV", [P, HALF])
        psZ = psum("psZ", [P, HALF])

        scores_done, max_done, exp_done, norm_done, rinv_done = (
            sem("scores_done"), sem("max_done"), sem("exp_done"), sem("norm_done"), sem("rinv_done"))
        tp_done, pthi_done, ptlo_done = sem("tp_done"), sem("pthi_done"), sem("ptlo_done")
        pv_done, ctxlo_done, ctx_done, ctx_out = sem("pv_done"), sem("ctxlo_done"), sem("ctx_done"), sem("ctx_out")
        z_done, zs_done, qkhi_done, qklo_done, qx_done = (
            sem("z_done"), sem("zs_done"), sem("qkhi_done"), sem("qklo_done"), sem("qx_done"))
        vt_done, vhi_done, vlo_done = sem("vt_done"), sem("vhi_done"), sem("vlo_done")
        w_in, whi_done, w_ready = [sem("w_in0"), sem("w_in1")], sem("whi_done"), sem("w_ready")
        consts_a, consts_ready = sem("consts_a"), sem("consts_ready")
        x_in = [sem("x_in0"), sem("x_in1")]
        bn0_done = sem("bn0_done")
        xc_in, xc_used = sem("xc_in"), sem("xc_used")
        wo_in, wo_hi, wo_lo = [sem(f"wo_in{k}") for k in range(KT // 2)], sem("wo_hi"), sem("wo_lo")
        st_done, xnorm_done, modb_done = sem("st_done"), sem("xnorm_done"), sem("modb_done")
        lnt_done, lnaff_done, lnhi_done, lnlo_done = (
            sem("lnt_done"), sem("lnaff_done"), sem("lnhi_done"), sem("lnlo_done"))

        def val(hk, per, n):
            h, k = hk
            return h * (2 * per) + (k * per + max(n, 0))

        def nxt(hk):
            return (hk[0], hk[1] + 1)

        def prev(hk):
            return (hk[0], hk[1] - 1)

        def run(eng, layer_norm, step):
            layer_norm(0)
            step(None, (0, 0), 1, True)

            def batch(b, last):
                with eng.Fori(0, 3) as c:
                    h = eng.snap(4 * b + c)
                    step((h, 0), (h, 1), 2 * c + 2, True)
                    step((h, 1), (h, 2), 2 * c + 3, True)
                h = 4 * b + 3
                step((h, 0), (h, 1), 0, not last, stats=None if last else b + 1)
                if last:
                    step((h, 1), None, None, False)
                else:
                    step((h, 1), (4 * b + 4, 0), 1, True, norm=b + 1)

            if nb > 1:
                with eng.Fori(0, nb - 1) as b:
                    batch(b, False)
            batch(nb - 1, True)

        block = ctx.enter_context(nc.Block())

        @block.sync
        def _(sp):
            def load_w(hk, pair, part):
                n = 3 * hk[1] + part
                if not (isinstance(hk[0], int) and val(hk, 3, part) < 2):
                    sp.wait_ge(w_ready, val(hk, 3, part - 1) if part else val(prev(hk), 3, 2))
                sp.dma_start(W_in[:, n % 2, :, :], wqkv[bass.ds(pair, 1), part, :, :, :] if not isinstance(pair, int)
                             else wqkv[pair:pair + 1, part, :, :, :]).then_inc(w_in[n % 2], 16)

            def load_x(b):
                xt = x.rearrange("b (t p) e -> b p t e", p=P)
                if not (isinstance(b, int) and b == 0):
                    sp.wait_ge(ctx_done, b * (PAIRS * GROUPS) - GROUPS)
                for half in range(2):
                    sp.dma_start(xn[:, 4 * half:4 * half + 4, :],
                                 (xt[b] if isinstance(b, int) else xt[bass.ds(b, 1)].rearrange("o p t e -> (o p) t e"))
                                 [:, 4 * half:4 * half + 4, :]).then_inc(x_in[half], 16)

            def step(att, proj, wnext, prefetch, stats=None, norm=None):
                if norm is not None:
                    load_x(norm)
                if proj is not None:
                    par = proj[1] % 2
                    if prefetch:
                        load_w(nxt(proj), wnext, 0)
                    sp.wait_ge(qklo_done, val(proj, 8, 4))
                    sp.dma_start(Qx[par][0:D, :, :].bitcast(F32), Qs[par][D:P, :, :].bitcast(F32)).then_inc(qx_done, 16)
                    sp.dma_start(Qx[par][D:P, :, :].bitcast(F32), Qs[par][0:D, :, :].bitcast(F32)).then_inc(qx_done, 16)
                    if prefetch:
                        load_w(nxt(proj), wnext, 1)
                        load_w(nxt(proj), wnext, 2)
                if proj is None:
                    sp.wait_ge(z_done, ZUNITS * nb * PAIRS)
                    for k in range(0, KT, 2):
                        sp.dma_start(Wo_in[:, k:k + 2, :], wo[:, k:k + 2, :]).then_inc(wo_in[k // 2], 16)
                if att is not None:
                    sp.wait_ge(ctx_done, val(att, GROUPS, GROUPS))
                    h, k = att
                    n = h * 2 + k
                    sp.dma_start((ctxT[n:n + 1] if isinstance(n, int) else ctxT[bass.ds(n, 1)])
                                 .rearrange("o p t -> (o p) t"), ctxs[:, :]).then_inc(ctx_out, 16)

            load_x(0)
            for part in range(3):
                load_w((0, 0), 0, part)
            run(sp, lambda b: None, step)
            sp.wait_ge(ctx_out, 16 * (nb * PAIRS + 1))

        @block.gpsimd
        def _(pool):
            pool.memset(ident16[:, :], 0.0).then_inc(consts_a, 1)
            pool.memset(mask16[:, :], 0.0).then_inc(consts_a, 1)
            pool.memset(one[:, :], 1.0).then_inc(consts_a, 1)
            pool.wait_ge(consts_a, 3)
            pool.affine_select(out=ident16[:, :], in_=ident16[:, :], compare_op=ALU.not_equal, fill=1.0,
                               base=0, pattern=[[-1, P]], channel_multiplier=1).then_inc(consts_ready, 1)
            pool.affine_select(out=mask16[:, :], in_=mask16[:, :], compare_op=ALU.is_ge, fill=MASKED,
                               base=0, pattern=[[-1, P]], channel_multiplier=1).then_inc(consts_ready, 1)

            def split_w(hk, part):
                n = 3 * hk[1] + part
                pool.wait_ge(w_in[n % 2], hk[0] * 48 + 16 * (n // 2 + 1))
                if not (isinstance(hk[0], int) and hk == (0, 0)):
                    pool.wait_ge(z_done, val(prev(hk), ZUNITS, 2 * part + 2))
                pool.tensor_tensor(out=W[0][:, part, :, :], in0=W_in[:, n % 2, :, :],
                                   in1=one[:, 0:1].rearrange("p (a b) -> p a b", a=1).broadcast_to([P, KT, P]),
                                   op=ALU.mult).then_inc(whi_done, 1)
                pool.wait_ge(whi_done, val(hk, 3, part + 1))
                pool.tensor_tensor(out=W[1][:, part, :, :], in0=W_in[:, n % 2, :, :],
                                   in1=W[0][:, part, :, :].bitcast(F32), op=ALU.subtract).then_inc(w_ready, 1)

            for part in range(3):
                split_w((0, 0), part)

            def norm_lo(b):
                for n in range(LN_CHUNKS):
                    half, k = n // KT, n % KT
                    c = slice(half * HALF, (half + 1) * HALF)
                    pool.wait_ge(lnhi_done, b * LN_CHUNKS + n + 1)
                    pool.tensor_tensor(out=hT[1][:, k, c], in0=hn[n % 2][:, :], in1=hT[0][:, k, c].bitcast(F32),
                                       op=ALU.subtract).then_inc(lnlo_done, 1)

            def step(att, proj, wnext, prefetch, stats=None, norm=None):
                if norm is not None:
                    norm_lo(norm)
                if proj is not None and prefetch:
                    for part in range(3):
                        split_w(nxt(proj), part)
                if proj is None:
                    for k in range(KT):
                        pool.wait_ge(wo_hi, k + 1)
                        pool.tensor_tensor(out=Wo_lo[:, k, :], in0=Wo_in[:, k, :],
                                           in1=Wo_hi[:, k, :].bitcast(F32), op=ALU.subtract).then_inc(wo_lo, 1)
                    pool.wait_ge(wo_lo, KT)

            run(pool, norm_lo, step)

        @block.tensor
        def _(pe):
            def scores(att, u):
                par, head, t = att[1] % 2, u // TT, u % TT
                if u == 0:
                    pe.wait_ge(qklo_done, val(att, 8, 8))
                    pe.wait_ge(qx_done, val(att, 32, 32))
                if u >= 2:
                    pe.wait_ge(exp_done, val(att, UNITS, u - 1))
                for half in range(t // 4 + 1):
                    c0 = half * HALF
                    n = min(HALF, (t + 1) * P - c0)
                    diagonal = half == t // 4
                    out, keys = psS[u % 2][:, c0:c0 + n], Ks[par][:, head, c0:c0 + n]
                    q = slice(t * P, (t + 1) * P)
                    pe.matmul(out, Qs[par][:, head, q], keys, start=True, stop=False)
                    last = pe.matmul(out, Qx[par][:, head, q], keys, start=False, stop=not diagonal)
                    if diagonal:
                        last = pe.matmul(psS[u % 2][:, t * P:(t + 1) * P], ident16[:, :], mask16[:, :],
                                         start=False, stop=True)
                last.then_inc(scores_done, 1)

            def transposes(att, u):
                pe.wait_ge(norm_done, val(att, UNITS, u + 1))
                for n, (k0, nk) in enumerate(unit_chunks(u), CHUNK0[u]):
                    if n >= 2:
                        pe.wait_ge(ptlo_done, val(att, CHUNKS, n - 1))
                    for i in range(nk):
                        last = pe.transpose(psT[n % 2][:, i * P:(i + 1) * P],
                                            Pb[:, u % 2, (k0 + i) * P:(k0 + i + 1) * P], identf[:, :])
                    last.then_inc(tp_done, 1)

            def context(att, g, v_seen):
                par, head, gg = att[1] % 2, g // 4, g % 4
                pe.wait_ge(ptlo_done, val(att, CHUNKS, CHUNK0[2 * g + 2]))
                if g:
                    pe.wait_ge(ctx_done, val(att, GROUPS, g))
                pe.wait_ge(vlo_done, v_seen)
                hi, lo = PT[gg % 2]
                for k in range(2 * gg + 2):
                    q = slice(P if k == 2 * gg + 1 else 0, 2 * P)
                    v = Vs[par][:, head, k, :]
                    pe.matmul(psPV[:, q], v, hi[:, k, q], start=k == 0, stop=False)
                    last = pe.matmul(psPV[:, q], v, lo[:, k, q], start=False, stop=k == 2 * gg + 1)
                last.then_inc(pv_done, 1)

            def project(proj, norm, unit, part):
                which, half = unit // 2, unit % 2
                if part == 0 and unit < 2 and norm is not None:
                    pe.wait_ge(lnlo_done, norm * LN_CHUNKS + (half + 1) * KT)
                    pe.wait_ge(lnaff_done, norm * LN_CHUNKS + LN_CHUNKS)
                if part == 0:
                    pe.wait_ge(zs_done, val(proj, ZUNITS, unit))
                    if half == 0:
                        pe.wait_ge(w_ready, val(proj, 3, which + 1))
                mms = [(k, a, b) for k in range(KT) for a, b in ((0, 0), (0, 1), (1, 0))]
                lo, hi = part * ZMM // ZPARTS, (part + 1) * ZMM // ZPARTS
                for i in range(lo, hi):
                    k, a, b = mms[i]
                    last = pe.matmul(psZ[:, :], W[a][:, which, k, :], hT[b][:, k, half * HALF:(half + 1) * HALF],
                                     start=i == 0, stop=i == ZMM - 1)
                if part == ZPARTS - 1:
                    last.then_inc(z_done, 1)

            def v_transposes(proj, half, ctx_seen):
                pe.wait_ge(zs_done, val(proj, ZUNITS, 5 + half))
                pe.wait_ge(ctx_done, ctx_seen)
                pe.wait_ge(vlo_done, val(proj, 2, half))
                for i in range(4):
                    last = pe.transpose(psPV[:, i * P:(i + 1) * P], Zs[:, i * P:(i + 1) * P], identf[:, :])
                last.then_inc(vt_done, 1)

            def norm_chunk(b, n, banks):
                half, k = n // KT, n % KT
                if n % KT == 0:
                    pe.wait_ge(xnorm_done, b * TT + 4 * half + 4)
                if not isinstance(b, int) or b * LN_CHUNKS + n + 1 > len(banks):
                    pe.wait_ge(lnaff_done, b * LN_CHUNKS + n - len(banks) + 1)
                for i in range(4):
                    last = pe.transpose(banks[n % len(banks)][:, i * P:(i + 1) * P],
                                        xn[:, 4 * half + i, k * P:(k + 1) * P], identf[:, :])
                last.then_inc(lnt_done, 1)

            def layer_norm(b):
                for n in range(LN_CHUNKS):
                    norm_chunk(b, n, psT)

            def step(att, proj, wnext, prefetch, stats=None, norm=None):
                plan = PLAIN if norm is None else AFTER_NORM
                v_slot = [slot_of(plan, 4) + 1, slot_of(plan, 5) + 1]
                for j in range(len(plan)):
                    chunks = [2 * (j - LN_FIRST), 2 * (j - LN_FIRST) + 1] if (
                        norm is not None and 0 <= j - LN_FIRST < LN_CHUNKS // 2) else []
                    if att is not None:
                        if j < UNITS:
                            scores(att, j)
                        if chunks:
                            norm_chunk(norm, chunks[0], [psZ])
                        if 2 <= j < UNITS + 2:
                            transposes(att, j - 2)
                        if 4 <= j < SLOTS and j % 2 == 0:
                            other = proj is not None and j > v_slot[0]
                            context(att, (j - 4) // 2, val(proj, 2, 1) if other else val(att, 2, 2))
                        if chunks:
                            norm_chunk(norm, chunks[1], [psZ])
                    if proj is not None:
                        for part in plan[j]:
                            project(proj, 0 if att is None else norm, part // ZPARTS, part % ZPARTS)
                        for half in range(2):
                            if j == v_slot[half]:
                                v_transposes(proj, half, val(att, GROUPS, 6) if j < SLOTS - 1 and att is not None
                                             else val(proj, GROUPS, 0))

            pe.wait_ge(consts_ready, 2)
            run(pe, layer_norm, step)

        @block.scalar
        def _(act):
            def pt_hi(att, u):
                g = u // 2
                hi = PT[g % 2][0]
                for n, (k0, nk) in enumerate(unit_chunks(u), CHUNK0[u]):
                    act.wait_ge(tp_done, val(att, CHUNKS, n + 1))
                    if g >= 2:
                        act.wait_ge(pv_done, val(att, GROUPS, g - 1))
                    q = (u % 2) * P
                    act.activation(hi[:, k0:k0 + nk, q:q + P],
                                   psT[n % 2][:, 0:nk * P].rearrange("p (k q) -> p k q", q=P), ACT.Copy
                                   ).then_inc(pthi_done, 1)

            def exps(att, u):
                n = (u % TT + 1) * P
                act.wait_ge(max_done, val(att, UNITS, u + 1))
                if u >= 2:
                    act.wait_ge(tp_done, val(att, CHUNKS, CHUNK0[u - 1]))
                act.activation(Pb[:, u % 2, 0:n], psS[u % 2][:, 0:n], ACT.Exp, bias=negmax[:, u:u + 1],
                               accum_out=rowsum[:, u:u + 1]).then_inc(exp_done, 1)

            def context_lo(att, g):
                act.wait_ge(pv_done, val(att, GROUPS, g + 1))
                if g:
                    act.wait_ge(ctx_done, val(att, GROUPS, g))
                act.activation(ctx_lo[:, :], psPV[D:P, 0:2 * P], ACT.Copy).then_inc(ctxlo_done, 1)

            def copy_z(proj, unit, norm):
                act.wait_ge(z_done, val(proj, ZUNITS, unit + 1))
                if unit == 0:
                    act.wait_ge(vt_done, val(proj, 2, 0))
                    if norm is not None:
                        act.wait_ge(lnlo_done, norm * LN_CHUNKS + LN_CHUNKS)
                elif unit == 5:
                    act.wait_ge(vt_done, val(proj, 2, 1))
                else:
                    act.wait_ge(qklo_done, val(proj, 8, 2 * unit))
                act.activation(Zs[:, :], psZ[:, :], ACT.Copy).then_inc(zs_done, 1)

            def qk_hi(proj, unit):
                par, c = proj[1] % 2, slice((unit % 2) * HALF, (unit % 2 + 1) * HALF)
                dst = (Qs if unit < 2 else Ks)[par]
                act.wait_ge(zs_done, val(proj, ZUNITS, unit + 1))
                for head in range(2):
                    rows = slice(head * D, (head + 1) * D)
                    act.activation(dst[rows, head, c], Zs[rows, :], ACT.Copy, scale=QSCALE if unit < 2 else 1.0
                                   ).then_inc(qkhi_done, 1)

            def v_hi(proj, half):
                act.wait_ge(vt_done, val(proj, 2, half + 1))
                act.activation(Vs[proj[1] % 2][:, :, 4 * half:4 * half + 4, 0:D],
                               psPV[:, :].rearrange("p (t h d) -> p h t d", h=2, d=D), ACT.Copy
                               ).then_inc(vhi_done, 1)

            def norm_affine(b, n, banks):
                k = n % KT
                act.wait_ge(lnt_done, b * LN_CHUNKS + n + 1)
                if n >= 2:
                    act.wait_ge(lnlo_done, b * LN_CHUNKS + n - 1)
                act.activation(hn[n % 2][:, :], banks[n % len(banks)][:, :], ACT.Identity,
                               bias=modb[:, 0, k:k + 1], scale=modb[:, 1, k:k + 1]).then_inc(lnaff_done, 1)

            def layer_norm(b):
                act.wait_ge(modb_done, b + 1)
                for n in range(LN_CHUNKS):
                    norm_affine(b, n, psT)

            def load_chunk(b, n):
                if n:
                    act.wait_ge(xc_used, b * STAT_CHUNKS + n - STAT_CHUNKS)
                src = x.rearrange("b (t p) e -> b t p e", p=P)
                src = src[b:b + 1] if isinstance(b, int) else src[bass.ds(b, 1)]
                act.dma_start(hn[1][:, :], src[:, n // 2, :, (n % 2) * HALF:(n % 2 + 1) * HALF]
                              .rearrange("o p e -> (o p) e")).then_inc(xc_in, 16)

            def step(att, proj, wnext, prefetch, stats=None, norm=None):
                plan = PLAIN if norm is None else AFTER_NORM
                ends = {slot_of(plan, unit): unit for unit in range(ZUNITS)}
                if norm is not None:
                    act.wait_ge(modb_done, norm + 1)
                for j in range(len(plan)):
                    chunks = [2 * (j - LN_FIRST), 2 * (j - LN_FIRST) + 1] if (
                        norm is not None and 0 <= j - LN_FIRST < LN_CHUNKS // 2) else []
                    if att is not None:
                        if chunks:
                            norm_affine(norm, chunks[0], [psZ])
                        if 2 <= j < UNITS + 2:
                            pt_hi(att, j - 2)
                        if j < UNITS:
                            exps(att, j)
                        if 4 <= j < SLOTS and j % 2 == 0:
                            context_lo(att, (j - 4) // 2)
                        if chunks:
                            norm_affine(norm, chunks[1], [psZ])
                    if proj is not None:
                        unit = ends.get(j - 1)
                        if unit is not None and unit < 4:
                            qk_hi(proj, unit)
                        elif unit is not None:
                            v_hi(proj, unit - 4)
                        if j in ends:
                            copy_z(proj, ends[j], 0 if att is None else norm)
                    if stats is not None and j < STAT_CHUNKS:
                        load_chunk(stats, j)
                    if proj is None and j % 2 == 0 and j // 2 < KT:
                        k = j // 2
                        act.wait_ge(wo_in[k // 2], 16)
                        act.activation(Wo_hi[:, k, :], Wo_in[:, k, :], ACT.Copy).then_inc(wo_hi, 1)

            run(act, layer_norm, step)

        @block.vector
        def _(dve):
            def row_max(att, u):
                dve.wait_ge(scores_done, val(att, UNITS, u + 1))
                dve.tensor_reduce(negmax[:, u:u + 1], psS[u % 2][:, 0:(u % TT + 1) * P], AX.X, ALU.max,
                                  negate=True).then_inc(max_done, 1)

            def invert(att, u):
                dve.wait_ge(exp_done, val(att, UNITS, u + 1))
                dve.reciprocal(rinv[:, u:u + 1], rowsum[:, u:u + 1]).then_inc(rinv_done, 1)

            def normalize(att, u):
                n = (u % TT + 1) * P
                dve.wait_ge(rinv_done, val(att, UNITS, u + 1))
                dve.tensor_scalar(Pb[:, u % 2, 0:n], Pb[:, u % 2, 0:n], rinv[:, u:u + 1], None, ALU.mult
                                  ).then_inc(norm_done, 1)

            def pt_lo(att, u):
                hi, lo = PT[(u // 2) % 2]
                for n, (k0, nk) in enumerate(unit_chunks(u), CHUNK0[u]):
                    dve.wait_ge(pthi_done, val(att, CHUNKS, n + 1))
                    q = (u % 2) * P
                    dve.tensor_tensor(lo[:, k0:k0 + nk, q:q + P],
                                      psT[n % 2][:, 0:nk * P].rearrange("p (k q) -> p k q", q=P),
                                      hi[:, k0:k0 + nk, q:q + P].bitcast(F32), ALU.subtract
                                      ).then_inc(ptlo_done, 1)

            def context_sum(att, g):
                head, gg = g // 4, g % 4
                dve.wait_ge(ctxlo_done, val(att, GROUPS, g + 1))
                if g == 0:
                    dve.wait_ge(ctx_out, val(att, 16, 16))
                dve.tensor_tensor(ctxs[head * D:(head + 1) * D, gg * 2 * P:(gg + 1) * 2 * P],
                                  psPV[0:D, 0:2 * P], ctx_lo[:, :], ALU.add).then_inc(ctx_done, 1)

            def qk_lo(proj, unit):
                par, c = proj[1] % 2, slice((unit % 2) * HALF, (unit % 2 + 1) * HALF)
                dst = (Qs if unit < 2 else Ks)[par]
                for head in range(2):
                    rows, other = slice(head * D, (head + 1) * D), slice((1 - head) * D, (2 - head) * D)
                    dve.wait_ge(qkhi_done, val(proj, 8, 2 * unit + head + 1))
                    if unit < 2:
                        ins = dve.scalar_tensor_tensor(out=dst[other, head, c], in0=Zs[rows, :], scalar=QSCALE,
                                                       in1=dst[rows, head, c].bitcast(F32), op0=ALU.mult,
                                                       op1=ALU.subtract)
                    else:
                        ins = dve.tensor_tensor(dst[other, head, c], Zs[rows, :], dst[rows, head, c].bitcast(F32),
                                                ALU.subtract)
                    ins.then_inc(qklo_done, 1)

            def v_lo(proj, half):
                v = Vs[proj[1] % 2][:, :, 4 * half:4 * half + 4, :]
                dve.wait_ge(vhi_done, val(proj, 2, half + 1))
                dve.tensor_tensor(v[:, :, :, D:2 * D], psPV[:, :].rearrange("p (t h d) -> p h t d", h=2, d=D),
                                  v[:, :, :, 0:D].bitcast(F32), ALU.subtract).then_inc(vlo_done, 1)

            def norm_chain(b):
                count = [0]

                def chain(ins):
                    count[0] += 1
                    ins.then_inc(st_done, 1)
                    dve.wait_ge(st_done, b * stat_steps(TT) + count[0])
                return chain

            def piece_statistics(b, n):
                dve.wait_ge(xc_in, b * (16 * STAT_CHUNKS) + 16 * (n + 1 - STAT_CHUNKS))
                ins = dve.bn_stats(st[:, n // 2, 2 * (n % 2):2 * (n % 2) + 2, :].rearrange("p a c -> p (a c)"),
                                   hn[1][:, :])
                ins.then_inc(xc_used, 1)

            def statistics(b, chain):
                norm_statistics(dve, chain, TT, st[:, :, :, :], dm[:, :, :], mean[:, :], rstd[:, :],
                                var[:, :], hvar[:, :], rtmp[:, :])

            def columns(b):
                bs = slice(b, b + 1) if isinstance(b, int) else bass.ds(b, 1)
                dve.tensor_copy(modb[:, :, :], mod_cols[:, 0:2, :, bs].rearrange("p v k o -> p v (k o)")
                                ).then_inc(modb_done, 1)

            def normalize_x(b, t):
                if t % 4 == 0:
                    dve.wait_ge(x_in[t // 4], b * 16 + 16)
                dve.tensor_scalar(xn[:, t, :], xn[:, t, :], mean[:, t:t + 1], rstd[:, t:t + 1],
                                  ALU.subtract, ALU.mult).then_inc(xnorm_done, 1)

            def norm_hi(b, n):
                half, k = n // KT, n % KT
                dve.wait_ge(lnaff_done, b * LN_CHUNKS + n + 1)
                dve.tensor_copy(hT[0][:, k, half * HALF:(half + 1) * HALF], hn[n % 2][:, :]).then_inc(lnhi_done, 1)

            def layer_norm(b):
                columns(b)
                for t in range(TT):
                    if t % 4 == 0:
                        dve.wait_ge(x_in[t // 4], b * 16 + 16)
                    for half in range(2):
                        last = dve.bn_stats(st[:, t, 2 * half:2 * half + 2, :].rearrange("p a c -> p (a c)"),
                                            xn[:, t, half * HALF:(half + 1) * HALF])
                last.then_inc(bn0_done, 1)
                dve.wait_ge(bn0_done, 1)
                statistics(b, norm_chain(b))
                for t in range(TT):
                    normalize_x(b, t)
                for n in range(LN_CHUNKS):
                    norm_hi(b, n)

            def step(att, proj, wnext, prefetch, stats=None, norm=None):
                plan = PLAIN if norm is None else AFTER_NORM
                ends = {slot_of(plan, unit): unit for unit in range(ZUNITS)}
                if norm is not None:
                    columns(norm)
                for j in range(len(plan)):
                    chunks = [2 * (j - LN_FIRST), 2 * (j - LN_FIRST) + 1] if (
                        norm is not None and 0 <= j - LN_FIRST < LN_CHUNKS // 2) else []
                    if att is not None:
                        if 1 <= j < UNITS + 1:
                            invert(att, j - 1)
                        if j < UNITS:
                            row_max(att, j)
                        if chunks:
                            norm_hi(norm, chunks[0])
                        if 1 <= j < UNITS + 1:
                            normalize(att, j - 1)
                        if 2 <= j < UNITS + 2:
                            pt_lo(att, j - 2)
                        if 4 <= j < SLOTS and j % 2 == 0:
                            context_sum(att, (j - 4) // 2)
                        if chunks:
                            norm_hi(norm, chunks[1])
                        if norm is not None and 3 <= j < 3 + TT // 2:
                            normalize_x(norm, 2 * (j - 3))
                            normalize_x(norm, 2 * (j - 3) + 1)
                    if proj is not None:
                        unit = ends.get(j - 1)
                        if unit is not None and unit < 4:
                            qk_lo(proj, unit)
                        elif unit is not None:
                            v_lo(proj, unit - 4)
                    if stats is not None:
                        if 1 <= j < STAT_CHUNKS + 1:
                            piece_statistics(stats, j - 1)
                        if j == STAT_CHUNKS + 1:
                            dve.wait_ge(xc_used, stats * STAT_CHUNKS)
                            statistics(stats, norm_chain(stats))

            dve.memset(ctxs[:, :], 0.0).then_inc(ctx_out, 16)
            run(dve, layer_norm, step)


def feed_forward_phase(nc, x, ctxT, gate_rows, mod_cols, identf, Wo, w, lb, bo, bw, gate_b, out, nb=B):
    tiles = nb * TT
    with ExitStack() as ctx:
        def sb(name, shape, dt=F32):
            return ctx.enter_context(nc.sbuf_tensor(name, shape, dt))

        def sem(name):
            return ctx.enter_context(nc.semaphore(name))

        def split_pair(name, shape):
            hi = sb(name + "_hi", shape, F32R)
            at = nc.sbuf_base
            sb(name + "_bytes", shape)
            lo = nc.alloc_sbuf_tensor_at(name + "_lo", shape, F32R, offset=at)
            return hi, lo, nc.alloc_sbuf_tensor_at(name + "_in", shape, F32, offset=at)

        Wo_hi, Wo_lo, _ = Wo
        Ww_hi, Ww_lo, Ww_in = split_pair("Ww", [P, KT, E + NAG])
        LB_hi, LB_lo, LB_in = split_pair("LB", [P, E])
        ctx_in = sb("ctx_in", [P, 2, KT, P])
        c_hi, c_lo = sb("c_hi", [P, KT, P], F32R), sb("c_lo", [P, KT, P], F32R)
        xt = sb("xt", [P, 2, E])
        xn2 = sb("xn2", [P, E])
        h2n = sb("h2n", [P, KT, P])
        h2_hi, h2_lo = sb("h2_hi", [P, KT, P], F32R), sb("h2_lo", [P, KT, P], F32R)
        ga, gb = sb("ga", [P, E]), sb("gb", [P, E])
        bo_b, bw_b, gate_bb = sb("bo_b", [P, E]), sb("bw_b", [P, E]), sb("gate_bb", [P, NE])
        yb = sb("yb", [P, E])
        xa = sb("xa", [P, P])
        xaT_hi, xaT_lo = sb("xaT_hi", [P, P], F32R), sb("xaT_lo", [P, P], F32R)
        iota_i, iota = sb("iota_i", [P, NE], I32), sb("iota", [P, NE])
        logits, top, topi, topf = sb("logits", [P, NE]), sb("top", [P, 8]), sb("topi", [P, 8], U32), sb("topf", [P, 8])
        first, gates = sb("first", [P, NE]), sb("gates", [P, NE])
        gap, e2, g1, g2 = [sb(n, [P, 1]) for n in ("gap", "e2", "g1", "g2")]
        st, dm = sb("st2", [P, 1, 4, 3]), sb("dm2", [P, 1, 4])
        mean, rstd, var, hvar, rtmp = [sb(n + "2", [P, 1]) for n in ("mean", "rstd", "var", "hvar", "rtmp")]
        modb = sb("modb2", [P, 2, KT])

        def psum(name, shape):
            return ctx.enter_context(nc.psum_tensor(name, shape, F32))

        psO, psF = psum("psO", [P, E]), psum("psF", [P, 3 * HALF])
        psH = psum("psH", [P, 2, 4, P])
        psX = psum("psX", [P, HALF])
        FC = [(0, 388), (388, 776), (776, E + NAG)]
        psA = psF[:, 2 * HALF + E - FC[2][0]:2 * HALF + FC[2][1] - FC[2][0]]

        ww_in = [sem(f"ww_in{i}") for i in range(4)]
        lb_in, rows_in = sem("lb_in"), sem("rows_in")
        ww_hi, ww_ready = sem("ww_hi"), sem("ww_ready")
        iota_done, iota_ready = sem("iota_done"), sem("iota_ready")
        c_in, x_in = [sem("c_in0"), sem("c_in1")], [sem("xt_in0"), sem("xt_in1")]
        out_done = [sem("out_done0"), sem("out_done1")]
        ga_in, gb_in = sem("ga_in"), sem("gb_in")
        chi_done, clo_done, o_done, po_free, x1_done = (
            sem("chi_done"), sem("clo_done"), sem("o_done"), sem("po_free"), sem("x1_done"))
        x1_chain, xn_done, xt_done, aff_done, h2hi_done, h2lo_done, modb_done = (
            sem("x1_chain"), sem("xn2_done"), sem("xt_done"), sem("aff_done"), sem("h2hi_done"),
            sem("h2lo_done"), sem("modb2_done"))
        bn_done, px_free = sem("bn_done"), sem("px_free")
        ag_done, xa_copied, gap_done, e2_done, gate_chain, xa_done = (
            sem("ag_done"), sem("xa_copied"), sem("gap_done"), sem("e2_done"), sem("gate_chain"), sem("xa_done"))
        xat_done, xathi_done, xatlo_done, f_done, pf_free, yb_done, y_done = (
            sem("xat_done"), sem("xathi_done"), sem("xatlo_done"), sem("f_done"), sem("pf_free"),
            sem("yb_done"), sem("y_done"))
        block = ctx.enter_context(nc.Block())

        def val(t, per, n):
            m, k = t
            return m * (2 * per) + (k * per + n)

        def uses(t, per=16):
            m, k = t
            return m * per + (k // 2 + 1) * per

        def add(t, n):
            return (t[0], t[1] + n)

        def number(t):
            return t[0] * 2 + t[1]

        def run(eng, head, body, tail):
            head()

            def batch(b, last):
                with eng.Fori(0, 3) as c:
                    m = eng.snap(4 * b + c)
                    body((m, 0), b, b)
                    body((m, 1), b, b)
                m = 4 * b + 3
                body((m, 0), b, b)
                if last:
                    tail((m, 1), b)
                else:
                    body((m, 1), b, b + 1)

            if nb > 1:
                with eng.Fori(0, nb - 1) as b:
                    batch(b, False)
            batch(nb - 1, True)

        def weight_lo(eng, k):
            eng.wait_ge(ww_hi, k + 1)
            eng.tensor_tensor(out=Ww_lo[:, k, :], in0=Ww_in[:, k, :], in1=Ww_hi[:, k, :].bitcast(F32),
                              op=ALU.subtract).then_inc(ww_ready, 1)

        def new_batch(t, b, b2):
            return b2 is not b

        @block.sync
        def _(sp):
            xf = x.rearrange("b (t p) e -> (b t) p e", p=P)
            of = out.rearrange("b (t p) e -> (b t) p e", p=P)

            def load_ctx(t, b, tile):
                c = ctxT.rearrange("(b k) p t -> b p k t", k=KT)
                c = c[b] if isinstance(b, int) else c[bass.ds(b, 1)].rearrange("o p k t -> (o p) k t")
                src = c[:, :, tile * P:(tile + 1) * P] if isinstance(tile, int) else c[:, :, bass.ds(tile * P, P)]
                sp.dma_start(ctx_in[:, t[1] % 2, :, :], src).then_inc(c_in[t[1] % 2], 16)

            def load_x(t):
                n = number(t)
                src = xf[n] if isinstance(n, int) else xf[bass.ds(n, 1)].rearrange("o p e -> (o p) e")
                sp.dma_start(xt[:, t[1] % 2, :], src).then_inc(x_in[t[1] % 2], 16)

            def load_gate(b, which, dst, s):
                src = gate_rows[b:b + 1, which, :] if isinstance(b, int) else gate_rows[bass.ds(b, 1), which, :]
                sp.dma_start(dst[:, :], src.broadcast_to([P, E])).then_inc(s, 16)

            load_ctx((0, 0), 0, 0)
            for i in range(2):
                sp.dma_start(Ww_in[:, 2 * i:2 * i + 2, :], w[:, 2 * i:2 * i + 2, :]).then_inc(ww_in[i], 16)
            for dst, src in ((bo_b, bo), (bw_b, bw)):
                sp.dma_start(dst[:, :], src.broadcast_to([P, E])).then_inc(rows_in, 16)
            sp.dma_start(gate_bb[:, :], gate_b.broadcast_to([P, NE])).then_inc(rows_in, 16)
            load_x((0, 0))
            load_gate(0, 0, ga, ga_in)
            load_gate(0, 1, gb, gb_in)
            for i in range(2, 4):
                sp.dma_start(Ww_in[:, 2 * i:2 * i + 2, :], w[:, 2 * i:2 * i + 2, :]).then_inc(ww_in[i], 16)
            sp.dma_start(LB_in[:, :], lb).then_inc(lb_in, 16)
            load_ctx((0, 1), 0, 1)
            load_x((0, 1))

            def store(t):
                sp.wait_ge(y_done, val(t, 1, 2))
                n = number(t)
                dst = of[n] if isinstance(n, int) else of[bass.ds(n, 1)].rearrange("o p e -> (o p) e")
                sp.dma_start(dst, xt[:, t[1] % 2, :]).then_inc(out_done[t[1] % 2], 16)

            def body(t, b, b2, ahead=None):
                b3, tile = ahead
                if b3 is not None:
                    sp.wait_ge(clo_done, val(t, 1, 1))
                    load_ctx(add(t, 2), b3, tile)
                if ahead_gate(t, b, b2, ahead):
                    sp.wait_ge(x1_done, val(t, 1, 1))
                    load_gate(b + 1, 0, ga, ga_in)
                store(t)
                if new_batch(t, b, b2):
                    sp.wait_ge(yb_done, val(t, 1, 1))
                    load_gate(b2, 1, gb, gb_in)
                if b3 is not None:
                    sp.wait_ge(out_done[t[1] % 2], uses(t))
                    load_x(add(t, 2))

            def ahead_gate(t, b, b2, ahead):
                return new_batch(t, b, b2)

            def batch(b, last):
                with sp.Fori(0, 3) as c:
                    m = sp.snap(4 * b + c)
                    body((m, 0), b, b, (b, 2 * c + 2))
                    body((m, 1), b, b, (b, 2 * c + 3))
                m = 4 * b + 3
                body((m, 0), b, b, (None, 0) if last else (b + 1, 0))
                if last:
                    store((m, 1))
                else:
                    body((m, 1), b, b + 1, (b + 1, 1))

            if nb > 1:
                with sp.Fori(0, nb - 1) as b:
                    batch(b, False)
            batch(nb - 1, True)
            for par in range(2):
                sp.wait_ge(out_done[par], 16 * (tiles // 2))

        @block.gpsimd
        def _(pool):
            pool.iota(iota_i[:, :], pattern=[[1, NE]], base=0, channel_multiplier=0).then_inc(iota_done, 1)

            def context_lo(t):
                pool.wait_ge(chi_done, val(t, 1, 1))
                pool.tensor_tensor(out=c_lo[:, :, :], in0=ctx_in[:, t[1] % 2, :, :],
                                   in1=c_hi[:, :, :].bitcast(F32), op=ALU.subtract).then_inc(clo_done, 1)

            def residual(t):
                pool.wait_ge(yb_done, val(t, 1, 1))
                pool.tensor_tensor(out=xt[:, t[1] % 2, :], in0=xt[:, t[1] % 2, :], in1=yb[:, :], op=ALU.add
                                   ).then_inc(y_done, 1)

            def head():
                context_lo((0, 0))
                for k in range(1, KT, 2):
                    weight_lo(pool, k)
                context_lo((0, 1))

            def body(t, b, b2):
                if not (isinstance(t[0], int) and number(t) + 2 >= tiles):
                    context_lo(add(t, 2))
                residual(t)

            pool.memset(yb[:, :], 0.0).then_inc(y_done, 1)
            run(pool, head, body, lambda t, b: residual(t))

        @block.tensor
        def _(pe):
            def output_projection(t, ks, first, last_k):
                if first:
                    pe.wait_ge(clo_done, val(t, 1, 1))
                    if not (isinstance(t[0], int) and number(t) == 0):
                        pe.wait_ge(po_free, val(t, 1, 0))
                for k in ks:
                    for a, wv in ((c_hi, Wo_hi), (c_hi, Wo_lo), (c_lo, Wo_hi)):
                        for half in range(2):
                            c = slice(half * HALF, (half + 1) * HALF)
                            last = pe.matmul(psO[:, c], a[:, k, :], wv[:, k, c],
                                             start=k == 0 and a is c_hi and wv is Wo_hi,
                                             stop=k == KT - 1 and a is c_lo)
                if last_k:
                    last.then_inc(o_done, 1)

            def norm_transposes(t):
                pe.wait_ge(xn_done, val(t, 1, 1))
                for k in range(KT):
                    last = pe.transpose(psH[:, k // 4, k % 4, :], xn2[:, k * P:(k + 1) * P], identf[:, :])
                    if k % 4 == 3:
                        last.then_inc(xt_done, 1)

            def feed_forward(t):
                pe.wait_ge(ww_ready, KT + 1)
                pe.wait_ge(h2lo_done, val(t, 1, 1))

                def base(g, k):
                    c0, c1 = FC[g]
                    o = psF[:, g * HALF:g * HALF + c1 - c0]
                    pe.matmul(o, h2_hi[:, k, :], Ww_hi[:, k, c0:c1], start=k == 0, stop=False)
                    pe.matmul(o, h2_hi[:, k, :], Ww_lo[:, k, c0:c1], start=False, stop=False)
                    return pe.matmul(o, h2_lo[:, k, :], Ww_hi[:, k, c0:c1], start=False,
                                     stop=g == 2 and k == KT - 1)

                for k in range(KT):
                    last = base(2, k)
                last.then_inc(ag_done, 1)
                for k in range(KT):
                    base(0, k)
                for k in range(KT):
                    if k == 5:
                        pe.wait_ge(xa_done, val(t, 1, 1))
                        pe.transpose(psX[:, 0:P], xa[:, :], identf[:, :]).then_inc(xat_done, 1)
                    base(1, k)
                pe.wait_ge(xatlo_done, val(t, 1, 1))
                for g in range(3):
                    c0, c1 = FC[g][0], min(FC[g][1], E)
                    o = psX[:, 0:c1 - c0] if g == 2 else psF[:, g * HALF:g * HALF + c1 - c0]
                    pe.matmul(o, xaT_hi[:, :], LB_hi[:, c0:c1], start=g == 2, stop=False)
                    pe.matmul(o, xaT_hi[:, :], LB_lo[:, c0:c1], start=False, stop=False)
                    last = pe.matmul(o, xaT_lo[:, :], LB_hi[:, c0:c1], start=False, stop=True)
                last.then_inc(f_done, 1)

            def head():
                output_projection((0, 0), range(KT), True, True)

            def body(t, b, b2):
                output_projection(add(t, 1), range(2), True, False)
                norm_transposes(t)
                output_projection(add(t, 1), range(2, KT), False, True)
                feed_forward(t)

            def tail(t, b):
                norm_transposes(t)
                feed_forward(t)

            run(pe, head, body, tail)

        @block.scalar
        def _(act):
            def context_hi(t):
                act.wait_ge(c_in[t[1] % 2], uses(t))
                act.wait_ge(o_done, val(t, 1, 0))
                act.activation(c_hi[:, :, :], ctx_in[:, t[1] % 2, :, :], ACT.Copy).then_inc(chi_done, 1)

            def norm_hi(t):
                act.wait_ge(modb_done, val(t, 1, 1))
                for k in range(KT):
                    if k % 4 == 0:
                        act.wait_ge(xt_done, val(t, 2, k // 4 + 1))
                    last = act.activation(h2n[:, k, :], psH[:, k // 4, k % 4, :], ACT.Identity,
                                          bias=modb[:, 0, k:k + 1], scale=modb[:, 1, k:k + 1])
                    if k % 4 == 3:
                        last.then_inc(aff_done, 1)
                act.wait_ge(aff_done, val(t, 2, 2))
                act.activation(h2_hi[:, :, :], h2n[:, :, :], ACT.Copy).then_inc(h2hi_done, 1)

            def gate_exp(t):
                act.wait_ge(gap_done, val(t, 1, 1))
                act.activation(e2[:, :], gap[:, :], ACT.Exp).then_inc(e2_done, 1)

            def xa_hi(t):
                act.wait_ge(xat_done, val(t, 1, 1))
                act.activation(xaT_hi[:, :], psX[:, 0:P], ACT.Copy).then_inc(xathi_done, 1)

            def head():
                context_hi((0, 0))
                for k in range(KT):
                    act.wait_ge(ww_in[k // 2], 16)
                    act.activation(Ww_hi[:, k, :], Ww_in[:, k, :], ACT.Copy).then_inc(ww_hi, 1)
                act.wait_ge(lb_in, 16)
                act.activation(LB_hi[:, :], LB_in[:, :], ACT.Copy).then_inc(ww_hi, 1)
                context_hi((0, 1))

            def body(t, b, b2):
                norm_hi(t)
                if not (isinstance(t[0], int) and number(t) + 2 >= tiles):
                    context_hi(add(t, 2))
                gate_exp(t)
                xa_hi(t)

            def tail(t, b):
                norm_hi(t)
                gate_exp(t)
                xa_hi(t)

            run(act, head, body, tail)

        @block.vector
        def _(dve):
            X_STEPS = 1 + stat_steps(1)
            G_STEPS = 10

            def norm_chain(t, before=0):
                count = [before]

                def chain(ins):
                    count[0] += 1
                    ins.then_inc(x1_chain, 1)
                    dve.wait_ge(x1_chain, val(t, X_STEPS, count[0]))
                return chain

            def residual(t, b, starts):
                chain = norm_chain(t)
                bs = slice(b, b + 1) if isinstance(b, int) else bass.ds(b, 1)
                dve.tensor_copy(modb[:, :, :], mod_cols[:, 2:4, :, bs].rearrange("p v k o -> p v (k o)")
                                ).then_inc(modb_done, 1)
                dve.wait_ge(o_done, val(t, 1, 1))
                if starts:
                    dve.wait_ge(ga_in, b * 16 + 16)
                dve.tensor_tensor(xn2[:, :], psO[:, :], bo_b[:, :], ALU.add).then_inc(po_free, 1)
                dve.wait_ge(po_free, val(t, 1, 1))
                chain(dve.tensor_tensor(xn2[:, :], xn2[:, :], ga[:, :], ALU.mult))
                dve.wait_ge(x_in[t[1] % 2], uses(t))
                x1 = xt[:, t[1] % 2, :]
                dve.tensor_tensor(x1, x1, xn2[:, :], ALU.add).then_inc(x1_done, 1)
                dve.wait_ge(x1_done, val(t, 1, 1))
                for half in range(2):
                    last = dve.bn_stats(st[:, 0, 2 * half:2 * half + 2, :].rearrange("p a c -> p (a c)"),
                                        x1[:, half * HALF:(half + 1) * HALF])
                last.then_inc(bn_done, 1)

            def statistics(t):
                chain = norm_chain(t, 1)
                dve.wait_ge(bn_done, val(t, 1, 1))
                norm_statistics(dve, chain, 1, st[:, :, :, :], dm[:, :, :], mean[:, :], rstd[:, :],
                                var[:, :], hvar[:, :], rtmp[:, :])

            def normalize(t):
                dve.tensor_scalar(xn2[:, :], xt[:, t[1] % 2, :], mean[:, 0:1], rstd[:, 0:1],
                                  ALU.subtract, ALU.mult).then_inc(xn_done, 1)

            def gating(t):
                count = [0]

                def chain(ins):
                    count[0] += 1
                    ins.then_inc(gate_chain, 1)
                    dve.wait_ge(gate_chain, val(t, G_STEPS, count[0]))

                dve.wait_ge(ag_done, val(t, 1, 1))
                chain(dve.tensor_tensor(logits[:, :], psA[:, P:NAG], gate_bb[:, :], ALU.add))
                dve.tensor_copy(xa[:, :], psA[:, 0:P]).then_inc(xa_copied, 1)
                chain(dve.max(out=top[:, :], in_=logits[:, :]))
                dve.tensor_tensor(gap[:, :], top[:, 1:2], top[:, 0:1], ALU.subtract).then_inc(gap_done, 1)
                chain(dve.max_index(out=topi[:, :], in_max=top[:, :], in_values=logits[:, :]))
                chain(dve.tensor_copy(topf[:, :], topi[:, :]))
                dve.wait_ge(e2_done, val(t, 1, 1))
                chain(dve.tensor_scalar(g2[:, :], e2[:, :], 1.0, None, ALU.add))
                chain(dve.reciprocal(g1[:, :], g2[:, :]))
                chain(dve.tensor_tensor(g2[:, :], e2[:, :], g1[:, :], ALU.mult))
                chain(dve.tensor_scalar(first[:, :], iota[:, :], topf[:, 0:1], g1[:, :], ALU.is_equal, ALU.mult))
                chain(dve.tensor_scalar(gates[:, :], iota[:, :], topf[:, 1:2], g2[:, :], ALU.is_equal, ALU.mult))
                chain(dve.tensor_tensor(gates[:, :], gates[:, :], first[:, :], ALU.add))
                assert count[0] == G_STEPS
                dve.wait_ge(xa_copied, val(t, 1, 1))
                dve.tensor_tensor(xa[:, :].rearrange("p (e r) -> p e r", r=R),
                                  xa[:, :].rearrange("p (e r) -> p e r", r=R),
                                  gates[:, :].rearrange("p (e o) -> p e o", o=1).broadcast_to([P, NE, R]),
                                  ALU.mult).then_inc(xa_done, 1)

            def xa_lo(t):
                dve.wait_ge(xathi_done, val(t, 1, 1))
                dve.tensor_tensor(xaT_lo[:, :], psX[:, 0:P], xaT_hi[:, :].bitcast(F32), ALU.subtract
                                  ).then_inc(xatlo_done, 1)

            def output(t, b, starts):
                dve.wait_ge(f_done, val(t, 1, 1))
                dve.wait_ge(y_done, val(t, 1, 1))
                w2, c2 = FC[0][1], FC[2][0]
                dve.tensor_tensor(yb[:, 0:c2].rearrange("p (g c) -> p g c", c=w2),
                                  psF[:, 0:2 * HALF].rearrange("p (g c) -> p g c", c=HALF)[:, :, 0:w2],
                                  bw_b[:, 0:c2].rearrange("p (g c) -> p g c", c=w2), ALU.add)
                dve.tensor_tensor(yb[:, c2:E], psX[:, 0:E - c2], bw_b[:, c2:E], ALU.add).then_inc(px_free, 1)
                dve.wait_ge(px_free, val(t, 1, 1))
                dve.tensor_tensor(yb[:, c2:E], yb[:, c2:E], psF[:, 2 * HALF:2 * HALF + E - c2], ALU.add
                                  ).then_inc(pf_free, 1)
                if starts:
                    dve.wait_ge(gb_in, b * 16 + 16)
                dve.wait_ge(pf_free, val(t, 1, 1))
                dve.tensor_tensor(yb[:, :], yb[:, :], gb[:, :], ALU.mult).then_inc(yb_done, 1)

            def norm_lo(t):
                dve.wait_ge(h2hi_done, val(t, 1, 1))
                dve.tensor_tensor(h2_lo[:, :, :], h2n[:, :, :], h2_hi[:, :, :].bitcast(F32), ALU.subtract
                                  ).then_inc(h2lo_done, 1)

            def head():
                for k in range(0, KT, 2):
                    weight_lo(dve, k)
                dve.wait_ge(ww_hi, KT + 1)
                dve.tensor_tensor(LB_lo[:, :], LB_in[:, :], LB_hi[:, :].bitcast(F32), ALU.subtract
                                  ).then_inc(ww_ready, 1)
                dve.wait_ge(iota_done, 1)
                dve.tensor_copy(iota[:, :], iota_i[:, :]).then_inc(iota_ready, 1)
                dve.wait_ge(iota_ready, 1)
                dve.wait_ge(rows_in, 48)
                residual((0, 0), 0, True)
                statistics((0, 0))
                normalize((0, 0))

            def body(t, b, b2):
                norm_lo(t)
                residual(add(t, 1), b2, new_batch(t, b, b2))
                gating(t)
                statistics(add(t, 1))
                normalize(add(t, 1))
                xa_lo(t)
                output(t, b, True)

            def tail(t, b):
                norm_lo(t)
                gating(t)
                xa_lo(t)
                output(t, b, True)

            run(dve, head, body, tail)


def program(nc, x, cT, wmod, wqkv, wo, w, lb, bo, bw, gate_b, out, nb=B):
    gate_rows = nc.dram_tensor("gate_rows", [B, 2, E], F32, kind="Internal").ap()
    ctxT = nc.dram_tensor("ctxT", [nb * PAIRS, P, S], F32, kind="Internal").ap()
    with ExitStack() as ctx:
        identf = ctx.enter_context(nc.sbuf_tensor("identf", [P, P], F32))
        mod_cols = ctx.enter_context(nc.sbuf_tensor("mod_cols", [P, 4, KT, B], F32))
        modulation_phase(nc, cT, wmod, mod_cols, identf, gate_rows)
        wo_at = nc.sbuf_base
        ctx.enter_context(nc.sbuf_tensor("Wo_bytes", [P, 2, KT, E], F32))
        Wo = [nc.alloc_sbuf_tensor_at(n, [P, KT, E], t, offset=wo_at + i * 4 * KT * E)
              for n, i, t in (("Wo_hi", 0, F32R), ("Wo_lo", 1, F32R), ("Wo_in", 1, F32))]
        attention_phase(nc, x, wqkv, mod_cols, identf, ctxT, wo, Wo, wo_at, nb)
        feed_forward_phase(nc, x, ctxT, gate_rows, mod_cols, identf, Wo, w, lb, bo, bw, gate_b, out, nb)


def kernel(L0_attn_x, L0_attn_Wq, L0_attn_Wk, L0_attn_Wv, L0_attn_Wo, L0_attn_bo, L0_ffn_W, L0_ffn_b,
           L0_ffn_lora_A, L0_ffn_lora_B, L0_ffn_gate_w, L0_ffn_gate_b, L0_c, L0_wmod):
    import numpy as np
    import concourse.bacc as bacc
    from concourse.bass_utils import run_bass_kernel_spmd

    def features_by_partition(a):
        return np.ascontiguousarray(a.T.reshape(KT, P, a.shape[0]).transpose(1, 0, 2))

    def by_pair(a):
        return a.T.reshape(KT, P, PAIRS, P).transpose(2, 1, 0, 3)

    c, W, A, gw = (np.asarray(a) for a in (L0_c, L0_ffn_W, L0_ffn_lora_A, L0_ffn_gate_w))
    arrays = {
        "x": np.ascontiguousarray(L0_attn_x),
        "cT": features_by_partition(c),
        "wmod": np.ascontiguousarray(L0_wmod),
        "wqkv": np.ascontiguousarray(np.stack([by_pair(np.asarray(a)) for a in (L0_attn_Wq, L0_attn_Wk, L0_attn_Wv)], 1)),
        "wo": features_by_partition(np.asarray(L0_attn_Wo)),
        "w": features_by_partition(np.concatenate([W, A.reshape(NE * R, E), gw], 0)),
        "lb": np.ascontiguousarray(np.asarray(L0_ffn_lora_B).transpose(0, 2, 1).reshape(NE * R, E)),
        "bo": np.asarray(L0_attn_bo).reshape(1, E),
        "bw": np.asarray(L0_ffn_b).reshape(1, E),
        "gate_b": np.asarray(L0_ffn_gate_b).reshape(1, NE),
    }
    nc = bacc.Bacc("TRN2", target_bir_lowering=False, num_devices=1)
    args = [nc.dram_tensor(f"in_{n}", a.shape, F32, kind="ExternalInput").ap() for n, a in arrays.items()]
    out = nc.dram_tensor("out", (B, S, E), F32, kind="ExternalOutput").ap()
    program(nc, *args, out)
    r = run_bass_kernel_spmd(nc, [{f"in_{n}": a for n, a in arrays.items()}], core_ids=[0])
    return r.results[0]["out"]
```

```python
from contextlib import ExitStack

import concourse.bass as bass
from concourse import mybir

F32 = mybir.dt.float32
F32R = mybir.dt.float32r
BF16 = mybir.dt.bfloat16
I32 = mybir.dt.int32
U32 = mybir.dt.uint32
ALU = mybir.AluOpType
ACT = mybir.ActivationFunctionType
AX = mybir.AxisListType

P = 128
B, S, E = 4, 1024, 1024
H = 16
D = E // H
KT = E // P
TT = S // P
PAIRS = H // 2
NE, R = 8, 16
NAG = NE * R + NE
HALF = 512
EPS = 1e-5
QSCALE = D ** -0.5
MASKED = -3.0e38
RSQRT_MAGIC = 0x5F3759DF
NEWTON = 4

EARLY, LATE = (0, 1, 3, 4), (2, 5)

UNITS = 2 * TT


def unit_chunks(u):
    t = u % TT
    return [(k0, min(4, t + 1 - k0)) for k0 in range(0, t + 1, 4)]


CHUNK0 = [sum(len(unit_chunks(v)) for v in range(u)) for u in range(UNITS + 1)]
CHUNKS = CHUNK0[UNITS]
GROUPS = UNITS // 2
ZUNITS = 6
ZMM = KT * 3
SLOTS = UNITS + 3
LN_CHUNKS = 2 * KT
STAT_CHUNKS = 2 * TT

LATE_W = 2 * P
LATE_N = len(LATE) * E // LATE_W
LATE_RING = 4
LATE_SPLIT = {slot: n for n, slot in enumerate((5, 6, 7, 8, 9, 10, 12, 13))}
LATE_MM = {slot + 2: n for slot, n in LATE_SPLIT.items()}
WO_PLAN = {slot: k for k, slot in enumerate((8, 11, 13, 14, 15, 16, 17, 18))}

NORM_FIRST, LN_FIRST = 3, 7
PLAIN = [(0, (7, 8, 9)), (3, (8, 8, 8)), (6, (8, 9, 7)), (9, (7, 7, 10)), (12, (7, 8, 9)), (15, (9, 8, 7))]
ALONE = [(SLOTS + i, (24,)) for i in range(ZUNITS)]
AFTER_NORM = [(15, (12, 12)), (17, (12, 12))] + [(SLOTS + i, (24,)) for i in range(4)]


def parts_of(plan, slot):
    return [(unit, sum(counts[:slot - first]), sum(counts[:slot - first + 1]))
            for unit, (first, counts) in enumerate(plan) if 0 <= slot - first < len(counts)]


def second_bank(plan, unit):
    return plan[unit][0] >= SLOTS and unit % 2 == 0


def slots_of(plan):
    return max(SLOTS, plan[-1][0] + len(plan[-1][1]))


def slot_of(plan, unit):
    return plan[unit][0] + len(plan[unit][1]) - 1


assert all(sum(counts) == ZMM for plan in (PLAIN, ALONE, AFTER_NORM) for _, counts in plan)


STAT_PARTS = 2 + NEWTON // 2


def stat_steps(tiles, parts=STAT_PARTS):
    return (0, 5, 8)[min(parts, 2)] + (4 if tiles == 1 else 6) * max(0, parts - 2)


def norm_statistics(eng, step, parts, tiles, st, dm, mean, rstd, v, half_v, t):
    for part in parts:
        if part == 0:
            sums = mean
            spread = sums.rearrange("p (t o) -> p t o", o=1).broadcast_to([P, tiles, 4])
            step(eng.tensor_reduce(sums, st[:, :, :, 1], AX.X, ALU.add))
            step(eng.scalar_tensor_tensor(out=dm, in0=spread, scalar=0.25, in1=st[:, :, :, 1],
                                          op0=ALU.mult, op1=ALU.subtract))
            eng.tensor_scalar(mean, sums, 0.25, None, ALU.mult)
            step(eng.tensor_tensor(dm, dm, dm, ALU.mult))
            step(eng.scalar_tensor_tensor(out=dm, in0=dm, scalar=E / 4.0, in1=st[:, :, :, 2],
                                          op0=ALU.mult, op1=ALU.add))
            step(eng.tensor_reduce(t, dm, AX.X, ALU.add))
        elif part == 1:
            eng.tensor_scalar(half_v, t, 0.5 / E, 0.5 * EPS, ALU.mult, ALU.add)
            step(eng.tensor_scalar(v, t, 1.0 / E, EPS, ALU.mult, ALU.add))
            step(eng.tensor_scalar(t.bitcast(I32), v.bitcast(I32), 1, None, ALU.logical_shift_right))
            step(eng.tensor_scalar(rstd.bitcast(I32), t.bitcast(I32), -1.0, float(RSQRT_MAGIC), ALU.mult, ALU.add))
        else:
            for _ in range(2):
                if tiles == 1:
                    step(eng.scalar_tensor_tensor(out=t, in0=rstd, scalar=half_v, in1=rstd,
                                                  op0=ALU.mult, op1=ALU.mult))
                else:
                    step(eng.tensor_tensor(t, rstd, rstd, ALU.mult))
                    step(eng.tensor_tensor(t, t, half_v, ALU.mult))
                step(eng.scalar_tensor_tensor(out=rstd, in0=t, scalar=1.5, in1=rstd, op0=ALU.subtract, op1=ALU.mult))


def modulate(pe, out, c_split, w_hi, w_lo):
    for k in range(KT):
        pe.matmul(out, c_split[:, k, :], w_hi[:, k, :], start=k == 0, stop=False)
        last = pe.matmul(out, c_split[:, k, :], w_lo[:, k, :], start=False, stop=k == KT - 1)
    return last


def sum_transposed(pe, out, rows, select):
    for tile in range(rows.shape[1] // P):
        last = pe.matmul(out[:, tile, :], rows[:, tile * P:(tile + 1) * P], select, start=True, stop=True)
    return last


def modulation_weights(wmod, vector, part, width):
    c0 = vector * E + part * width
    return wmod[:, c0:c0 + width].rearrange("(k p) n -> p k n", p=P)


def modulation_phase(nc, x, cT, wmod, c_split, select, mod_cols, identf, xn, ring_at):
    CH = 2 * len(EARLY)
    RING = 4
    with ExitStack() as ctx:
        def sb(name, shape, dt=F32):
            return ctx.enter_context(nc.sbuf_tensor(name, shape, dt))

        def sem(name):
            return ctx.enter_context(nc.semaphore(name))

        c_in = sb("c_in", [P, KT, B])
        c_exp = sb("c_exp", [P, KT, B])
        c_silu = sb("c_silu", [P, KT, B])
        w_hi = sb("wring_hi", [P, RING, KT, HALF], F32R)
        w_in, w_lo = [[nc.alloc_sbuf_tensor_at(f"{n}{i}", [P, KT, HALF], t, offset=at) for i, at in enumerate(ring_at)]
                      for n, t in (("wring_in", F32), ("wring_lo", F32R))]
        RING_IN = len(ring_at)
        rows = sb("mod_rows", [2 * B, 2, HALF])
        st, dm = sb("st0", [P, TT, 4, 3]), sb("dm0", [P, TT, 4])
        mean, rstd, var, hvar, rtmp = [sb(n + "0", [P, TT]) for n in ("mean", "rstd", "var", "hvar", "rtmp")]
        psR = ctx.enter_context(nc.psum_tensor("psR", [P, 2, HALF], F32))
        psM = ctx.enter_context(nc.psum_tensor("psM", [P, len(EARLY), KT, B], F32))
        c_loaded = sem("c_loaded")
        w_loaded = [sem(f"w_loaded{n}") for n in range(CH)]
        x_loaded = [sem("x_loaded0"), sem("x_loaded1")]
        exp_done, dve_chain, stats_done = sem("m_exp_done"), sem("m_dve_chain"), sem("m_stats_done")
        silu_ready, ident_zeroed, ident_ready = sem("silu_ready"), sem("ident_zeroed"), sem("ident_ready")
        chunk_done, all_written = sem("chunk_done"), sem("all_written")
        w_hi_done, rows_done, select_ready = sem("w_hi_done"), sem("rows_done"), sem("select_ready")
        w_lo_done = [sem("w_lo_pool"), sem("w_lo_dve")]
        lo_of = [[n for n in range(CH) if n % 2 == 0 and n < CH - 2], [n for n in range(CH) if n % 2 or n == CH - 2]]
        cols_done = sem("cols_done")
        block = ctx.enter_context(nc.Block())

        @block.sync
        def _(sp):
            sp.dma_start(c_in[:, :, :], cT).then_inc(c_loaded, 16)
            for half in range(2):
                sp.dma_start(xn[:, 4 * half:4 * half + 4, :],
                             x.rearrange("b (t p) e -> b p t e", p=P)[0][:, 4 * half:4 * half + 4, :]
                             ).then_inc(x_loaded[half], 16)
            for n in range(CH):
                if n >= RING_IN:
                    sp.wait_ge(chunk_done, n - RING_IN + 1)
                sp.dma_start(w_in[n % RING_IN][:, :, :], modulation_weights(wmod, EARLY[n // 2], n % 2, HALF)
                             ).then_inc(w_loaded[n], 16)

        def split_lo(eng, n, signal):
            eng.wait_ge(w_hi_done, n + 1)
            eng.tensor_tensor(out=w_lo[n % RING_IN][:, :, :], in0=w_in[n % RING_IN][:, :, :],
                              in1=w_hi[:, n % RING, :, :].bitcast(F32), op=ALU.subtract).then_inc(signal, 1)

        @block.gpsimd
        def _(pool):
            pool.memset(identf[:, :], 0.0).then_inc(ident_zeroed, 1)
            pool.wait_ge(ident_zeroed, 1)
            pool.affine_select(out=identf[:, :], in_=identf[:, :], compare_op=ALU.not_equal, fill=1.0,
                               base=0, pattern=[[-1, P]], channel_multiplier=1).then_inc(ident_ready, 1)
            pool.wait_ge(ident_ready, 1)
            pool.tensor_tensor(out=select[:, 0:B], in0=identf[0:2 * B, 0:B], in1=identf[0:2 * B, B:2 * B], op=ALU.add
                               ).then_inc(select_ready, 1)
            for n in lo_of[0]:
                split_lo(pool, n, w_lo_done[0])

        @block.scalar
        def _(act):
            act.wait_ge(c_loaded, 16)
            act.activation(c_exp[:, :, :], c_in[:, :, :], ACT.Exp, scale=-1.0).then_inc(exp_done, 1)
            for n in range(CH + 2):
                if n < CH:
                    act.wait_ge(w_loaded[n], 16)
                    if n >= RING:
                        act.wait_ge(chunk_done, n - RING + 1)
                    act.activation(w_hi[:, n % RING, :, :], w_in[n % RING_IN][:, :, :], ACT.Copy).then_inc(w_hi_done, 1)
                if n >= 2:
                    act.wait_ge(chunk_done, n - 1)
                    if n >= 4:
                        act.wait_ge(cols_done, n - 3)
                    act.activation(rows[:, n % 2, :], psR[0:2 * B, n % 2, :], ACT.Copy).then_inc(rows_done, 1)

        @block.tensor
        def _(pe):
            pe.wait_ge(silu_ready, 2)
            pe.wait_ge(select_ready, 1)
            for n in range(CH + 2):
                if n < CH:
                    by = 0 if n in lo_of[0] else 1
                    pe.wait_ge(w_lo_done[by], lo_of[by].index(n) + 1)
                    if n >= 2:
                        pe.wait_ge(rows_done, n - 1)
                    modulate(pe, psR[0:2 * B, n % 2, :], c_split, w_hi[:, n % RING, :, :], w_lo[n % RING_IN]
                             ).then_inc(chunk_done, 1)
                if n >= 2:
                    m = n - 2
                    pe.wait_ge(rows_done, m + 1)
                    sum_transposed(pe, psM[:, m // 2, 4 * (m % 2):4 * (m % 2) + 4, :], rows[:, m % 2, :], select[:, 0:B]
                                   ).then_inc(cols_done, 1)

        @block.vector
        def _(dve):
            chain = [0]

            def step(ins):
                chain[0] += 1
                ins.then_inc(dve_chain, 1)
                dve.wait_ge(dve_chain, chain[0])

            dve.wait_ge(exp_done, 1)
            step(dve.tensor_scalar(c_exp[:, :, :], c_exp[:, :, :], 1.0, None, ALU.add))
            step(dve.reciprocal(c_exp[:, :, :], c_exp[:, :, :]))
            step(dve.tensor_tensor(c_silu[:, :, :], c_in[:, :, :], c_exp[:, :, :], ALU.mult))
            step(dve.tensor_copy(c_split[:, :, 0:B], c_silu[:, :, :]))
            dve.tensor_tensor(c_split[:, :, B:2 * B], c_silu[:, :, :], c_split[:, :, 0:B].bitcast(F32), ALU.subtract
                              ).then_inc(silu_ready, 2)
            for t in range(TT):
                if t % 4 == 0:
                    dve.wait_ge(x_loaded[t // 4], 16)
                for half in range(2):
                    last = dve.bn_stats(st[:, t, 2 * half:2 * half + 2, :].rearrange("p a c -> p (a c)"),
                                        xn[:, t, half * HALF:(half + 1) * HALF])
            last.then_inc(stats_done, 1)
            dve.wait_ge(stats_done, 1)
            norm_statistics(dve, step, range(STAT_PARTS), TT, st[:, :, :, :], dm[:, :, :], mean[:, :], rstd[:, :],
                            var[:, :], hvar[:, :], rtmp[:, :])
            for t in range(TT):
                dve.tensor_scalar(xn[:, t, :], xn[:, t, :], mean[:, t:t + 1], rstd[:, t:t + 1],
                                  ALU.subtract, ALU.mult).then_inc(all_written, 1)
            for n in lo_of[1]:
                split_lo(dve, n, w_lo_done[1])
            dve.wait_ge(cols_done, CH)
            for i, vector in enumerate(EARLY):
                dve.tensor_scalar(mod_cols[:, i, :, :], psM[:, i, :, :], float(i % 2), None, ALU.add
                                  ).then_inc(all_written, 1)
            dve.wait_ge(all_written, TT + len(EARLY))


def attention_phase(nc, x, wqkv, wmod, c_split, select, mod_cols, identf, gate_rows, ctxT, wo, Wo, wo_at, arena_at, xn, nb=B):
    with ExitStack() as ctx:
        def sb(name, shape, dt=F32):
            return ctx.enter_context(nc.sbuf_tensor(name, shape, dt))

        def sem(name):
            return ctx.enter_context(nc.semaphore(name))

        BYTES = 4 * 2 * S
        Qs, Qx, Ks, Vs = [], [], [], []
        for par in range(2):
            o = arena_at + par * 4 * BYTES
            Qs.append(nc.alloc_sbuf_tensor_at(f"Qs{par}", [P, 2, S], F32R, offset=o))
            Qx.append(nc.alloc_sbuf_tensor_at(f"Qx{par}", [P, 2, S], F32R, offset=o + BYTES))
            Ks.append(nc.alloc_sbuf_tensor_at(f"Ks{par}", [P, 2, S], F32R, offset=o + 2 * BYTES))
            Vs.append(nc.alloc_sbuf_tensor_at(f"Vs{par}", [P, 2, TT, 2 * D], F32R, offset=o + 3 * BYTES))

        hT = [nc.alloc_sbuf_tensor_at(n, [P, KT, S], F32R, offset=wo_at + i * 4 * KT * S)
              for i, n in enumerate(("hT_hi", "hT_lo"))]
        Wo_hi, Wo_lo, Wo_in = Wo
        late_at = [arena_at, nc.sbuf_base]
        W = [sb("W_hi", [P, 3, KT, P], F32R), sb("W_lo", [P, 3, KT, P], F32R)]
        W_in = sb("W_in", [P, 2, KT, P])
        l_hi, l_in, l_lo = [[nc.alloc_sbuf_tensor_at(
            f"late_{part}{i}", [P, KT, LATE_W], t, offset=late_at[i // 2] + (2 * (i % 2) + lo) * 4 * KT * LATE_W)
            for i in range(LATE_RING)] for part, lo, t in (("hi", 0, F32R), ("in", 1, F32), ("lo", 1, F32R))]
        PT = [[sb(f"PT_{part}{g}", [P, 6 + 2 * g, 2 * P], F32R) for part in ("hi", "lo")] for g in range(2)]
        Pb = sb("Pb", [P, 2, S])
        Zs = sb("Zs", [P, HALF])
        ctxs = sb("ctxs", [P, S])
        ctx_lo = sb("ctx_lo", [D, 2 * P])
        hn1_at = nc.sbuf_base
        hn = [Zs, sb("hn1", [P, HALF])]
        hn0 = hn + [Pb[:, 0, 0:HALF], Pb[:, 0, HALF:S]]
        g_sign, g_abs = [nc.alloc_sbuf_tensor_at(n, [P, 2, KT, B], F32, offset=hn1_at + i * 8 * KT * B)
                         for i, n in enumerate(("g_sign", "g_abs"))]
        g_rows = nc.alloc_sbuf_tensor_at("g_rows", [2 * KT * B, P], F32, offset=hn1_at + 16 * KT * B)
        g_mod = nc.alloc_sbuf_tensor_at("g_mod", [2 * B, LATE_W], F32, offset=hn1_at + 16 * KT * B + 4 * P)
        ident16, mask16 = sb("ident16", [P, P], BF16), sb("mask16", [P, P], BF16)
        one = sb("one", [P, 1])
        negmax, rowsum, rinv = sb("negmax", [P, UNITS]), sb("rowsum", [P, UNITS]), sb("rinv", [P, UNITS])
        st, dm = sb("st", [P, TT, 4, 3]), sb("dm", [P, TT, 4])
        mean, rstd, var, hvar, rtmp = [sb(n, [P, TT]) for n in ("mean", "rstd", "var", "hvar", "rtmp")]
        modb = sb("modb", [P, 2, KT])

        def psum(name, shape):
            return ctx.enter_context(nc.psum_tensor(name, shape, F32))

        psS = [psum("psS0", [P, S]), psum("psS1", [P, S])]
        psT = [psum("psT0", [P, HALF]), psum("psT1", [P, HALF])]
        psPV = psum("psPV", [P, HALF])
        psZ = psum("psZ", [P, HALF])
        late_gates = psZ[:, LATE_W:LATE_W + 2 * KT * B].rearrange("p (t b) -> p t b", b=B)

        scores_done, max_done, exp_done, norm_done, rinv_done = (
            sem("scores_done"), sem("max_done"), sem("exp_done"), sem("norm_done"), sem("rinv_done"))
        tp_done, pthi_done, ptlo_done = sem("tp_done"), sem("pthi_done"), sem("ptlo_done")
        pv_done, ctxlo_done, ctx_done, ctx_out = sem("pv_done"), sem("ctxlo_done"), sem("ctx_done"), sem("ctx_out")
        z_done, zs_done, qkhi_done, qklo_done, qx_done = (
            sem("z_done"), sem("zs_done"), sem("qkhi_done"), sem("qklo_done"), sem("qx_done"))
        vt_done, vhi_done, vlo_done = sem("vt_done"), sem("vhi_done"), sem("vlo_done")
        w_in, whi_done, w_ready = [sem("w_in0"), sem("w_in1")], sem("whi_done"), sem("w_ready")
        consts_a, consts_ready = sem("consts_a"), sem("consts_ready")
        x_in = [sem("x_in0"), sem("x_in1")]
        ln0_lo = [sem("ln0_lo_even"), sem("ln0_lo_odd")]
        late_in = [sem(f"late_in{i}") for i in range(LATE_RING)]
        late_hi, late_lo, late_done = sem("late_hi"), [sem("late_lo_even"), sem("late_lo_odd")], sem("late_done")
        late_rows, late_cols = sem("late_rows"), sem("late_cols")
        gate_chain, gate_t, gate_copied, gates_out = (
            sem("late_gate_chain"), sem("gate_t"), sem("gate_copied"), sem("gates_out"))
        xc_in, xc_used = sem("xc_in"), sem("xc_used")
        wo_in, wo_hi, wo_lo = [sem(f"wo_in{k}") for k in range(KT // 2)], sem("wo_hi"), sem("wo_lo")
        st_done, xnorm_done, modb_done = sem("st_done"), sem("xnorm_done"), sem("modb_done")
        lnt_done, lnaff_done, lnhi_done, lnlo_done = (
            sem("lnt_done"), sem("lnaff_done"), sem("lnhi_done"), sem("lnlo_done"))

        def wait_norm_lo(eng, b, n):
            if isinstance(b, int) and b == 0:
                eng.wait_ge(ln0_lo[0], (n + 1) // 2)
                if n > 1:
                    eng.wait_ge(ln0_lo[1], n // 2)
            else:
                eng.wait_ge(lnlo_done, b * LN_CHUNKS + (n - LN_CHUNKS))

        def val(hk, per, n):
            h, k = hk
            return h * (2 * per) + (k * per + max(n, 0))

        def nxt(hk):
            return (hk[0], hk[1] + 1)

        def prev(hk):
            return (hk[0], hk[1] - 1)

        def run(eng, layer_norm, step):
            layer_norm(0)
            step(None, (0, 0), 1, True)

            def batch(b, last):
                with eng.Fori(0, 3) as c:
                    h = eng.snap(4 * b + c)
                    step((h, 0), (h, 1), 2 * c + 2, True)
                    step((h, 1), (h, 2), 2 * c + 3, True)
                h = 4 * b + 3
                step((h, 0), (h, 1), 0, not last, stats=None if last else b + 1)
                if last:
                    step((h, 1), None, None, False)
                else:
                    step((h, 1), (4 * b + 4, 0), 1, True, norm=b + 1)

            if nb > 1:
                with eng.Fori(0, nb - 1) as b:
                    batch(b, False)
            batch(nb - 1, True)

        block = ctx.enter_context(nc.Block())

        @block.sync
        def _(sp):
            def load_w(hk, pair, part):
                n = 3 * hk[1] + part
                if not (isinstance(hk[0], int) and val(hk, 3, part) < 2):
                    sp.wait_ge(w_ready, val(hk, 3, part - 1) if part else val(prev(hk), 3, 2))
                sp.dma_start(W_in[:, n % 2, :, :], wqkv[bass.ds(pair, 1), part, :, :, :] if not isinstance(pair, int)
                             else wqkv[pair:pair + 1, part, :, :, :]).then_inc(w_in[n % 2], 16)

            def load_x(b):
                xt = x.rearrange("b (t p) e -> b p t e", p=P)
                sp.wait_ge(ctx_done, b * (PAIRS * GROUPS) - GROUPS)
                for half in range(2):
                    sp.dma_start(xn[:, 4 * half:4 * half + 4, :],
                                 xt[bass.ds(b, 1)].rearrange("o p t e -> (o p) t e")[:, 4 * half:4 * half + 4, :]
                                 ).then_inc(x_in[half], 16)

            def load_wo(k):
                sp.dma_start(Wo_in[:, k:k + 2, :], wo[:, k:k + 2, :]).then_inc(wo_in[k // 2], 16)

            def step(att, proj, wnext, prefetch, stats=None, norm=None):
                if norm is not None:
                    load_x(norm)
                if proj is not None:
                    par = proj[1] % 2
                    if prefetch:
                        load_w(nxt(proj), wnext, 0)
                    sp.wait_ge(qklo_done, val(proj, 8, 4))
                    sp.dma_start(Qx[par][0:D, :, :].bitcast(F32), Qs[par][D:P, :, :].bitcast(F32)).then_inc(qx_done, 16)
                    sp.dma_start(Qx[par][D:P, :, :].bitcast(F32), Qs[par][0:D, :, :].bitcast(F32)).then_inc(qx_done, 16)
                    if prefetch:
                        load_w(nxt(proj), wnext, 1)
                        load_w(nxt(proj), wnext, 2)
                if proj is None:
                    sp.wait_ge(ctx_done, (nb * PAIRS - 1) * GROUPS)
                    sp.wait_ge(z_done, ZUNITS * nb * PAIRS)
                    for n in range(LATE_N):
                        if n >= LATE_RING:
                            sp.wait_ge(late_done, n - LATE_RING + 1)
                            if n % 2 == 0:
                                load_wo(n - LATE_RING)
                        per = E // LATE_W
                        sp.dma_start(l_in[n % LATE_RING][:, :, :], modulation_weights(wmod, LATE[n // per], n % per, LATE_W)
                                     ).then_inc(late_in[n % LATE_RING], 16)
                    for k in range(LATE_N - LATE_RING, KT, 2):
                        load_wo(k)
                if att is not None:
                    sp.wait_ge(ctx_done, val(att, GROUPS, GROUPS))
                    h, k = att
                    n = h * 2 + k
                    sp.dma_start((ctxT[n:n + 1] if isinstance(n, int) else ctxT[bass.ds(n, 1)])
                                 .rearrange("o p t -> (o p) t"), ctxs[:, :]).then_inc(ctx_out, 16)

            for part in range(3):
                load_w((0, 0), 0, part)
            run(sp, lambda b: None, step)
            sp.wait_ge(gate_copied, 1)
            sp.dma_start(gate_rows.rearrange("w t b p -> (w t b) p"), g_rows[:, :]).then_inc(gates_out, 16)
            sp.wait_ge(gates_out, 16)
            sp.wait_ge(ctx_out, 16 * (nb * PAIRS + 1))

        def late_split_lo(eng, n):
            eng.wait_ge(late_hi, n + 1)
            i = n % LATE_RING
            eng.tensor_tensor(out=l_lo[i][:, :, :], in0=l_in[i][:, :, :], in1=l_hi[i][:, :, :].bitcast(F32),
                              op=ALU.subtract).then_inc(late_lo[n % 2], 1)

        def norm_lo(eng, b, n, bufs, signal):
            half, k = n // KT, n % KT
            c = slice(half * HALF, (half + 1) * HALF)
            eng.wait_ge(lnhi_done, b * LN_CHUNKS + n + 1)
            eng.tensor_tensor(out=hT[1][:, k, c], in0=bufs[n % len(bufs)][:, :], in1=hT[0][:, k, c].bitcast(F32),
                              op=ALU.subtract).then_inc(signal, 1)

        @block.gpsimd
        def _(pool):
            pool.memset(ident16[:, :], 0.0).then_inc(consts_a, 1)
            pool.memset(mask16[:, :], 0.0).then_inc(consts_a, 1)
            pool.memset(one[:, :], 1.0).then_inc(consts_a, 1)
            pool.wait_ge(consts_a, 3)
            pool.affine_select(out=ident16[:, :], in_=ident16[:, :], compare_op=ALU.not_equal, fill=1.0,
                               base=0, pattern=[[-1, P]], channel_multiplier=1).then_inc(consts_ready, 1)
            pool.affine_select(out=mask16[:, :], in_=mask16[:, :], compare_op=ALU.is_ge, fill=MASKED,
                               base=0, pattern=[[-1, P]], channel_multiplier=1).then_inc(consts_ready, 1)

            def split_w(hk, part):
                n = 3 * hk[1] + part
                pool.wait_ge(w_in[n % 2], hk[0] * 48 + 16 * (n // 2 + 1))
                if not (isinstance(hk[0], int) and hk == (0, 0)):
                    pool.wait_ge(z_done, val(prev(hk), ZUNITS, 2 * part + 2))
                pool.tensor_tensor(out=W[0][:, part, :, :], in0=W_in[:, n % 2, :, :],
                                   in1=one[:, 0:1].rearrange("p (a b) -> p a b", a=1).broadcast_to([P, KT, P]),
                                   op=ALU.mult).then_inc(whi_done, 1)
                pool.wait_ge(whi_done, val(hk, 3, part + 1))
                pool.tensor_tensor(out=W[1][:, part, :, :], in0=W_in[:, n % 2, :, :],
                                   in1=W[0][:, part, :, :].bitcast(F32), op=ALU.subtract).then_inc(w_ready, 1)

            def layer_norm(b):
                split_w((0, 0), 0)
                for n in range(0, LN_CHUNKS, 2):
                    norm_lo(pool, b, n, hn0, ln0_lo[0])
                split_w((0, 0), 1)
                split_w((0, 0), 2)

            def step(att, proj, wnext, prefetch, stats=None, norm=None):
                if norm is not None:
                    for n in range(LN_CHUNKS):
                        norm_lo(pool, norm, n, hn, lnlo_done)
                if proj is not None and prefetch:
                    for part in range(3):
                        split_w(nxt(proj), part)
                if proj is None:
                    for j in range(SLOTS):
                        if j in LATE_SPLIT and LATE_SPLIT[j] % 2 == 0:
                            late_split_lo(pool, LATE_SPLIT[j])
                        if j in WO_PLAN:
                            k = WO_PLAN[j]
                            pool.wait_ge(wo_hi, k + 1)
                            pool.tensor_tensor(out=Wo_lo[:, k, :], in0=Wo_in[:, k, :],
                                               in1=Wo_hi[:, k, :].bitcast(F32), op=ALU.subtract).then_inc(wo_lo, 1)
                    pool.wait_ge(wo_lo, KT)

            run(pool, layer_norm, step)

        @block.tensor
        def _(pe):
            def scores(att, u):
                par, head, t = att[1] % 2, u // TT, u % TT
                if u == 0:
                    pe.wait_ge(qklo_done, val(att, 8, 8))
                    pe.wait_ge(qx_done, val(att, 32, 32))
                if u >= 2:
                    pe.wait_ge(exp_done, val(att, UNITS, u - 1))
                for half in range(t // 4 + 1):
                    c0 = half * HALF
                    n = min(HALF, (t + 1) * P - c0)
                    diagonal = half == t // 4
                    out, keys = psS[u % 2][:, c0:c0 + n], Ks[par][:, head, c0:c0 + n]
                    q = slice(t * P, (t + 1) * P)
                    pe.matmul(out, Qs[par][:, head, q], keys, start=True, stop=False)
                    last = pe.matmul(out, Qx[par][:, head, q], keys, start=False, stop=not diagonal)
                    if diagonal:
                        last = pe.matmul(psS[u % 2][:, t * P:(t + 1) * P], ident16[:, :], mask16[:, :],
                                         start=False, stop=True)
                last.then_inc(scores_done, 1)

            def transposes(att, u):
                pe.wait_ge(norm_done, val(att, UNITS, u + 1))
                for n, (k0, nk) in enumerate(unit_chunks(u), CHUNK0[u]):
                    if n >= 2:
                        pe.wait_ge(ptlo_done, val(att, CHUNKS, n - 1))
                    for i in range(nk):
                        last = pe.transpose(psT[n % 2][:, i * P:(i + 1) * P],
                                            Pb[:, u % 2, (k0 + i) * P:(k0 + i + 1) * P], identf[:, :])
                    last.then_inc(tp_done, 1)

            def context(att, g, v_seen):
                par, head, gg = att[1] % 2, g // 4, g % 4
                pe.wait_ge(ptlo_done, val(att, CHUNKS, CHUNK0[2 * g + 2]))
                if g:
                    pe.wait_ge(ctx_done, val(att, GROUPS, g))
                pe.wait_ge(vlo_done, v_seen)
                hi, lo = PT[gg % 2]
                for k in range(2 * gg + 2):
                    q = slice(P if k == 2 * gg + 1 else 0, 2 * P)
                    v = Vs[par][:, head, k, :]
                    pe.matmul(psPV[:, q], v, hi[:, k, q], start=k == 0, stop=False)
                    last = pe.matmul(psPV[:, q], v, lo[:, k, q], start=False, stop=k == 2 * gg + 1)
                last.then_inc(pv_done, 1)

            def project(proj, norm, plan, unit, lo, hi):
                which, half = unit // 2, unit % 2
                bank = psT[0] if second_bank(plan, unit) else psZ
                if lo == 0 and unit < 2 and norm is not None:
                    wait_norm_lo(pe, norm, (half + 1) * KT)
                    pe.wait_ge(lnaff_done, norm * LN_CHUNKS + LN_CHUNKS)
                if lo == 0:
                    other = unit > 0 and second_bank(plan, unit) != second_bank(plan, unit - 1)
                    pe.wait_ge(zs_done, val(proj, ZUNITS, unit - 1 if other else unit))
                    if half == 0:
                        pe.wait_ge(w_ready, val(proj, 3, which + 1))
                mms = [(k, a, b) for k in range(KT) for a, b in ((0, 0), (0, 1), (1, 0))]
                for i in range(lo, hi):
                    k, a, b = mms[i]
                    last = pe.matmul(bank[:, :], W[a][:, which, k, :], hT[b][:, k, half * HALF:(half + 1) * HALF],
                                     start=i == 0, stop=i == ZMM - 1)
                if hi == ZMM:
                    last.then_inc(z_done, 1)

            def v_transposes(proj, half, ctx_seen):
                pe.wait_ge(zs_done, val(proj, ZUNITS, 5 + half))
                if ctx_seen is not None:
                    pe.wait_ge(ctx_done, ctx_seen)
                pe.wait_ge(vlo_done, val(proj, 2, half))
                for i in range(4):
                    last = pe.transpose(psPV[:, i * P:(i + 1) * P], Zs[:, i * P:(i + 1) * P], identf[:, :])
                last.then_inc(vt_done, 1)

            def norm_chunk(b, n, banks):
                half, k = n // KT, n % KT
                if n % KT == 0 and not (isinstance(b, int) and b == 0):
                    pe.wait_ge(xnorm_done, b * TT + (4 * half + 4 - TT))
                if not isinstance(b, int) or b * LN_CHUNKS + n + 1 > len(banks):
                    pe.wait_ge(lnaff_done, b * LN_CHUNKS + n - len(banks) + 1)
                for i in range(4):
                    last = pe.transpose(banks[n % len(banks)][:, i * P:(i + 1) * P],
                                        xn[:, 4 * half + i, k * P:(k + 1) * P], identf[:, :])
                last.then_inc(lnt_done, 1)

            def layer_norm(b):
                for n in range(LN_CHUNKS):
                    norm_chunk(b, n, psT)

            def step(att, proj, wnext, prefetch, stats=None, norm=None):
                plan = ALONE if att is None else PLAIN if norm is None else AFTER_NORM
                v_slot = slot_of(plan, 4) + 1
                for j in range(slots_of(plan)):
                    chunks = [2 * (j - LN_FIRST), 2 * (j - LN_FIRST) + 1] if (
                        norm is not None and 0 <= j - LN_FIRST < LN_CHUNKS // 2) else []
                    if att is not None:
                        if j < UNITS:
                            scores(att, j)
                        if chunks:
                            norm_chunk(norm, chunks[0], [psZ])
                        if 2 <= j < UNITS + 2:
                            transposes(att, j - 2)
                        if j == 2:
                            v_transposes(att, 1, None)
                        if 4 <= j < SLOTS and j % 2 == 0:
                            other = proj is not None and j > v_slot
                            context(att, (j - 4) // 2, val(proj, 2, 1) if other else val(att, 2, 2))
                        if chunks:
                            norm_chunk(norm, chunks[1], [psZ])
                    if proj is not None:
                        for part in parts_of(plan, j):
                            project(proj, 0 if att is None else norm, plan, *part)
                        if j == v_slot:
                            contexts = min(GROUPS, (j - 4) // 2 + 1)
                            v_transposes(proj, 0, None if att is None else val(att, GROUPS, contexts))
                    else:
                        if j - 1 in LATE_MM:
                            late_columns(LATE_MM[j - 1])
                        if j in LATE_MM:
                            late_products(LATE_MM[j])

            def late_products(n):
                if n == 0:
                    pe.wait_ge(zs_done, ZUNITS * nb * PAIRS)
                else:
                    pe.wait_ge(late_rows, n)
                pe.wait_ge(late_lo[n % 2], n // 2 + 1)
                i = n % LATE_RING
                modulate(pe, psZ[0:2 * B, 0:LATE_W], c_split, l_hi[i], l_lo[i]).then_inc(late_done, 1)

            def late_columns(n):
                pe.wait_ge(late_rows, n + 1)
                tiles = LATE_W // P
                sum_transposed(pe, late_gates[:, n * tiles:(n + 1) * tiles, :], g_mod[:, :], select[:, 0:B]
                               ).then_inc(late_cols, 1)

            pe.wait_ge(consts_ready, 2)
            run(pe, layer_norm, step)
            pe.wait_ge(gate_chain, 5)
            pe.transpose(psT[0][0:2 * KT * B, 0:P], g_abs[:, :, :, :].rearrange("p w t b -> p (w t b)"), identf[:, :]
                         ).then_inc(gate_t, 1)

        @block.scalar
        def _(act):
            def pt_hi(att, u):
                g = u // 2
                hi = PT[g % 2][0]
                for n, (k0, nk) in enumerate(unit_chunks(u), CHUNK0[u]):
                    act.wait_ge(tp_done, val(att, CHUNKS, n + 1))
                    if g >= 2:
                        act.wait_ge(pv_done, val(att, GROUPS, g - 1))
                    q = (u % 2) * P
                    act.activation(hi[:, k0:k0 + nk, q:q + P],
                                   psT[n % 2][:, 0:nk * P].rearrange("p (k q) -> p k q", q=P), ACT.Copy
                                   ).then_inc(pthi_done, 1)

            def exps(att, u):
                n = (u % TT + 1) * P
                act.wait_ge(max_done, val(att, UNITS, u + 1))
                if u >= 2:
                    act.wait_ge(tp_done, val(att, CHUNKS, CHUNK0[u - 1]))
                act.activation(Pb[:, u % 2, 0:n], psS[u % 2][:, 0:n], ACT.Exp, bias=negmax[:, u:u + 1],
                               accum_out=rowsum[:, u:u + 1]).then_inc(exp_done, 1)

            def context_lo(att, g):
                act.wait_ge(pv_done, val(att, GROUPS, g + 1))
                if g:
                    act.wait_ge(ctx_done, val(att, GROUPS, g))
                act.activation(ctx_lo[:, :], psPV[D:P, 0:2 * P], ACT.Copy).then_inc(ctxlo_done, 1)

            def copy_z(proj, unit, norm, plan):
                act.wait_ge(z_done, val(proj, ZUNITS, unit + 1))
                if unit == 0:
                    act.wait_ge(vt_done, val(proj, 2, 0))
                    if norm is not None:
                        wait_norm_lo(act, norm, LN_CHUNKS)
                elif unit == 5:
                    act.wait_ge(vt_done, val(proj, 2, 1))
                else:
                    act.wait_ge(qklo_done, val(proj, 8, 2 * unit))
                act.activation(Zs[:, :], (psT[0] if second_bank(plan, unit) else psZ)[:, :], ACT.Copy).then_inc(zs_done, 1)

            def qk_hi(proj, unit):
                par, c = proj[1] % 2, slice((unit % 2) * HALF, (unit % 2 + 1) * HALF)
                dst = (Qs if unit < 2 else Ks)[par]
                act.wait_ge(zs_done, val(proj, ZUNITS, unit + 1))
                for head in range(2):
                    rows = slice(head * D, (head + 1) * D)
                    act.activation(dst[rows, head, c], Zs[rows, :], ACT.Copy, scale=QSCALE if unit < 2 else 1.0
                                   ).then_inc(qkhi_done, 1)

            def v_hi(proj, half):
                act.wait_ge(vt_done, val(proj, 2, half + 1))
                act.activation(Vs[proj[1] % 2][:, :, 4 * half:4 * half + 4, 0:D],
                               psPV[:, :].rearrange("p (t h d) -> p h t d", h=2, d=D), ACT.Copy
                               ).then_inc(vhi_done, 1)

            def norm_affine(b, n, banks, bufs):
                k = n % KT
                act.wait_ge(lnt_done, b * LN_CHUNKS + n + 1)
                if n >= len(bufs):
                    wait_norm_lo(act, b, n + 1 - len(bufs))
                act.activation(bufs[n % len(bufs)][:, :], banks[n % len(banks)][:, :], ACT.Identity,
                               bias=modb[:, 0, k:k + 1], scale=modb[:, 1, k:k + 1]).then_inc(lnaff_done, 1)

            def layer_norm(b):
                act.wait_ge(modb_done, b + 1)
                for n in range(LN_CHUNKS):
                    norm_affine(b, n, psT, hn0)

            def load_chunk(b, n):
                if n:
                    act.wait_ge(xc_used, b * STAT_CHUNKS + n - STAT_CHUNKS)
                src = x.rearrange("b (t p) e -> b t p e", p=P)
                src = src[b:b + 1] if isinstance(b, int) else src[bass.ds(b, 1)]
                act.dma_start(hn[1][:, :], src[:, n // 2, :, (n % 2) * HALF:(n % 2 + 1) * HALF]
                              .rearrange("o p e -> (o p) e")).then_inc(xc_in, 16)

            def step(att, proj, wnext, prefetch, stats=None, norm=None):
                plan = ALONE if att is None else PLAIN if norm is None else AFTER_NORM
                ends = {slot_of(plan, unit): unit for unit in range(ZUNITS)}
                if norm is not None:
                    act.wait_ge(modb_done, norm + 1)
                for j in range(slots_of(plan)):
                    chunks = [2 * (j - LN_FIRST), 2 * (j - LN_FIRST) + 1] if (
                        norm is not None and 0 <= j - LN_FIRST < LN_CHUNKS // 2) else []
                    if att is not None:
                        if chunks:
                            norm_affine(norm, chunks[0], [psZ], hn)
                        if 2 <= j < UNITS + 2:
                            pt_hi(att, j - 2)
                        if j == 3:
                            v_hi(att, 1)
                        if j < UNITS:
                            exps(att, j)
                        if 4 <= j < SLOTS and j % 2 == 0:
                            context_lo(att, (j - 4) // 2)
                        if chunks:
                            norm_affine(norm, chunks[1], [psZ], hn)
                    if proj is not None:
                        unit = ends.get(j - 1)
                        if unit is not None and unit < 4:
                            qk_hi(proj, unit)
                        elif unit == 4:
                            v_hi(proj, 0)
                        if j in ends:
                            copy_z(proj, ends[j], 0 if att is None else norm, plan)
                    if stats is not None and j < STAT_CHUNKS:
                        load_chunk(stats, j)
                    if proj is None and j in LATE_SPLIT:
                        n = LATE_SPLIT[j]
                        i = n % LATE_RING
                        act.wait_ge(late_in[i], 16 * (n // LATE_RING + 1))
                        act.activation(l_hi[i][:, :, :], l_in[i][:, :, :], ACT.Copy).then_inc(late_hi, 1)
                    if proj is None and j in LATE_MM:
                        n = LATE_MM[j]
                        act.wait_ge(late_done, n + 1)
                        if n:
                            act.wait_ge(late_cols, n)
                        act.activation(g_mod[:, :], psZ[0:2 * B, 0:LATE_W], ACT.Copy).then_inc(late_rows, 1)
                    if proj is None and j in WO_PLAN:
                        k = WO_PLAN[j]
                        act.wait_ge(wo_in[k // 2], 16)
                        act.activation(Wo_hi[:, k, :], Wo_in[:, k, :], ACT.Copy).then_inc(wo_hi, 1)

            run(act, layer_norm, step)
            act.wait_ge(gate_t, 1)
            act.activation(g_rows[:, :], psT[0][0:2 * KT * B, 0:P], ACT.Copy).then_inc(gate_copied, 1)

        @block.vector
        def _(dve):
            def row_max(att, u):
                dve.wait_ge(scores_done, val(att, UNITS, u + 1))
                dve.tensor_reduce(negmax[:, u:u + 1], psS[u % 2][:, 0:(u % TT + 1) * P], AX.X, ALU.max,
                                  negate=True).then_inc(max_done, 1)

            def invert(att, u):
                dve.wait_ge(exp_done, val(att, UNITS, u + 1))
                dve.reciprocal(rinv[:, u:u + 1], rowsum[:, u:u + 1]).then_inc(rinv_done, 1)

            def normalize(att, u):
                n = (u % TT + 1) * P
                dve.wait_ge(rinv_done, val(att, UNITS, u + 1))
                dve.tensor_scalar(Pb[:, u % 2, 0:n], Pb[:, u % 2, 0:n], rinv[:, u:u + 1], None, ALU.mult
                                  ).then_inc(norm_done, 1)

            def pt_lo(att, u):
                hi, lo = PT[(u // 2) % 2]
                for n, (k0, nk) in enumerate(unit_chunks(u), CHUNK0[u]):
                    dve.wait_ge(pthi_done, val(att, CHUNKS, n + 1))
                    q = (u % 2) * P
                    dve.tensor_tensor(lo[:, k0:k0 + nk, q:q + P],
                                      psT[n % 2][:, 0:nk * P].rearrange("p (k q) -> p k q", q=P),
                                      hi[:, k0:k0 + nk, q:q + P].bitcast(F32), ALU.subtract
                                      ).then_inc(ptlo_done, 1)

            def context_sum(att, g):
                head, gg = g // 4, g % 4
                dve.wait_ge(ctxlo_done, val(att, GROUPS, g + 1))
                if g == 0:
                    dve.wait_ge(ctx_out, val(att, 16, 16))
                dve.tensor_tensor(ctxs[head * D:(head + 1) * D, gg * 2 * P:(gg + 1) * 2 * P],
                                  psPV[0:D, 0:2 * P], ctx_lo[:, :], ALU.add).then_inc(ctx_done, 1)

            def qk_lo(proj, unit):
                par, c = proj[1] % 2, slice((unit % 2) * HALF, (unit % 2 + 1) * HALF)
                dst = (Qs if unit < 2 else Ks)[par]
                for head in range(2):
                    rows, other = slice(head * D, (head + 1) * D), slice((1 - head) * D, (2 - head) * D)
                    dve.wait_ge(qkhi_done, val(proj, 8, 2 * unit + head + 1))
                    if unit < 2:
                        ins = dve.scalar_tensor_tensor(out=dst[other, head, c], in0=Zs[rows, :], scalar=QSCALE,
                                                       in1=dst[rows, head, c].bitcast(F32), op0=ALU.mult,
                                                       op1=ALU.subtract)
                    else:
                        ins = dve.tensor_tensor(dst[other, head, c], Zs[rows, :], dst[rows, head, c].bitcast(F32),
                                                ALU.subtract)
                    ins.then_inc(qklo_done, 1)

            def v_lo(proj, half):
                v = Vs[proj[1] % 2][:, :, 4 * half:4 * half + 4, :]
                dve.wait_ge(vhi_done, val(proj, 2, half + 1))
                dve.tensor_tensor(v[:, :, :, D:2 * D], psPV[:, :].rearrange("p (t h d) -> p h t d", h=2, d=D),
                                  v[:, :, :, 0:D].bitcast(F32), ALU.subtract).then_inc(vlo_done, 1)

            def norm_chain(b, before):
                count = [before]

                def chain(ins):
                    count[0] += 1
                    ins.then_inc(st_done, 1)
                    dve.wait_ge(st_done, b * stat_steps(TT) + (count[0] - stat_steps(TT)))
                return chain

            def piece_statistics(b, n):
                dve.wait_ge(xc_in, b * (16 * STAT_CHUNKS) + 16 * (n + 1 - STAT_CHUNKS))
                ins = dve.bn_stats(st[:, n // 2, 2 * (n % 2):2 * (n % 2) + 2, :].rearrange("p a c -> p (a c)"),
                                   hn[1][:, :])
                ins.then_inc(xc_used, 1)

            def statistics(b, part):
                chain = norm_chain(b, stat_steps(TT, part))
                norm_statistics(dve, chain, [part], TT, st[:, :, :, :], dm[:, :, :], mean[:, :], rstd[:, :],
                                var[:, :], hvar[:, :], rtmp[:, :])

            def columns(b):
                bs = slice(b, b + 1) if isinstance(b, int) else bass.ds(b, 1)
                dve.tensor_copy(modb[:, :, :], mod_cols[:, 0:2, :, bs].rearrange("p v k o -> p v (k o)")
                                ).then_inc(modb_done, 1)

            def normalize_x(b, t):
                if t % 4 == 0:
                    dve.wait_ge(x_in[t // 4], b * 16)
                dve.tensor_scalar(xn[:, t, :], xn[:, t, :], mean[:, t:t + 1], rstd[:, t:t + 1],
                                  ALU.subtract, ALU.mult).then_inc(xnorm_done, 1)

            def norm_hi(b, n, bufs):
                half, k = n // KT, n % KT
                dve.wait_ge(lnaff_done, b * LN_CHUNKS + n + 1)
                dve.tensor_copy(hT[0][:, k, half * HALF:(half + 1) * HALF],
                                bufs[n % len(bufs)][:, :]).then_inc(lnhi_done, 1)

            def layer_norm(b):
                columns(b)
                for n in range(LN_CHUNKS):
                    norm_hi(b, n, hn0)
                    if n % 2:
                        norm_lo(dve, b, n, hn0, ln0_lo[1])

            def step(att, proj, wnext, prefetch, stats=None, norm=None):
                plan = ALONE if att is None else PLAIN if norm is None else AFTER_NORM
                ends = {slot_of(plan, unit): unit for unit in range(ZUNITS)}
                if norm is not None:
                    columns(norm)
                for j in range(slots_of(plan)):
                    chunks = [2 * (j - LN_FIRST), 2 * (j - LN_FIRST) + 1] if (
                        norm is not None and 0 <= j - LN_FIRST < LN_CHUNKS // 2) else []
                    if att is not None:
                        if 1 <= j < UNITS + 1:
                            invert(att, j - 1)
                        if j < UNITS:
                            row_max(att, j)
                        if chunks:
                            norm_hi(norm, chunks[0], hn)
                        if j == 3:
                            v_lo(att, 1)
                        if 1 <= j < UNITS + 1:
                            normalize(att, j - 1)
                        if 2 <= j < UNITS + 2:
                            pt_lo(att, j - 2)
                        if 4 <= j < SLOTS and j % 2 == 0:
                            context_sum(att, (j - 4) // 2)
                        if chunks:
                            norm_hi(norm, chunks[1], hn)
                        if norm is not None and j < STAT_PARTS - 2:
                            statistics(norm, 2 + j)
                        if norm is not None and 0 <= j - NORM_FIRST < TT:
                            normalize_x(norm, j - NORM_FIRST)
                    if proj is not None:
                        unit = ends.get(j - 1)
                        if unit is not None and unit < 4:
                            qk_lo(proj, unit)
                        elif unit == 4:
                            v_lo(proj, 0)
                    if proj is None and j in LATE_SPLIT and LATE_SPLIT[j] % 2:
                        late_split_lo(dve, LATE_SPLIT[j])
                    if stats is not None:
                        if 1 <= j < STAT_CHUNKS + 1:
                            piece_statistics(stats, j - 1)
                        if j == STAT_CHUNKS + 1:
                            dve.wait_ge(xc_used, stats * STAT_CHUNKS)
                            statistics(stats, 0)
                        if j == STAT_CHUNKS + 2:
                            statistics(stats, 1)

            dve.memset(ctxs[:, :], 0.0).then_inc(ctx_out, 16)
            run(dve, layer_norm, step)
            dve.wait_ge(late_cols, LATE_N)
            gates = late_gates.rearrange("p (w t) b -> p w t b", w=2)
            dve.tensor_scalar(g_sign[:, :, :, :], gates, 0.0, 2.0, ALU.is_ge, ALU.mult).then_inc(gate_chain, 1)
            dve.tensor_scalar(g_abs[:, :, :, :], gates, -1.0, None, ALU.mult).then_inc(gate_chain, 1)
            dve.wait_ge(gate_chain, 2)
            dve.tensor_tensor(g_abs[:, :, :, :], g_abs[:, :, :, :], gates, ALU.max).then_inc(gate_chain, 1)
            dve.wait_ge(gate_chain, 3)
            dve.tensor_scalar(g_abs[:, :, :, :], g_abs[:, :, :, :], 0.25, None, ALU.max).then_inc(gate_chain, 1)
            dve.wait_ge(gate_chain, 4)
            dve.scalar_tensor_tensor(out=g_abs[:, :, :, :], in0=g_sign[:, :, :, :], scalar=1.0, in1=g_abs[:, :, :, :],
                                     op0=ALU.subtract, op1=ALU.mult).then_inc(gate_chain, 1)


def feed_forward_phase(nc, x, ctxT, gate_rows, mod_cols, identf, Wo, w, lb, bo, bw, gate_b, out, nb=B):
    tiles = nb * TT
    with ExitStack() as ctx:
        def sb(name, shape, dt=F32):
            return ctx.enter_context(nc.sbuf_tensor(name, shape, dt))

        def sem(name):
            return ctx.enter_context(nc.semaphore(name))

        def split_pair(name, shape):
            hi = sb(name + "_hi", shape, F32R)
            at = nc.sbuf_base
            sb(name + "_bytes", shape)
            lo = nc.alloc_sbuf_tensor_at(name + "_lo", shape, F32R, offset=at)
            return hi, lo, nc.alloc_sbuf_tensor_at(name + "_in", shape, F32, offset=at)

        Wo_hi, Wo_lo, _ = Wo
        Ww_hi, Ww_lo, Ww_in = split_pair("Ww", [P, KT, E + NAG])
        LB_hi, LB_lo, LB_in = split_pair("LB", [P, E])
        ctx_in = sb("ctx_in", [P, 2, KT, P])
        c_hi, c_lo = sb("c_hi", [P, KT, P], F32R), sb("c_lo", [P, KT, P], F32R)
        xt = sb("xt", [P, 2, E])
        xn2 = sb("xn2", [P, E])
        h2n = sb("h2n", [P, KT, P])
        h2_hi, h2_lo = sb("h2_hi", [P, KT, P], F32R), sb("h2_lo", [P, KT, P], F32R)
        ga, gb = sb("ga", [P, E]), sb("gb", [P, E])
        bo_b, bw_b, gate_bb = sb("bo_b", [P, E]), sb("bw_b", [P, E]), sb("gate_bb", [P, NE])
        yb = sb("yb", [P, E])
        xa = sb("xa", [P, P])
        xaT_hi, xaT_lo = sb("xaT_hi", [P, P], F32R), sb("xaT_lo", [P, P], F32R)
        iota_i, iota = sb("iota_i", [P, NE], I32), sb("iota", [P, NE])
        logits, top, topi, topf = sb("logits", [P, NE]), sb("top", [P, 8]), sb("topi", [P, 8], U32), sb("topf", [P, 8])
        first, gates = sb("first", [P, NE]), sb("gates", [P, NE])
        gap, e2, g1, g2 = [sb(n, [P, 1]) for n in ("gap", "e2", "g1", "g2")]
        st, dm = sb("st2", [P, 1, 4, 3]), sb("dm2", [P, 1, 4])
        mean, rstd, var, hvar, rtmp = [sb(n + "2", [P, 1]) for n in ("mean", "rstd", "var", "hvar", "rtmp")]
        modb = sb("modb2", [P, 2, KT])

        def psum(name, shape):
            return ctx.enter_context(nc.psum_tensor(name, shape, F32))

        psO, psF = psum("psO", [P, E]), psum("psF", [P, 3 * HALF])
        psH = psum("psH", [P, 2, 4, P])
        psX = psum("psX", [P, HALF])
        FC = [(0, 388), (388, 776), (776, E + NAG)]
        psA = psF[:, 2 * HALF + E - FC[2][0]:2 * HALF + FC[2][1] - FC[2][0]]

        ww_in = [sem(f"ww_in{i}") for i in range(4)]
        lb_in, rows_in = sem("lb_in"), sem("rows_in")
        ww_hi, ww_ready = sem("ww_hi"), sem("ww_ready")
        iota_done, iota_ready = sem("iota_done"), sem("iota_ready")
        c_in, x_in = [sem("c_in0"), sem("c_in1")], [sem("xt_in0"), sem("xt_in1")]
        out_done = [sem("out_done0"), sem("out_done1")]
        ga_in, gb_in = sem("ga_in"), sem("gb_in")
        chi_done, clo_done, o_done, po_free, x1_done = (
            sem("chi_done"), sem("clo_done"), sem("o_done"), sem("po_free"), sem("x1_done"))
        x1_chain, xn_done, xt_done, aff_done, h2hi_done, h2lo_done, modb_done = (
            sem("x1_chain"), sem("xn2_done"), sem("xt_done"), sem("aff_done"), sem("h2hi_done"),
            sem("h2lo_done"), sem("modb2_done"))
        bn_done, px_free = sem("bn_done"), sem("px_free")
        ag_done, xa_copied, gap_done, e2_done, gate_chain, xa_done = (
            sem("ag_done"), sem("xa_copied"), sem("gap_done"), sem("e2_done"), sem("gate_chain"), sem("xa_done"))
        xat_done, xathi_done, xatlo_done, f_done, pf_free, yb_done, y_done = (
            sem("xat_done"), sem("xathi_done"), sem("xatlo_done"), sem("f_done"), sem("pf_free"),
            sem("yb_done"), sem("y_done"))
        block = ctx.enter_context(nc.Block())

        def val(t, per, n):
            m, k = t
            return m * (2 * per) + (k * per + n)

        def uses(t, per=16):
            m, k = t
            return m * per + (k // 2 + 1) * per

        def add(t, n):
            return (t[0], t[1] + n)

        def number(t):
            return t[0] * 2 + t[1]

        def run(eng, head, body, tail):
            head()

            def batch(b, last):
                with eng.Fori(0, 3) as c:
                    m = eng.snap(4 * b + c)
                    body((m, 0), b, b)
                    body((m, 1), b, b)
                m = 4 * b + 3
                body((m, 0), b, b)
                if last:
                    tail((m, 1), b)
                else:
                    body((m, 1), b, b + 1)

            if nb > 1:
                with eng.Fori(0, nb - 1) as b:
                    batch(b, False)
            batch(nb - 1, True)

        def weight_lo(eng, k):
            eng.wait_ge(ww_hi, k + 1)
            eng.tensor_tensor(out=Ww_lo[:, k, :], in0=Ww_in[:, k, :], in1=Ww_hi[:, k, :].bitcast(F32),
                              op=ALU.subtract).then_inc(ww_ready, 1)

        def new_batch(t, b, b2):
            return b2 is not b

        @block.sync
        def _(sp):
            xf = x.rearrange("b (t p) e -> (b t) p e", p=P)
            of = out.rearrange("b (t p) e -> (b t) p e", p=P)

            def load_ctx(t, b, tile):
                c = ctxT.rearrange("(b k) p t -> b p k t", k=KT)
                c = c[b] if isinstance(b, int) else c[bass.ds(b, 1)].rearrange("o p k t -> (o p) k t")
                src = c[:, :, tile * P:(tile + 1) * P] if isinstance(tile, int) else c[:, :, bass.ds(tile * P, P)]
                sp.dma_start(ctx_in[:, t[1] % 2, :, :], src).then_inc(c_in[t[1] % 2], 16)

            def load_x(t):
                n = number(t)
                src = xf[n] if isinstance(n, int) else xf[bass.ds(n, 1)].rearrange("o p e -> (o p) e")
                sp.dma_start(xt[:, t[1] % 2, :], src).then_inc(x_in[t[1] % 2], 16)

            def load_gate(b, which, dst, s):
                src = gate_rows[which, :, b:b + 1, :] if isinstance(b, int) else gate_rows[which, :, bass.ds(b, 1), :]
                sp.dma_start(dst[:, :].rearrange("p (t e) -> p t e", e=P),
                             src.rearrange("t o p -> o t p").broadcast_to([P, KT, P])).then_inc(s, 16)

            def load_w(i):
                sp.dma_start(Ww_in[:, 2 * i:2 * i + 2, :], w[:, 2 * i:2 * i + 2, :]).then_inc(ww_in[i], 16)

            load_ctx((0, 0), 0, 0)
            load_x((0, 0))
            for dst, src in ((bo_b, bo), (bw_b, bw)):
                sp.dma_start(dst[:, :], src.broadcast_to([P, E])).then_inc(rows_in, 16)
            sp.dma_start(gate_bb[:, :], gate_b.broadcast_to([P, NE])).then_inc(rows_in, 16)
            load_gate(0, 0, ga, ga_in)
            load_w(0)
            load_ctx((0, 1), 0, 1)
            load_w(1)
            load_x((0, 1))
            load_gate(0, 1, gb, gb_in)
            load_w(2)
            load_w(3)
            sp.dma_start(LB_in[:, :], lb).then_inc(lb_in, 16)

            def store(t):
                sp.wait_ge(y_done, val(t, 1, 2))
                n = number(t)
                dst = of[n] if isinstance(n, int) else of[bass.ds(n, 1)].rearrange("o p e -> (o p) e")
                sp.dma_start(dst, xt[:, t[1] % 2, :]).then_inc(out_done[t[1] % 2], 16)

            def body(t, b, b2, ahead):
                b3, tile = ahead
                if b3 is not None:
                    sp.wait_ge(clo_done, val(t, 1, 1))
                    load_ctx(add(t, 2), b3, tile)
                if b3 is not None and b2 is b and b3 is not b:
                    sp.wait_ge(x1_done, val(t, 1, 2))
                    load_gate(b3, 0, ga, ga_in)
                store(t)
                if new_batch(t, b, b2):
                    sp.wait_ge(yb_done, val(t, 1, 1))
                    load_gate(b2, 1, gb, gb_in)
                if b3 is not None:
                    sp.wait_ge(out_done[t[1] % 2], uses(t))
                    load_x(add(t, 2))

            def batch(b, last):
                with sp.Fori(0, 3) as c:
                    m = sp.snap(4 * b + c)
                    body((m, 0), b, b, (b, 2 * c + 2))
                    body((m, 1), b, b, (b, 2 * c + 3))
                m = 4 * b + 3
                body((m, 0), b, b, (None, 0) if last else (b + 1, 0))
                if last:
                    store((m, 1))
                else:
                    body((m, 1), b, b + 1, (b + 1, 1))

            if nb > 1:
                with sp.Fori(0, nb - 1) as b:
                    batch(b, False)
            batch(nb - 1, True)
            for par in range(2):
                sp.wait_ge(out_done[par], 16 * (tiles // 2))

        @block.gpsimd
        def _(pool):
            pool.iota(iota_i[:, :], pattern=[[1, NE]], base=0, channel_multiplier=0).then_inc(iota_done, 1)

            def context_lo(t):
                pool.wait_ge(chi_done, val(t, 1, 1))
                pool.tensor_tensor(out=c_lo[:, :, :], in0=ctx_in[:, t[1] % 2, :, :],
                                   in1=c_hi[:, :, :].bitcast(F32), op=ALU.subtract).then_inc(clo_done, 1)

            def residual(t):
                pool.wait_ge(yb_done, val(t, 1, 1))
                pool.tensor_tensor(out=xt[:, t[1] % 2, :], in0=xt[:, t[1] % 2, :], in1=yb[:, :], op=ALU.add
                                   ).then_inc(y_done, 1)

            def head():
                weight_lo(pool, 1)
                weight_lo(pool, 3)
                context_lo((0, 1))
                weight_lo(pool, 5)
                weight_lo(pool, 7)

            def body(t, b, b2):
                if not (isinstance(t[0], int) and number(t) + 2 >= tiles):
                    context_lo(add(t, 2))
                residual(t)

            pool.memset(yb[:, :], 0.0).then_inc(y_done, 1)
            run(pool, head, body, lambda t, b: residual(t))

        @block.tensor
        def _(pe):
            def output_projection(t, ks, first, last_k):
                if first:
                    pe.wait_ge(clo_done, val(t, 1, 1))
                    if not (isinstance(t[0], int) and number(t) == 0):
                        pe.wait_ge(po_free, val(t, 1, 0))
                for k in ks:
                    for a, wv in ((c_hi, Wo_hi), (c_hi, Wo_lo), (c_lo, Wo_hi)):
                        for half in range(2):
                            c = slice(half * HALF, (half + 1) * HALF)
                            last = pe.matmul(psO[:, c], a[:, k, :], wv[:, k, c],
                                             start=k == 0 and a is c_hi and wv is Wo_hi,
                                             stop=k == KT - 1 and a is c_lo)
                if last_k:
                    last.then_inc(o_done, 1)

            def norm_transposes(t):
                pe.wait_ge(xn_done, val(t, 1, 1))
                for k in range(KT):
                    last = pe.transpose(psH[:, k // 4, k % 4, :], xn2[:, k * P:(k + 1) * P], identf[:, :])
                    if k % 4 == 3:
                        last.then_inc(xt_done, 1)

            def feed_forward(t):
                pe.wait_ge(ww_ready, KT + 1)
                pe.wait_ge(h2lo_done, val(t, 1, 1))

                def base(g, k):
                    c0, c1 = FC[g]
                    o = psF[:, g * HALF:g * HALF + c1 - c0]
                    pe.matmul(o, h2_hi[:, k, :], Ww_hi[:, k, c0:c1], start=k == 0, stop=False)
                    pe.matmul(o, h2_hi[:, k, :], Ww_lo[:, k, c0:c1], start=False, stop=False)
                    return pe.matmul(o, h2_lo[:, k, :], Ww_hi[:, k, c0:c1], start=False,
                                     stop=g == 2 and k == KT - 1)

                for k in range(KT):
                    last = base(2, k)
                last.then_inc(ag_done, 1)
                for k in range(KT):
                    base(0, k)
                for k in range(KT):
                    if k == 5:
                        pe.wait_ge(xa_done, val(t, 1, 1))
                        pe.transpose(psX[:, 0:P], xa[:, :], identf[:, :]).then_inc(xat_done, 1)
                    base(1, k)
                pe.wait_ge(xatlo_done, val(t, 1, 1))
                for g in range(3):
                    c0, c1 = FC[g][0], min(FC[g][1], E)
                    o = psX[:, 0:c1 - c0] if g == 2 else psF[:, g * HALF:g * HALF + c1 - c0]
                    pe.matmul(o, xaT_hi[:, :], LB_hi[:, c0:c1], start=g == 2, stop=False)
                    pe.matmul(o, xaT_hi[:, :], LB_lo[:, c0:c1], start=False, stop=False)
                    last = pe.matmul(o, xaT_lo[:, :], LB_hi[:, c0:c1], start=False, stop=True)
                last.then_inc(f_done, 1)

            def head():
                output_projection((0, 0), range(KT), True, True)

            def body(t, b, b2):
                output_projection(add(t, 1), range(2), True, False)
                norm_transposes(t)
                output_projection(add(t, 1), range(2, KT), False, True)
                feed_forward(t)

            def tail(t, b):
                norm_transposes(t)
                feed_forward(t)

            run(pe, head, body, tail)

        @block.scalar
        def _(act):
            def context_hi(t):
                act.wait_ge(c_in[t[1] % 2], uses(t))
                act.wait_ge(o_done, val(t, 1, 0))
                act.activation(c_hi[:, :, :], ctx_in[:, t[1] % 2, :, :], ACT.Copy).then_inc(chi_done, 1)

            def norm_hi(t):
                act.wait_ge(modb_done, val(t, 1, 1))
                for k in range(KT):
                    if k % 4 == 0:
                        act.wait_ge(xt_done, val(t, 2, k // 4 + 1))
                    last = act.activation(h2n[:, k, :], psH[:, k // 4, k % 4, :], ACT.Identity,
                                          bias=modb[:, 0, k:k + 1], scale=modb[:, 1, k:k + 1])
                    if k % 4 == 3:
                        last.then_inc(aff_done, 1)
                act.wait_ge(aff_done, val(t, 2, 2))
                act.activation(h2_hi[:, :, :], h2n[:, :, :], ACT.Copy).then_inc(h2hi_done, 1)

            def gate_exp(t):
                act.wait_ge(gap_done, val(t, 1, 1))
                act.activation(e2[:, :], gap[:, :], ACT.Exp).then_inc(e2_done, 1)

            def xa_hi(t):
                act.wait_ge(xat_done, val(t, 1, 1))
                act.activation(xaT_hi[:, :], psX[:, 0:P], ACT.Copy).then_inc(xathi_done, 1)

            def head():
                context_hi((0, 0))
                for k in range(KT):
                    if k == KT // 2:
                        context_hi((0, 1))
                    act.wait_ge(ww_in[k // 2], 16)
                    act.activation(Ww_hi[:, k, :], Ww_in[:, k, :], ACT.Copy).then_inc(ww_hi, 1)
                act.wait_ge(lb_in, 16)
                act.activation(LB_hi[:, :], LB_in[:, :], ACT.Copy).then_inc(ww_hi, 1)

            def body(t, b, b2):
                norm_hi(t)
                if not (isinstance(t[0], int) and number(t) + 2 >= tiles):
                    context_hi(add(t, 2))
                gate_exp(t)
                xa_hi(t)

            def tail(t, b):
                norm_hi(t)
                gate_exp(t)
                xa_hi(t)

            run(act, head, body, tail)

        @block.vector
        def _(dve):
            X_STEPS = 1 + stat_steps(1)
            G_STEPS = 10

            def norm_chain(t, before=0):
                count = [before]

                def chain(ins):
                    count[0] += 1
                    ins.then_inc(x1_chain, 1)
                    dve.wait_ge(x1_chain, val(t, X_STEPS, count[0]))
                return chain

            def residual(t, b, starts):
                chain = norm_chain(t)
                bs = slice(b, b + 1) if isinstance(b, int) else bass.ds(b, 1)
                dve.tensor_copy(modb[:, :, :], mod_cols[:, 2:4, :, bs].rearrange("p v k o -> p v (k o)")
                                ).then_inc(modb_done, 1)
                dve.wait_ge(o_done, val(t, 1, 1))
                if starts:
                    dve.wait_ge(ga_in, b * 16 + 16)
                dve.tensor_tensor(xn2[:, :], psO[:, :], bo_b[:, :], ALU.add).then_inc(po_free, 1)
                dve.wait_ge(po_free, val(t, 1, 1))
                chain(dve.tensor_tensor(xn2[:, :], xn2[:, :], ga[:, :], ALU.mult))
                dve.wait_ge(x_in[t[1] % 2], uses(t))
                x1 = xt[:, t[1] % 2, :]
                dve.tensor_tensor(x1, x1, xn2[:, :], ALU.add).then_inc(x1_done, 1)
                dve.wait_ge(x1_done, val(t, 1, 1))
                for half in range(2):
                    last = dve.bn_stats(st[:, 0, 2 * half:2 * half + 2, :].rearrange("p a c -> p (a c)"),
                                        x1[:, half * HALF:(half + 1) * HALF])
                last.then_inc(bn_done, 1)

            def statistics(t):
                chain = norm_chain(t, 1)
                dve.wait_ge(bn_done, val(t, 1, 1))
                norm_statistics(dve, chain, range(STAT_PARTS), 1, st[:, :, :, :], dm[:, :, :], mean[:, :], rstd[:, :],
                                var[:, :], hvar[:, :], rtmp[:, :])

            def normalize(t):
                dve.tensor_scalar(xn2[:, :], xt[:, t[1] % 2, :], mean[:, 0:1], rstd[:, 0:1],
                                  ALU.subtract, ALU.mult).then_inc(xn_done, 1)

            def gating(t):
                count = [0]

                def chain(ins):
                    count[0] += 1
                    ins.then_inc(gate_chain, 1)
                    dve.wait_ge(gate_chain, val(t, G_STEPS, count[0]))

                dve.wait_ge(ag_done, val(t, 1, 1))
                chain(dve.tensor_tensor(logits[:, :], psA[:, P:NAG], gate_bb[:, :], ALU.add))
                dve.tensor_copy(xa[:, :], psA[:, 0:P]).then_inc(xa_copied, 1)
                chain(dve.max(out=top[:, :], in_=logits[:, :]))
                dve.tensor_tensor(gap[:, :], top[:, 1:2], top[:, 0:1], ALU.subtract).then_inc(gap_done, 1)
                chain(dve.max_index(out=topi[:, :], in_max=top[:, :], in_values=logits[:, :]))
                chain(dve.tensor_copy(topf[:, :], topi[:, :]))
                dve.wait_ge(e2_done, val(t, 1, 1))
                chain(dve.tensor_scalar(g2[:, :], e2[:, :], 1.0, None, ALU.add))
                chain(dve.reciprocal(g1[:, :], g2[:, :]))
                chain(dve.tensor_tensor(g2[:, :], e2[:, :], g1[:, :], ALU.mult))
                chain(dve.tensor_scalar(first[:, :], iota[:, :], topf[:, 0:1], g1[:, :], ALU.is_equal, ALU.mult))
                chain(dve.tensor_scalar(gates[:, :], iota[:, :], topf[:, 1:2], g2[:, :], ALU.is_equal, ALU.mult))
                chain(dve.tensor_tensor(gates[:, :], gates[:, :], first[:, :], ALU.add))
                assert count[0] == G_STEPS
                dve.wait_ge(xa_copied, val(t, 1, 1))
                dve.tensor_tensor(xa[:, :].rearrange("p (e r) -> p e r", r=R),
                                  xa[:, :].rearrange("p (e r) -> p e r", r=R),
                                  gates[:, :].rearrange("p (e o) -> p e o", o=1).broadcast_to([P, NE, R]),
                                  ALU.mult).then_inc(xa_done, 1)

            def xa_lo(t):
                dve.wait_ge(xathi_done, val(t, 1, 1))
                dve.tensor_tensor(xaT_lo[:, :], psX[:, 0:P], xaT_hi[:, :].bitcast(F32), ALU.subtract
                                  ).then_inc(xatlo_done, 1)

            def output(t, b, starts):
                dve.wait_ge(f_done, val(t, 1, 1))
                dve.wait_ge(y_done, val(t, 1, 1))
                w2, c2 = FC[0][1], FC[2][0]
                dve.tensor_tensor(yb[:, 0:c2].rearrange("p (g c) -> p g c", c=w2),
                                  psF[:, 0:2 * HALF].rearrange("p (g c) -> p g c", c=HALF)[:, :, 0:w2],
                                  bw_b[:, 0:c2].rearrange("p (g c) -> p g c", c=w2), ALU.add)
                dve.tensor_tensor(yb[:, c2:E], psX[:, 0:E - c2], bw_b[:, c2:E], ALU.add).then_inc(px_free, 1)
                dve.wait_ge(px_free, val(t, 1, 1))
                dve.tensor_tensor(yb[:, c2:E], yb[:, c2:E], psF[:, 2 * HALF:2 * HALF + E - c2], ALU.add
                                  ).then_inc(pf_free, 1)
                if starts:
                    dve.wait_ge(gb_in, b * 16 + 16)
                dve.wait_ge(pf_free, val(t, 1, 1))
                dve.tensor_tensor(yb[:, :], yb[:, :], gb[:, :], ALU.mult).then_inc(yb_done, 1)

            def norm_lo(t):
                dve.wait_ge(h2hi_done, val(t, 1, 1))
                dve.tensor_tensor(h2_lo[:, :, :], h2n[:, :, :], h2_hi[:, :, :].bitcast(F32), ALU.subtract
                                  ).then_inc(h2lo_done, 1)

            def head():
                dve.wait_ge(chi_done, 1)
                dve.tensor_tensor(c_lo[:, :, :], ctx_in[:, 0, :, :], c_hi[:, :, :].bitcast(F32), ALU.subtract
                                  ).then_inc(clo_done, 1)
                dve.wait_ge(iota_done, 1)
                dve.tensor_copy(iota[:, :], iota_i[:, :]).then_inc(iota_ready, 1)
                dve.wait_ge(iota_ready, 1)
                weight_lo(dve, 0)
                dve.wait_ge(rows_in, 48)
                residual((0, 0), 0, True)
                statistics((0, 0))
                normalize((0, 0))
                for k in range(2, KT, 2):
                    weight_lo(dve, k)
                dve.wait_ge(ww_hi, KT + 1)
                dve.tensor_tensor(LB_lo[:, :], LB_in[:, :], LB_hi[:, :].bitcast(F32), ALU.subtract
                                  ).then_inc(ww_ready, 1)

            def body(t, b, b2):
                norm_lo(t)
                residual(add(t, 1), b2, new_batch(t, b, b2))
                gating(t)
                statistics(add(t, 1))
                xa_lo(t)
                normalize(add(t, 1))
                output(t, b, True)

            def tail(t, b):
                norm_lo(t)
                gating(t)
                xa_lo(t)
                output(t, b, True)

            run(dve, head, body, tail)


def program(nc, x, cT, wmod, wqkv, wo, w, lb, bo, bw, gate_b, out, nb=B):
    gate_rows = nc.dram_tensor("gate_rows", [2, KT, B, P], F32, kind="Internal").ap()
    ctxT = nc.dram_tensor("ctxT", [nb * PAIRS, P, S], F32, kind="Internal").ap()
    with ExitStack() as ctx:
        identf = ctx.enter_context(nc.sbuf_tensor("identf", [P, P], F32))
        mod_cols = ctx.enter_context(nc.sbuf_tensor("mod_cols", [P, 4, KT, B], F32))
        wo_at = nc.sbuf_base
        ctx.enter_context(nc.sbuf_tensor("Wo_bytes", [P, 2, KT, E], F32))
        Wo = [nc.alloc_sbuf_tensor_at(n, [P, KT, E], t, offset=wo_at + i * 4 * KT * E)
              for n, i, t in (("Wo_hi", 0, F32R), ("Wo_lo", 1, F32R), ("Wo_in", 1, F32))]
        arena_at = nc.sbuf_base
        with nc.sbuf_tensor("pair_arena", [P, 2 * 4 * 2 * S], F32), \
                nc.sbuf_tensor("c_split", [P, KT, 2 * B], F32R) as c_split, \
                nc.sbuf_tensor("select", [2 * B, 2 * B], F32) as select:
            xn = nc.alloc_sbuf_tensor_at("xn", [P, TT, E], F32, offset=arena_at)
            modulation_phase(nc, x, cT, wmod, c_split, select, mod_cols, identf, xn,
                             [wo_at + i * 4 * KT * HALF for i in range(4)] + [arena_at + i * 4 * KT * HALF for i in (2, 3)])
            attention_phase(nc, x, wqkv, wmod, c_split, select, mod_cols, identf, gate_rows, ctxT, wo, Wo, wo_at,
                            arena_at, xn, nb)
        feed_forward_phase(nc, x, ctxT, gate_rows, mod_cols, identf, Wo, w, lb, bo, bw, gate_b, out, nb)


def kernel(L0_attn_x, L0_attn_Wq, L0_attn_Wk, L0_attn_Wv, L0_attn_Wo, L0_attn_bo, L0_ffn_W, L0_ffn_b,
           L0_ffn_lora_A, L0_ffn_lora_B, L0_ffn_gate_w, L0_ffn_gate_b, L0_c, L0_wmod):
    import numpy as np
    import concourse.bacc as bacc
    from concourse.bass_utils import run_bass_kernel_spmd

    def features_by_partition(a):
        return np.ascontiguousarray(a.T.reshape(KT, P, a.shape[0]).transpose(1, 0, 2))

    def by_pair(a):
        return a.T.reshape(KT, P, PAIRS, P).transpose(2, 1, 0, 3)

    c, W, A, gw = (np.asarray(a) for a in (L0_c, L0_ffn_W, L0_ffn_lora_A, L0_ffn_gate_w))
    arrays = {
        "x": np.ascontiguousarray(L0_attn_x),
        "cT": features_by_partition(c),
        "wmod": np.ascontiguousarray(L0_wmod),
        "wqkv": np.ascontiguousarray(np.stack([by_pair(np.asarray(a)) for a in (L0_attn_Wq, L0_attn_Wk, L0_attn_Wv)], 1)),
        "wo": features_by_partition(np.asarray(L0_attn_Wo)),
        "w": features_by_partition(np.concatenate([W, A.reshape(NE * R, E), gw], 0)),
        "lb": np.ascontiguousarray(np.asarray(L0_ffn_lora_B).transpose(0, 2, 1).reshape(NE * R, E)),
        "bo": np.asarray(L0_attn_bo).reshape(1, E),
        "bw": np.asarray(L0_ffn_b).reshape(1, E),
        "gate_b": np.asarray(L0_ffn_gate_b).reshape(1, NE),
    }
    nc = bacc.Bacc("TRN2", target_bir_lowering=False, num_devices=1)
    args = [nc.dram_tensor(f"in_{n}", a.shape, F32, kind="ExternalInput").ap() for n, a in arrays.items()]
    out = nc.dram_tensor("out", (B, S, E), F32, kind="ExternalOutput").ap()
    program(nc, *args, out)
    r = run_bass_kernel_spmd(nc, [{f"in_{n}": a for n, a in arrays.items()}], core_ids=[0])
    return r.results[0]["out"]
```
